# Optimizing a Trainium2 kernel written in Bass

```python
import numpy as np
import jax
import jax.numpy as jnp

def _softmax(x, axis=-1):
    return jax.nn.softmax(x, axis=axis)

def _gelu(x):
    return jax.nn.gelu(x, approximate=True)

def _silu(x):
    return jax.nn.silu(x)

def _sigmoid(x):
    return jax.nn.sigmoid(x)

def _layernorm(x, axis=-1, eps=1e-05):
    m = jnp.mean(x, axis=axis, keepdims=True)
    v = jnp.var(x, axis=axis, keepdims=True)
    return (x - m) / jnp.sqrt(v + eps)

def _scatter_add(tgt, idx, src, axis=0):
    return tgt.at[idx].add(src)

def _segment_sum(src, seg, n):
    return jax.ops.segment_sum(src, seg, n)
kernel_name = 'mk_flamingo_gated_d1_seqx_r4_9675d2'

def setup_inputs(seed: int=0):
    np.random.seed(seed)
    _w = jnp.asarray

    def _rec_inputs():
        import jax
        import jax.numpy as jnp
        _rk = jax.random.key(seed)
        x = -0.0005146 + 1 * jax.random.normal(jax.random.fold_in(_rk, 1), (4, 1024, 256), jnp.float32)
        _lenS = 1024 - jax.random.randint(jax.random.fold_in(_rk, 7), (4,), 0, max(1, 1024 // 4) + 1, jnp.int32)
        _lenS2 = 64 - jax.random.randint(jax.random.fold_in(_rk, 8), (4,), 0, max(1, 64 // 4) + 1, jnp.int32)
        _ctx_768P = jax.random.normal(jax.random.fold_in(_rk, 11), (4, 16, 192), jnp.float32)
        _ctx_768c = jax.random.dirichlet(jax.random.fold_in(_rk, 511), 0.3 * jnp.ones((16,), jnp.float32), (4, 64))
        _ctx_768t = jnp.einsum('bsk,bkd->bsd', _ctx_768c, _ctx_768P)
        _ctx_768t = _ctx_768t * jax.lax.rsqrt(jnp.mean(jnp.square(_ctx_768t)) + 1e-12) * 0.953939
        ctx_768 = -0.00040386 + 0.999972 * (_ctx_768t + 0.3 * jax.random.normal(jax.random.fold_in(_rk, 611), (4, 64, 192), jnp.float32))
        _validS = jnp.arange(1024)[None, :] < _lenS[:, None]
        _validS2 = jnp.arange(64)[None, :] < _lenS2[:, None]
        _causal = jnp.tril(jnp.ones((1024, 1024), dtype=bool))
        mask_BxS2_bk0 = jnp.logical_not(jnp.broadcast_to(_validS2[:, :], (4, 64)))
        _g = jax.random.normal(jax.random.fold_in(_rk, 9001), (2, 1), jnp.float32)
        _g = jnp.sign(_g) * jnp.maximum(jnp.abs(_g), 1.0) + (_g == 0) * 1.0
        g_xattn = _g[0]
        g_ffn = _g[1]
        return (x, ctx_768, mask_BxS2_bk0, g_xattn, g_ffn)
    x, ctx_768, mask_BxS2_bk0, g_xattn, g_ffn = _rec_inputs()

    def _L0_xattn_setup():
        import jax, jax.numpy as jnp
        import numpy as np
        DIM_IN, DIM_LAT, DIM_HEAD = (192, 256, 64)
        INNER = max(DIM_LAT, DIM_IN)
        HEADS = INNER // DIM_HEAD
        SCALE = DIM_HEAD ** (-0.5)
        RMS_EPS = 1e-08
        LN_EPS = 1e-05

        def layernorm(x, g, b):
            mu = jnp.mean(x, axis=-1, keepdims=True)
            var = jnp.mean((x - mu) ** 2, axis=-1, keepdims=True)
            return (x - mu) * jax.lax.rsqrt(var + LN_EPS) * g + b

        def rmsnorm(x, gamma):
            norm = jnp.sqrt(jnp.sum(x * x, axis=-1, keepdims=True)) * x.shape[-1] ** (-0.5)
            return x / jnp.maximum(norm, RMS_EPS) * gamma
        key = jax.random.key(seed)
        ks = jax.random.split(key, 12)
        b, n, m = (4, 1024, 128)
        x = jax.random.normal(ks[0], (b, n, DIM_IN), jnp.float32)
        latents = jax.random.normal(ks[1], (b, m, DIM_LAT), jnp.float32)
        mask = jax.random.randint(ks[2], (b, n), 0, 2).astype(bool)
        s = lambda k, sh, fan: jax.random.normal(k, sh, jnp.float32) * fan ** (-0.5)
        return {'x': x, 'latents': latents, 'mask': mask, 'ln_x_g': jnp.ones((DIM_IN,), jnp.float32), 'ln_x_b': jnp.zeros((DIM_IN,), jnp.float32), 'ln_l_g': jnp.ones((DIM_LAT,), jnp.float32), 'ln_l_b': jnp.zeros((DIM_LAT,), jnp.float32), 'qn_g': jnp.ones((DIM_HEAD,), jnp.float32), 'kn_g': jnp.ones((DIM_HEAD,), jnp.float32), 'Wq': s(ks[3], (INNER, DIM_LAT), DIM_LAT), 'Wkv': s(ks[4], (2 * INNER, DIM_IN), DIM_IN), 'Wlkv': s(ks[5], (2 * INNER, DIM_LAT), DIM_LAT), 'Wo': s(ks[6], (DIM_LAT, INNER), INNER), 'bo': jnp.zeros((DIM_LAT,), jnp.float32)}
    _L0_xattn_all = _L0_xattn_setup()
    _L0_xattn_in = {k: v for k, v in _L0_xattn_all.items() if k in ('ln_x_g', 'ln_x_b', 'ln_l_g', 'ln_l_b', 'qn_g', 'kn_g', 'Wq', 'Wkv', 'Wlkv', 'Wo', 'bo')}
    del _L0_xattn_all

    def _L0_ffn_setup():
        import jax, jax.numpy as jnp
        import numpy as np
        EMBED_DIM = 256
        HIDDEN_DIM = 1024
        NUM_EXPERTS = 8
        TOP_K = 2
        key = jax.random.key(seed)
        ks = jax.random.split(key, 4)
        std1 = float(np.sqrt(2.0 / EMBED_DIM))
        std2 = float(np.sqrt(2.0 / HIDDEN_DIM))
        x = jax.random.normal(ks[0], (1, 512, EMBED_DIM), dtype=jnp.float32)
        w_router = jax.random.normal(ks[1], (EMBED_DIM, NUM_EXPERTS), dtype=jnp.float32) * 0.02
        w1 = jax.random.normal(ks[2], (NUM_EXPERTS, EMBED_DIM, HIDDEN_DIM), dtype=jnp.float32) * std1
        b1 = jnp.zeros((NUM_EXPERTS, HIDDEN_DIM), dtype=jnp.float32)
        w2 = jax.random.normal(ks[3], (NUM_EXPERTS, HIDDEN_DIM, EMBED_DIM), dtype=jnp.float32) * std2
        b2 = jnp.zeros((NUM_EXPERTS, EMBED_DIM), dtype=jnp.float32)
        return {'x': x, 'w_router': w_router, 'w1': w1, 'b1': b1, 'w2': w2, 'b2': b2}
    _L0_ffn_all = _L0_ffn_setup()
    _L0_ffn_in = {k: v for k, v in _L0_ffn_all.items() if k in ('w_router', 'w1', 'b1', 'w2', 'b2')}
    del _L0_ffn_all
    return {'x': x, 'ctx_768': ctx_768, 'mask_BxS2_bk0': mask_BxS2_bk0, 'g_xattn': g_xattn, 'g_ffn': g_ffn, 'L0_xattn_ln_x_g': _L0_xattn_in['ln_x_g'], 'L0_xattn_ln_x_b': _L0_xattn_in['ln_x_b'], 'L0_xattn_ln_l_g': _L0_xattn_in['ln_l_g'], 'L0_xattn_ln_l_b': _L0_xattn_in['ln_l_b'], 'L0_xattn_qn_g': _L0_xattn_in['qn_g'], 'L0_xattn_kn_g': _L0_xattn_in['kn_g'], 'L0_xattn_Wq': _L0_xattn_in['Wq'], 'L0_xattn_Wkv': _L0_xattn_in['Wkv'], 'L0_xattn_Wlkv': _L0_xattn_in['Wlkv'], 'L0_xattn_Wo': _L0_xattn_in['Wo'], 'L0_xattn_bo': _L0_xattn_in['bo'], 'L0_ffn_w_router': _L0_ffn_in['w_router'], 'L0_ffn_w1': _L0_ffn_in['w1'], 'L0_ffn_b1': _L0_ffn_in['b1'], 'L0_ffn_w2': _L0_ffn_in['w2'], 'L0_ffn_b2': _L0_ffn_in['b2']}

def reference(x, ctx_768, mask_BxS2_bk0, g_xattn, g_ffn, L0_xattn_ln_x_g, L0_xattn_ln_x_b, L0_xattn_ln_l_g, L0_xattn_ln_l_b, L0_xattn_qn_g, L0_xattn_kn_g, L0_xattn_Wq, L0_xattn_Wkv, L0_xattn_Wlkv, L0_xattn_Wo, L0_xattn_bo, L0_ffn_w_router, L0_ffn_w1, L0_ffn_b1, L0_ffn_w2, L0_ffn_b2):
    import jax
    import jax.numpy as jnp

    def _L0_xattn_ref(x, latents, mask, ln_x_g, ln_x_b, ln_l_g, ln_l_b, qn_g, kn_g, Wq, Wkv, Wlkv, Wo, bo):
        import jax, jax.numpy as jnp
        import numpy as np
        DIM_IN, DIM_LAT, DIM_HEAD = (192, 256, 64)
        INNER = max(DIM_LAT, DIM_IN)
        HEADS = INNER // DIM_HEAD
        SCALE = DIM_HEAD ** (-0.5)
        RMS_EPS = 1e-08
        LN_EPS = 1e-05

        def layernorm(x, g, b):
            mu = jnp.mean(x, axis=-1, keepdims=True)
            var = jnp.mean((x - mu) ** 2, axis=-1, keepdims=True)
            return (x - mu) * jax.lax.rsqrt(var + LN_EPS) * g + b

        def rmsnorm(x, gamma):
            norm = jnp.sqrt(jnp.sum(x * x, axis=-1, keepdims=True)) * x.shape[-1] ** (-0.5)
            return x / jnp.maximum(norm, RMS_EPS) * gamma
        b, n, _ = x.shape
        m = latents.shape[1]
        xn = layernorm(x, ln_x_g, ln_x_b)
        ln = layernorm(latents, ln_l_g, ln_l_b)
        q = ln @ Wq.T
        kv = jnp.concatenate([xn @ Wkv.T, ln @ Wlkv.T], axis=1)
        k, v = (kv[..., :INNER], kv[..., INNER:])
        split_heads = lambda t: t.reshape(t.shape[0], t.shape[1], HEADS, DIM_HEAD).transpose(0, 2, 1, 3)
        q, k, v = (split_heads(q), split_heads(k), split_heads(v))
        qn = rmsnorm(q, qn_g) * SCALE
        kn = rmsnorm(k, kn_g)
        attn = jnp.einsum('bhid,bhjd->bhij', qn, kn)
        full_mask = jnp.pad(mask, ((0, 0), (0, m)), constant_values=True)
        attn = jnp.where(full_mask[:, None, None, :], attn, -jnp.finfo(attn.dtype).max)
        attn = jax.nn.softmax(attn, axis=-1)
        out = jnp.einsum('bhij,bhjd->bhid', attn, v)
        out = out.transpose(0, 2, 1, 3).reshape(b, m, INNER)
        return out @ Wo.T + bo

    def _L0_ffn_ref(x, w_router, w1, b1, w2, b2):
        import jax, jax.numpy as jnp
        import numpy as np
        EMBED_DIM = 256
        HIDDEN_DIM = 1024
        NUM_EXPERTS = 8
        TOP_K = 2
        orig_shape = x.shape
        xf = x.reshape(-1, EMBED_DIM)
        logits = xf @ w_router
        probs = jax.nn.softmax(logits, axis=-1)
        topk_w, topk_idx = jax.lax.top_k(probs, TOP_K)
        mask = jax.nn.one_hot(topk_idx, NUM_EXPERTS, dtype=xf.dtype)
        weights = jnp.sum(topk_w[..., None] * mask, axis=1)
        h = jnp.einsum('te,ieh->tih', xf, w1) + b1
        h = jax.nn.gelu(h)
        out = jnp.einsum('tih,ihe->tie', h, w2) + b2
        out = jnp.sum(out * weights[..., None], axis=1)
        return out.reshape(orig_shape)
    x = x + jnp.tanh(g_xattn[0]) * _L0_xattn_ref(ctx_768, _layernorm(x, axis=-1), mask_BxS2_bk0, L0_xattn_ln_x_g, L0_xattn_ln_x_b, L0_xattn_ln_l_g, L0_xattn_ln_l_b, L0_xattn_qn_g, L0_xattn_kn_g, L0_xattn_Wq, L0_xattn_Wkv, L0_xattn_Wlkv, L0_xattn_Wo, L0_xattn_bo)
    x = x + jnp.tanh(g_ffn[0]) * _L0_ffn_ref(_layernorm(x, axis=-1), L0_ffn_w_router, L0_ffn_w1, L0_ffn_b1, L0_ffn_w2, L0_ffn_b2)
    return x

_drawn_inputs = setup_inputs


def setup_inputs(seed=0):
    import zlib

    import numpy as np

    out = dict(_drawn_inputs(seed))
    spreads = {'L0_xattn_ln_x_g': (1.0, 0.6),
     'L0_xattn_ln_x_b': (0.0, 0.764),
     'L0_xattn_ln_l_g': (1.0, 0.2),
     'L0_xattn_ln_l_b': (0.0, 0.1),
     'L0_xattn_qn_g': (1.0, 0.2),
     'L0_xattn_kn_g': (1.0, 0.2),
     'L0_xattn_bo': (0.0, 0.1),
     'L0_ffn_b1': (0.0, 0.347),
     'L0_ffn_b2': (0.0, 0.356)}
    factors = {'ctx_768': 2.919, 'L0_xattn_Wkv': 2.823}
    for name, (base, spread) in spreads.items():
        noise = np.random.default_rng([zlib.crc32(name.encode()), seed]).standard_normal(out[name].shape)
        drawn = base * np.exp(spread * noise) if base else spread * noise
        out[name] = jnp.asarray(drawn.astype(out[name].dtype))
    for name, factor in factors.items():
        out[name] = (out[name] * factor).astype(out[name].dtype)
    return out
```

```python
from contextlib import ExitStack

import concourse.bass as bass
from concourse import mybir

F32 = mybir.dt.float32
F32R = mybir.dt.float32r
BF16 = mybir.dt.bfloat16
I32 = mybir.dt.int32
U8 = mybir.dt.uint8
ALU = mybir.AluOpType
ACT = mybir.ActivationFunctionType
AX = mybir.AxisListType.X

P = 128


def flamingo_gated_layer(nc, x, ctx_768, mask, g_xattn, g_ffn, ln_x_g, ln_x_b, ln_l_g, ln_l_b, qn_g, kn_g,
                         Wq, Wkv, Wlkv, Wo, bo, w_router, w1, b1, w2, b2, out):
    B, S, D = x.shape
    _, SC, DC = ctx_768.shape
    DH = qn_g.shape[0]
    H = Wq.shape[0] // DH
    NE = w_router.shape[1]
    HID = w1.shape[2]
    T = S // P
    NT = T + 1
    EC = D // P
    QK = 2 * H * DH
    HALF = S // 2
    HT = T // 2
    GROUPS_W = 6
    GROUPS = 2 + 2 * EC
    KT = NT
    NI = H * KT
    NP_RING = 3
    EPS, RMS_EPS = 1e-5, 1e-8
    SCALE = float(DH) ** -0.5
    SAFE = 60.0
    TM = 256
    MH = TM // P
    NTOK = B * S
    REGION = NTOK + TM
    ROW = D + 2
    HC = HID // P
    MAXT = NTOK // TM

    routed = nc.dram_tensor("routed", (NE * REGION, ROW), F32).ap()
    total = nc.dram_tensor("total", (NTOK + TM, D), F32).ap()

    persistent = ExitStack()
    with persistent, nc.allow_non_contiguous_dma(reason="columns of parameters, a few bytes each"):
        pad_rows = persistent.enter_context(nc.sbuf_tensor("pad_rows", [P, MH, ROW], F32))
        counts = persistent.enter_context(nc.sbuf_tensor("counts", [P, NE], F32))
        plan = persistent.enter_context(nc.sbuf_tensor("plan", [P, 3 * NE], I32))
        w1_raw = persistent.enter_context(nc.sbuf_tensor("w1_raw", [P, EC, HID], F32))
        w2_raw = persistent.enter_context(nc.sbuf_tensor("w2_raw", [P, HC, D], F32))
        ident = persistent.enter_context(nc.sbuf_tensor("ident", [P, P], F32))

        with ExitStack() as ctx:
            def sb(name, shape, dt=F32):
                return ctx.enter_context(nc.sbuf_tensor(name, shape, dt))

            def sem(name):
                return ctx.enter_context(nc.semaphore(name))

            w_hi = sb("w_hi", [P, EC, 768], F32R)
            w_lo = sb("w_lo", [P, EC, 768], F32R)
            wo_hi = sb("wo_hi", [P, EC, D], F32R)
            wo_lo = sb("wo_lo", [P, EC, D], F32R)
            wc_hi = sb("wc_hi", [P, 2, 512], F32R)
            wc_lo = sb("wc_lo", [P, 2, 512], F32R)
            router = sb("router", [P, EC, NE])
            tri = sb("tri", [P, P], BF16)
            ones = sb("ones", [P, P], BF16)
            gl = sb("gl", [P, EC])
            bl = sb("bl", [P, EC])
            gx = sb("gx", [P, 2])
            bx = sb("bx", [P, 2])
            qg = sb("qg", [P, 1])
            kg = sb("kg", [P, 1])
            gqk = sb("gqk", [P, 1])
            qg_row = sb("qg_row", [P, DH])
            kg_row = sb("kg_row", [P, DH])
            gate_raw = sb("gate_raw", [P, 2])
            gate = sb("gate", [P, 2])
            bo_row = sb("bo_row", [P, D])
            tbo = sb("tbo", [P, D])
            shift = sb("shift", [P, 1])
            minus_half = sb("minus_half", [P, 16])
            iota_i = sb("iota_i", [P, 16], I32)
            expert_id = sb("expert_id", [P, NE])
            region0 = sb("region0", [P, NE])
            token_id = sb("token_id", [P, T])
            xr = sb("xr", [P, T, D])
            cr = sb("cr", [SC, DC])
            mask_u8 = sb("mask_u8", [SC, 1], U8)
            mask_bias = sb("mask_bias", [SC, 1])
            stats = sb("stats", [P, NT, 6])
            mv = sb("mv", [P, NT, 2])
            var_in = sb("var_in", [P, NT])
            rstd = sb("rstd", [P, NT])
            xn = sb("xn", [P, T, D])
            cn = sb("cn", [SC, 2 * P])
            xb = sb("xb", [P, T, D])
            lnf = sb("lnf", [P, 2, HALF])
            ln_hi = sb("ln_hi", [P, EC, S], F32R)
            ln_lo = sb("ln_lo", [P, EC, S], F32R)
            lc_hi = sb("lc_hi", [P, 2, P], F32R)
            lc_lo = sb("lc_lo", [P, 2, P], F32R)
            big = sb("big", [P, 2 * T * ROW])
            qk_sb = sb("qk_sb", [P, 3, QK])
            sq = sb("sq", [P, 2, QK])
            ss = sb("ss", [P, 2, 8])
            ssm = sb("ssm", [P, 2, 8])
            rr = sb("rr", [P, 2, 8])
            qkd = sb("qkd", [P, 2, 2 * QK])
            Q1 = sb("Q1", [P, H, S], F32R)
            K1 = sb("K1", [P, H, S + P], F32R)
            K2 = sb("K2", [DH, H, S + P], F32R)
            Vt = sb("Vt", [P, KT, H * P])
            st2 = sb("st2", [P, T, 6])
            mv2 = sb("mv2", [P, T, 2])
            var2 = sb("var2", [P, T])
            rstd2 = sb("rstd2", [P, T])
            lg = sb("lg", [P, T, NE])
            lmax = sb("lmax", [P, T])
            lz = sb("lz", [P, T, NE])
            pe_ = sb("pe_", [P, T, NE])
            psum_ = sb("psum_", [P, T])
            prob = sb("prob", [P, T, NE])
            top = sb("top", [P, 2, T])
            eq = sb("eq", [P, T, NE])
            cand = sb("cand", [P, T, NE])
            pick = sb("pick", [P, 2, T])
            hot = sb("hot", [P, 2, T, NE])
            prob2 = sb("prob2", [P, T, NE])
            chosen = sb("chosen", [P, T * NE], BF16)
            base = sb("base", [P, T + 1, NE])
            slot = sb("slot", [P, T, NE])
            slot_hot = sb("slot_hot", [P, 2, T, NE])
            slot_f = sb("slot_f", [P, 2, T])
            slot_i = sb("slot_i", [P, 2, T], I32)
            plan_f = sb("plan_f", [P, 3 * NE])
            tiles_i = sb("tiles_i", [P, NE], I32)

            att_hi, att_lo = ln_hi, ln_lo
            pr = [xn[:, 0:HT, :].rearrange("p t d -> p (t d)"), xn[:, HT:T, :].rearrange("p t d -> p (t d)"),
                  sq[:].rearrange("p t d -> p (t d)")]
            den = lnf[:].rearrange("p t d -> p (t d)")
            attf = qkd
            yT = qkd
            wst_q = big[:, 0:512].rearrange("p (b e) -> p b e", b=2)
            wst_l = big[:, 512:1536].rearrange("p (b e) -> p b e", b=4)
            wst_o = big[:, 1536:2048].rearrange("p (b e) -> p b e", b=2)
            wst_c = big[:, 2048:2048 + 4 * 2 * P].rearrange("p (b e) -> p b e", b=4)
            rows = [big[:, k * T * ROW:(k + 1) * T * ROW].rearrange("p (t r) -> p t r", t=T) for k in range(2)]

            psS = [ctx.enter_context(nc.psum_tensor(f"psS{i}", [P, S], F32)) for i in range(2)]
            psO = [ctx.enter_context(nc.psum_tensor(f"psO{i}", [P, S], F32)) for i in range(2)]

            consts_loaded = sem("consts_loaded")
            weights_loaded = sem("weights_loaded")
            ident_ready = sem("ident_ready")
            iota_done = sem("iota_done")
            pool_const = sem("pool_const")
            dve_const = sem("dve_const")
            gate_ready = sem("gate_ready")
            wT_done = sem("wT_done")
            w_hi_ready = sem("w_hi_ready")
            w_ready = sem("w_ready")
            seq_loaded = sem("seq_loaded")
            stat_ready = sem("stat_ready")
            mv_ready = sem("mv_ready")
            var_ready = sem("var_ready")
            rstd_ready = sem("rstd_ready")
            xn_ready = sem("xn_ready")
            xb_ready = sem("xb_ready")
            mask_cut = sem("mask_cut")
            mask_ready = sem("mask_ready")
            xT_done = sem("xT_done")
            lnf_ready = sem("lnf_ready")
            ln_hi_ready = sem("ln_hi_ready")
            ln_ready = sem("ln_ready")
            proj_done = sem("proj_done")
            proj_read = sem("proj_read")
            ss_ready = sem("ss_ready")
            ssm_ready = sem("ssm_ready")
            rr_ready = sem("rr_ready")
            qkd_ready = sem("qkd_ready")
            qkT_done = sem("qkT_done")
            qk_hi_ready = sem("qk_hi_ready")
            qk_ready = sem("qk_ready")
            s_done = sem("s_done")
            exp_done = sem("exp_done")
            av_done = sem("av_done")
            den_ready = sem("den_ready")
            o_read = sem("o_read")
            att_hi_ready = sem("att_hi_ready")
            att_ready = sem("att_ready")
            o_done = sem("o_done")
            x2_ready = sem("x2_ready")
            x2_stored = sem("x2_stored")
            st2_ready = sem("st2_ready")
            mv2_ready = sem("mv2_ready")
            var2_ready = sem("var2_ready")
            rstd2_ready = sem("rstd2_ready")
            y_ready = sem("y_ready")
            y2_ready = sem("y2_ready")
            yT_done = sem("yT_done")
            yT_ready = sem("yT_ready")
            logits_done = sem("logits_done")
            route = sem("route")
            ez_ready = sem("ez_ready")
            chosen_ready = sem("chosen_ready")
            rank_done = sem("rank_done")
            base_ready = sem("base_ready")
            plan_ready = sem("plan_ready")
            slots_ready = sem("slots_ready")
            scattered = sem("scattered")
            dump_zeroed = sem("dump_zeroed")
            zero_ready = sem("zero_ready")
            raw_loaded = sem("raw_loaded")
            passed = sem("passed")

            NCONST = 16
            NPOOL = 16
            ROUTE = 21
            block = ctx.enter_context(nc.Block())

            def load_sequence(sp, b):
                sp.dma_start(xr[:], x[bass.ds(b, 1)].rearrange("a (t p) d -> p (a t) d", p=P)).then_inc(seq_loaded, 16)
                sp.dma_start(cr[:], ctx_768[bass.ds(b, 1)].rearrange("a s d -> (a s) d")).then_inc(seq_loaded, 16)
                sp.dma_start(mask_u8[:], mask[bass.ds(b, 1)].rearrange("a s -> s a")).then_inc(seq_loaded, 16)

            def store_tokens(sp, b):
                sp.wait_ge(x2_ready, b * T + T)
                sp.dma_start(total[bass.ds(b * S, S)].rearrange("(t p) d -> p t d", p=P), xb[:]).then_inc(x2_stored, 16)

            def value_slots(t, p):
                return Vt[0:p, t, :].rearrange("p (i s d) -> p i s d", i=2, s=4)[:, :, 0:4:3, :]

            def norm_group(g):
                if g < 2:
                    return lnf[:, g % 2, 0:SC], lc_hi[:, g, 0:SC], lc_lo[:, g, 0:SC]
                hb, c = divmod(g - 2, EC)
                cols = slice(hb * HALF, (hb + 1) * HALF)
                return lnf[:, g % 2, :], ln_hi[:, c, cols], ln_lo[:, c, cols]

            def weight_groups():
                f = lambda o, n: o[:, n * HALF:(n + 1) * HALF]
                two = lambda a: a.rearrange("p (c n) -> p c n", c=2)
                yield f(psS[0], 0), w_hi[:, 0, 0:QK], w_lo[:, 0, 0:QK]
                yield f(psS[0], 1), w_hi[:, 1, 0:QK], w_lo[:, 1, 0:QK]
                yield two(f(psS[1], 0)), w_hi[:, :, QK:768], w_lo[:, :, QK:768]
                yield two(f(psS[1], 1)), wo_hi[:], wo_lo[:]
                yield f(psO[0], 0), wc_hi[:, 0, :], wc_lo[:, 0, :]
                yield f(psO[0], 1), wc_hi[:, 1, :], wc_lo[:, 1, :]

            def norm_psum(g):
                if g < 2:
                    return psO[0][:, g * HALF:g * HALF + SC]
                hb, c = divmod(g - 2, EC)
                return psS[hb][:, c * HALF:(c + 1) * HALF]

            def out_psum(t):
                return psS[(t % 4) // 2][:, (t % 2) * HALF:(t % 2) * HALF + D]

            @block.sync
            def _(sp):
                sp.dma_start(wst_q, Wq.rearrange("(b p) e -> p b e", p=P)).then_inc(weights_loaded, 16)
                sp.dma_start(wst_l, Wlkv.rearrange("(b p) e -> p b e", p=P)).then_inc(weights_loaded, 16)
                sp.dma_start(wst_c[:, :, 0:DC], Wkv.rearrange("(b p) e -> p b e", p=P)).then_inc(weights_loaded, 16)
                sp.dma_start(wst_o, Wo.rearrange("(b p) e -> p b e", p=P)).then_inc(weights_loaded, 16)
                load_sequence(sp, 0)
                sp.wait_ge(pool_const, NPOOL)
                column = lambda v: v.rearrange("(d a) -> d a", a=1)
                wide = lambda v: v.rearrange("(a d) -> a d", a=1)
                for dst, src in (
                    (gl[:], ln_l_g.rearrange("(c p) -> p c", p=P)), (bl[:], ln_l_b.rearrange("(c p) -> p c", p=P)),
                    (gx[:, 0:1], column(ln_x_g[0:P])), (bx[:, 0:1], column(ln_x_b[0:P])),
                    (gx[0:DC - P, 1:2], column(ln_x_g[P:DC])), (bx[0:DC - P, 1:2], column(ln_x_b[P:DC])),
                    (qg[0:DH, :], column(qn_g)), (qg[DH:P, :], column(qn_g)),
                    (kg[0:DH, :], column(kn_g)), (kg[DH:P, :], column(kn_g)),
                    (qg_row[:], wide(qn_g).to_broadcast([P, DH])), (kg_row[:], wide(kn_g).to_broadcast([P, DH])),
                    (gate_raw[:, 0:1], wide(g_xattn).to_broadcast([P, 1])),
                    (gate_raw[:, 1:2], wide(g_ffn).to_broadcast([P, 1])),
                    (bo_row[:], wide(bo).to_broadcast([P, D])),
                    (router[:], w_router.rearrange("(c p) e -> p c e", p=P)),
                ):
                    sp.dma_start(dst, src).then_inc(consts_loaded, 16)
                sp.dma_start(w1_raw[:], w1[0].rearrange("(c p) h -> p c h", p=P)).then_inc(raw_loaded, 16)
                sp.dma_start(w2_raw[:], w2[0].rearrange("(c p) d -> p c d", p=P)).then_inc(raw_loaded, 16)
                sp.wait_ge(zero_ready, 1)
                sp.dma_start(total[NTOK:NTOK + TM].rearrange("(t p) d -> p t d", p=P),
                             pad_rows[:, :, 0:D]).then_inc(dump_zeroed, 16)
                with sp.Fori(0, B - 1) as b:
                    sp.wait_ge(xn_ready, b * 3 + 3)
                    sp.sem_inc(passed, 1)
                    sp.wait_ge(xb_ready, b + 1)
                    sp.wait_ge(mask_ready, b + 1)
                    load_sequence(sp, b + 1)
                    store_tokens(sp, b)
                store_tokens(sp, B - 1)
                sp.wait_ge(x2_stored, 16 * B)
                sp.wait_ge(dump_zeroed, 16)
                sp.wait_ge(raw_loaded, 32)

            @block.gpsimd
            def _(pool):
                pool.memset(ident[:], 0.0).then_inc(pool_const, 1)
                pool.memset(tri[:], 1.0).then_inc(pool_const, 1)
                pool.memset(ones[:], 1.0).then_inc(pool_const, 1)
                pool.memset(minus_half[:], -0.5).then_inc(pool_const, 1)
                pool.memset(pad_rows[:], 0.0).then_inc(pool_const, 1)
                pool.memset(var_in[:], 1.0).then_inc(pool_const, 1)
                pool.memset(base[:], 0.0).then_inc(pool_const, 1)
                for pad in (gx[:], bx[:], cn[:, DC:2 * P], wst_c[:, :, DC:2 * P], lc_hi[:, :, SC:P], lc_lo[:, :, SC:P],
                            K1[:, :, S + SC:S + P], K2[:, :, S + SC:S + P]):
                    pool.memset(pad if pad.dtype == F32 else pad.bitcast(F32), 0.0).then_inc(pool_const, 1)
                pool.memset(Vt[:], 1.0).then_inc(pool_const, 1)
                pool.wait_ge(pool_const, NPOOL)
                pool.affine_select(out=ident[:], in_=ident[:], compare_op=ALU.not_equal, fill=1.0, base=0,
                                   pattern=[[-1, P]], channel_multiplier=1).then_inc(ident_ready, 1)
                pool.affine_select(out=tri[:], in_=tri[:], compare_op=ALU.is_gt, fill=0.0, base=0,
                                   pattern=[[1, P]], channel_multiplier=-1).then_inc(ident_ready, 1)
                pool.iota(iota_i[:, 0:8], [[1, 8]], base=0, channel_multiplier=0).then_inc(iota_done, 1)
                pool.iota(iota_i[:, 8:16], [[P, 8]], base=0, channel_multiplier=1).then_inc(iota_done, 1)
                pool.engine_nop().then_inc(zero_ready, 1)

                with pool.Fori(0, B) as b:
                    pool.wait_ge(var_ready, b + 1)
                    pool.tensor_tensor(rstd[:], var_in[:], minus_half[:, 0:NT], ALU.pow).then_inc(rstd_ready, 1)
                    for t in range(NT):
                        n = 8 if t < T else H
                        p = P if t < T else SC
                        pool.wait_ge(ssm_ready, b * NT + (t + 1))
                        pool.tensor_tensor(rr[0:p, t % 2, 0:n], ssm[0:p, t % 2, 0:n], minus_half[0:p, 0:n],
                                           ALU.pow).then_inc(rr_ready, 1)
                    pool.wait_ge(dve_const, 6)
                    pool.wait_ge(seq_loaded, b * 48 + 48)
                    pool.tensor_tensor(xb[:], xr[:], tbo[:].unsqueeze(1).to_broadcast([P, T, D]),
                                       ALU.add).then_inc(xb_ready, 1)
                    pool.wait_ge(var2_ready, b + 1)
                    pool.tensor_tensor(rstd2[:], var2[:], minus_half[:, 0:T], ALU.pow).then_inc(rstd2_ready, 1)
                    pool.wait_ge(slots_ready, b + 1)
                    pool.wait_ge(y2_ready, b + 1)
                    pool.sem_inc(passed, 1)
                    for t in range(T):
                        for k in range(2):
                            pool.indirect_dma_start(routed, bass.IndirectOffsetOnAxis(ap=slot_i[:, k, t:t + 1], axis=0),
                                                    rows[k][:, t, :], None,
                                                    bounds_check=NE * REGION - 1).then_inc(scattered, 16)
                    pool.wait_ge(scattered, b * (32 * T) + 32 * T)
                    pool.wait_ge(x2_stored, b * 16 + 16)
                    pool.sem_inc(passed, 1)

            @block.scalar
            def _(act):
                act.wait_ge(consts_loaded, 16 * NCONST)
                act.activation(gate[:], gate_raw[:], ACT.Tanh).then_inc(gate_ready, 1)
                for g, (src, dst, _) in enumerate(weight_groups()):
                    act.wait_ge(wT_done, g + 1)
                    act.activation(dst, src, ACT.Copy).then_inc(w_hi_ready, 1)

                with act.Fori(0, B) as b:
                    for g in range(GROUPS):
                        act.wait_ge(lnf_ready, b * GROUPS + (g + 1))
                        src, hi, _ = norm_group(g)
                        act.activation(hi, src, ACT.Copy).then_inc(ln_hi_ready, 1)

                    def read_projection(t):
                        act.wait_ge(proj_done, b * NT + (t + 1))
                        if t >= 3:
                            act.wait_ge(qkd_ready, b * NT + (t - 2))
                        if t >= 2:
                            act.wait_ge(ss_ready, b * NT + (t - 1))
                        o = psO[t % 2]
                        if t < T:
                            act.activation(qk_sb[:, t % 3, :], o[:, 0:QK], ACT.Copy)
                            act.activation(sq[:, t % 2, :], o[:, 0:QK], ACT.Square)
                            act.activation(value_slots(t, P), o[:, QK:QK + H * DH].rearrange(
                                "p (i s d) -> p i s d", i=2, s=2), ACT.Copy).then_inc(proj_read, 1)
                        else:
                            act.activation(qk_sb[0:SC, t % 3, 0:H * DH], o[0:SC, 0:H * DH], ACT.Copy)
                            act.activation(sq[0:SC, t % 2, 0:H * DH], o[0:SC, 0:H * DH], ACT.Square)
                            act.activation(value_slots(t, SC), o[0:SC, H * DH:2 * H * DH].rearrange(
                                "p (i s d) -> p i s d", i=2, s=2), ACT.Copy).then_inc(proj_read, 1)

                    def heads_hi(t):
                        act.wait_ge(qkT_done, b * NT + (t + 1))
                        ps = psS[t % 2]
                        if t < T:
                            act.activation(Q1[:, :, t * P:(t + 1) * P], ps[:, 0:512].rearrange("p (h n) -> p h n", h=H),
                                           ACT.Copy, scale=gqk[:, 0:1])
                            act.activation(K1[:, :, t * P:(t + 1) * P], ps[:, 512:1024].rearrange("p (h n) -> p h n", h=H),
                                           ACT.Copy).then_inc(qk_hi_ready, 1)
                        else:
                            act.activation(K1[:, :, S:S + SC], ps[:, 512:512 + H * SC].rearrange("p (h n) -> p h n", h=H),
                                           ACT.Copy).then_inc(qk_hi_ready, 1)

                    act.wait_ge(dve_const, 6)
                    for t in range(NT + 2):
                        if t < NT:
                            read_projection(t)
                        if t >= 2:
                            heads_hi(t - 2)

                    def attention_hi(c):
                        act.wait_ge(o_read, b * H + 2 * (c + 1))
                        act.activation(att_hi[:, c, :], attf[:, c, :], ACT.Copy).then_inc(att_hi_ready, 1)

                    act.wait_ge(mask_ready, b + 1)
                    for i in range(NI):
                        h, kt = divmod(i, KT)
                        p = P if kt < T else SC
                        bias = shift[:, 0:1] if kt < T else mask_bias[:, 0:1]
                        act.wait_ge(s_done, b * NI + (i + 1))
                        if i >= NP_RING:
                            act.wait_ge(av_done, b * NI + (i - NP_RING + 1))
                        act.activation(pr[i % NP_RING][0:p, :], psS[i % 2][0:p, :], ACT.Exp, bias=bias).then_inc(exp_done, 1)
                        if kt == 4 and h == 2:
                            attention_hi(0)
                    attention_hi(1)

                    for hb in range(2):
                        act.wait_ge(yT_done, b * 2 + (hb + 1))
                        act.activation(yT[:, :, hb * HALF:(hb + 1) * HALF],
                                       psO[hb][:].rearrange("p (c n) -> p c n", c=EC), ACT.Copy).then_inc(yT_ready, 1)
                    act.wait_ge(route, b * ROUTE + 3)
                    act.activation(pe_[:], lz[:], ACT.Exp).then_inc(ez_ready, 1)
                    act.wait_ge(y_ready, b * T + T)
                    act.activation(rows[1][:, :, 0:D], rows[0][:, :, 0:D], ACT.Copy).then_inc(y2_ready, 1)

            @block.vector
            def _(dve):
                dve.wait_ge(iota_done, 2)
                dve.tensor_copy(expert_id[:], iota_i[:, 0:8])
                dve.tensor_copy(token_id[:], iota_i[:, 8:16])
                dve.tensor_scalar(region0[:], iota_i[:, 0:8], float(REGION), None, ALU.mult).then_inc(dve_const, 1)
                dve.wait_ge(zero_ready, 1)
                dve.wait_ge(dump_zeroed, 16)
                dve.tensor_scalar(pad_rows[:, :, D:D + 1].rearrange("p m a -> p (m a)"), iota_i[:, 8:8 + MH],
                                  float(NTOK), None, ALU.add).then_inc(dve_const, 1)
                dve.wait_ge(consts_loaded, 16 * NCONST)
                dve.tensor_tensor(qg_row[:], qg_row[:], kg_row[:], ALU.mult).then_inc(dve_const, 1)
                dve.scalar_tensor_tensor(out=gqk[:], in0=qg[:], scalar=SCALE, in1=kg[:], op0=ALU.mult,
                                         op1=ALU.mult).then_inc(dve_const, 1)
                dve.wait_ge(dve_const, 3)
                dve.tensor_reduce(shift[:], qg_row[:], AX, ALU.max, apply_absolute_value=True).then_inc(dve_const, 1)
                dve.wait_ge(gate_ready, 1)
                dve.tensor_scalar(tbo[:], bo_row[:], gate[:, 0:1], None, ALU.mult).then_inc(dve_const, 1)
                dve.wait_ge(dve_const, 5)
                dve.tensor_scalar(shift[:], shift[:], -SCALE * DH, SAFE, ALU.mult, ALU.add).then_inc(dve_const, 1)
                dve.wait_ge(dve_const, 7)
                dve.tensor_scalar(shift[:], shift[:], 0.0, None, ALU.min).then_inc(dve_const, 1)
                dve.wait_ge(dve_const, 8)
                for g, (src, hi, lo) in enumerate(weight_groups()):
                    dve.wait_ge(w_hi_ready, g + 1)
                    dve.tensor_tensor(lo, src, hi.bitcast(F32), ALU.subtract).then_inc(w_ready, 1)

                with dve.Fori(0, B) as b:
                    dve.wait_ge(seq_loaded, b * 48 + 48)
                    dve.bn_stats(stats[0:SC, T, :], cr[:])
                    for t in range(T):
                        dve.bn_stats(stats[:, t, :], xr[:, t, :]).then_inc(stat_ready, 1)
                    dve.wait_ge(pool_const, NPOOL)
                    dve.wait_ge(stat_ready, b * T + T)
                    dve.sem_inc(passed, 1)
                    for t in range(T):
                        dve.bn_aggr(mv[:, t, :], stats[:, t, :])
                    dve.bn_aggr(mv[0:SC, T, :], stats[0:SC, T, :]).then_inc(mv_ready, 1)
                    dve.wait_ge(mv_ready, b + 1)
                    dve.tensor_scalar(var_in[:, 0:T], mv[:, 0:T, 1], 1.0 + EPS, EPS * EPS, ALU.mult, ALU.add)
                    dve.tensor_scalar(var_in[0:SC, T:NT], mv[0:SC, T, 1:2], EPS, None, ALU.add).then_inc(var_ready, 1)
                    dve.tensor_scalar(mask_bias[:], mask_u8[:], 3e38, -3e38, ALU.mult, ALU.add).then_inc(mask_cut, 1)
                    dve.wait_ge(mask_cut, b + 1)
                    dve.tensor_tensor(mask_bias[:], mask_bias[:], shift[0:SC, :], ALU.min).then_inc(mask_ready, 1)
                    dve.wait_ge(rstd_ready, b + 1)
                    dve.tensor_scalar(cn[:, 0:DC], cr[:], mv[0:SC, T, 0:1], rstd[0:SC, T:NT], ALU.subtract,
                                      ALU.mult).then_inc(xn_ready, 1)
                    for t in range(T):
                        ins = dve.tensor_scalar(xn[:, t, :], xr[:, t, :], mv[:, t, 0:1], rstd[:, t:t + 1], ALU.subtract, ALU.mult)
                        if t % HT == HT - 1:
                            ins.then_inc(xn_ready, 1)

                    def norm_affine(g):
                        dve.wait_ge(xT_done, b * GROUPS + (g + 1))
                        if g >= 2:
                            dve.wait_ge(ln_hi_ready, b * GROUPS + (g - 1))
                            dve.wait_ge(ln_ready, b * GROUPS + (g - 1))
                        ga, be = (gx, bx) if g < 2 else (gl, bl)
                        c = g if g < 2 else (g - 2) % EC
                        dst, _, _ = norm_group(g)
                        dve.tensor_scalar(dst, norm_psum(g), ga[:, c:c + 1], be[:, c:c + 1], ALU.mult,
                                          ALU.add).then_inc(lnf_ready, 1)

                    def norm_lo(g):
                        dve.wait_ge(ln_hi_ready, b * GROUPS + (g + 1))
                        src, hi, lo = norm_group(g)
                        dve.tensor_tensor(lo, src, hi.bitcast(F32), ALU.subtract).then_inc(ln_ready, 1)

                    for g in range(GROUPS + 1):
                        if g < GROUPS:
                            norm_affine(g)
                        if g >= 1:
                            norm_lo(g - 1)

                    def mean_squares(t):
                        p, n = (P, 8) if t < T else (SC, H)
                        dve.wait_ge(proj_read, b * NT + (t + 1))
                        if t >= 2:
                            dve.wait_ge(rr_ready, b * NT + (t - 1))
                        dve.tensor_reduce(ss[0:p, t % 2, 0:n], sq[0:p, t % 2, 0:n * DH].rearrange("p (h d) -> p h d", d=DH),
                                          AX, ALU.add).then_inc(ss_ready, 1)
                        dve.wait_ge(ss_ready, b * NT + (t + 1))
                        dve.tensor_scalar(ssm[0:p, t % 2, 0:n], ss[0:p, t % 2, 0:n], 1.0 / DH, RMS_EPS * RMS_EPS, ALU.mult,
                                          ALU.max).then_inc(ssm_ready, 1)

                    def scale_heads(t):
                        p, n = (P, 8) if t < T else (SC, H)
                        dve.wait_ge(rr_ready, b * NT + (t + 1))
                        if t >= 2:
                            dve.wait_ge(qkT_done, b * NT + (t - 1))
                        for k in range(2):
                            ins = dve.tensor_tensor(
                                qkd[0:p, t % 2, 0:n * P].rearrange("p (h k d) -> p h k d", k=2, d=DH)[:, :, k, :],
                                qk_sb[0:p, t % 3, 0:n * DH].rearrange("p (h d) -> p h d", d=DH),
                                rr[0:p, t % 2, 0:n].unsqueeze(2).to_broadcast([p, n, DH]), ALU.mult)
                        ins.then_inc(qkd_ready, 1)

                    def heads_lo(t):
                        dve.wait_ge(qk_hi_ready, b * NT + (t + 1))
                        ps = psS[t % 2]
                        if t < T:
                            cols = slice(t * P, (t + 1) * P)
                            q_lo = Q1[DH:P, :, cols]
                            dve.scalar_tensor_tensor(out=q_lo, in0=ps[DH:P, 0:512].rearrange("p (h n) -> p h n", h=H),
                                                     scalar=gqk[DH:P, 0:1], in1=q_lo.bitcast(F32), op0=ALU.mult,
                                                     op1=ALU.subtract)
                            dve.tensor_tensor(K2[:, :, cols], ps[0:DH, 512:1024].rearrange("p (h n) -> p h n", h=H),
                                              K1[0:DH, :, cols].bitcast(F32), ALU.subtract).then_inc(qk_ready, 1)
                        else:
                            dve.tensor_tensor(K2[:, :, S:S + SC], ps[0:DH, 512:512 + H * SC].rearrange("p (h n) -> p h n", h=H),
                                              K1[0:DH, :, S:S + SC].bitcast(F32), ALU.subtract).then_inc(qk_ready, 1)

                    for t in range(NT + 2):
                        if t < NT:
                            mean_squares(t)
                        if 1 <= t <= NT:
                            scale_heads(t - 1)
                        if t >= 2:
                            heads_lo(t - 2)

                    for h in range(H):
                        v0 = 0 if h % 2 == 0 else DH
                        d0 = DH - v0
                        dve.wait_ge(av_done, b * NI + KT * (h + 1))
                        dve.reciprocal(den[v0:v0 + DH, :], psO[h % 2][d0:d0 + DH, :]).then_inc(den_ready, 1)
                        dve.wait_ge(den_ready, b * H + (h + 1))
                        dve.tensor_tensor(attf[v0:v0 + DH, h // 2, :], psO[h % 2][v0:v0 + DH, :], den[v0:v0 + DH, :],
                                          ALU.mult).then_inc(o_read, 1)
                        if h % 2 == 1:
                            c = h // 2
                            dve.wait_ge(att_hi_ready, b * EC + (c + 1))
                            dve.tensor_tensor(att_lo[:, c, :], attf[:, c, :], att_hi[:, c, :].bitcast(F32),
                                              ALU.subtract).then_inc(att_ready, 1)

                    dve.wait_ge(xb_ready, b + 1)
                    for t in range(T):
                        dve.wait_ge(o_done, b * T + (t + 1))
                        dve.scalar_tensor_tensor(out=xb[:, t, :], in0=out_psum(t), scalar=gate[:, 0:1], in1=xb[:, t, :],
                                                 op0=ALU.mult, op1=ALU.add).then_inc(x2_ready, 1)
                        dve.wait_ge(x2_ready, b * T + (t + 1))
                        dve.bn_stats(st2[:, t, :], xb[:, t, :]).then_inc(st2_ready, 1)
                    dve.wait_ge(st2_ready, b * T + T)
                    dve.sem_inc(passed, 1)
                    for t in range(T):
                        ins = dve.bn_aggr(mv2[:, t, :], st2[:, t, :])
                    ins.then_inc(mv2_ready, 1)
                    dve.wait_ge(mv2_ready, b + 1)
                    dve.tensor_scalar(var2[:], mv2[:, :, 1], EPS, None, ALU.add).then_inc(var2_ready, 1)
                    dve.wait_ge(rstd2_ready, b + 1)
                    for t in range(T):
                        dve.tensor_scalar(rows[0][:, t, 0:D], xb[:, t, :], mv2[:, t, 0:1], rstd2[:, t:t + 1], ALU.subtract,
                                          ALU.mult).then_inc(y_ready, 1)

                    step = [0]

                    def then_step(ins):
                        step[0] += 1
                        ins.then_inc(route, 1)
                        dve.wait_ge(route, b * ROUTE + step[0])

                    wide = lambda a: a.unsqueeze(2).to_broadcast([P, T, NE])
                    experts = expert_id[:].unsqueeze(1).to_broadcast([P, T, NE])
                    dve.wait_ge(logits_done, b + 1)
                    then_step(dve.tensor_copy(lg[:], psS[0][:, 0:T * NE].rearrange("p (t e) -> p t e", t=T)))
                    then_step(dve.tensor_reduce(lmax[:], lg[:], AX, ALU.max))
                    then_step(dve.tensor_tensor(lz[:], lg[:], wide(lmax[:]), ALU.subtract))
                    dve.wait_ge(ez_ready, b + 1)
                    then_step(dve.tensor_reduce(psum_[:], pe_[:], AX, ALU.add))
                    then_step(dve.reciprocal(psum_[:], psum_[:]))
                    then_step(dve.tensor_tensor(prob[:], pe_[:], wide(psum_[:]), ALU.mult))
                    p_now = prob
                    for k in range(2):
                        then_step(dve.tensor_reduce(top[:, k, :], p_now[:], AX, ALU.max))
                        then_step(dve.tensor_tensor(eq[:], p_now[:], wide(top[:, k, :]), ALU.is_equal))
                        then_step(dve.scalar_tensor_tensor(out=cand[:], in0=eq[:], scalar=-float(NE), in1=experts, op0=ALU.mult,
                                                           op1=ALU.add))
                        then_step(dve.tensor_reduce(pick[:, k, :], cand[:], AX, ALU.min))
                        then_step(dve.tensor_tensor(hot[:, k], cand[:], wide(pick[:, k, :]), ALU.is_equal))
                        if k == 0:
                            then_step(dve.scalar_tensor_tensor(out=prob2[:], in0=hot[:, 0], scalar=-2.0, in1=prob[:], op0=ALU.mult,
                                                               op1=ALU.add))
                            p_now = prob2
                    dve.tensor_tensor(chosen[:].rearrange("p (t e) -> p t e", t=T), hot[:, 0], hot[:, 1],
                                      ALU.add).then_inc(chosen_ready, 1)
                    for k in range(2):
                        dve.tensor_scalar(rows[k][:, :, D:D + 1].rearrange("p t a -> p (t a)"), token_id[:], 0.0, None, ALU.add)
                        ins = dve.tensor_scalar(rows[k][:, :, D + 1:D + 2].rearrange("p t a -> p (t a)"), top[:, k, :], gate[:, 1:2],
                                                None, ALU.mult)
                    then_step(ins)
                    dve.tensor_scalar(token_id[:], token_id[:], float(S), None, ALU.add)
                    dve.wait_ge(rank_done, b + 1)
                    for t in range(T):
                        dve.tensor_tensor(base[:, t + 1, :], base[:, t, :], psS[1][:, HALF + t * NE:HALF + (t + 1) * NE],
                                          ALU.add).then_inc(base_ready, 1)
                        dve.wait_ge(base_ready, b * (T + 2) + (t + 1))
                    then_step(dve.tensor_tensor(slot[:], psS[1][:, 0:T * NE].rearrange("p (t e) -> p t e", t=T), base[:, 0:T, :], ALU.add))
                    then_step(dve.tensor_tensor(slot[:], slot[:], region0[:].unsqueeze(1).to_broadcast([P, T, NE]), ALU.add))
                    then_step(dve.tensor_tensor(slot_hot[:], hot[:], slot[:].unsqueeze(1).to_broadcast([P, 2, T, NE]), ALU.mult))
                    dve.tensor_reduce(slot_f[:], slot_hot[:], AX, ALU.add).then_inc(base_ready, 1)
                    dve.wait_ge(base_ready, b * (T + 2) + T + 1)
                    dve.tensor_copy(base[:, 0, :], base[:, T, :]).then_inc(base_ready, 1)
                    dve.tensor_copy(slot_i[:], slot_f[:]).then_inc(slots_ready, 1)
                    assert step[0] == ROUTE, step[0]
                    dve.wait_ge(base_ready, b * (T + 2) + T + 2)
                    dve.sem_inc(passed, 1)

                plan_step = [0]

                def then_plan(ins):
                    plan_step[0] += 1
                    ins.then_inc(plan_ready, 1)
                    dve.wait_ge(plan_ready, plan_step[0])

                then_plan(dve.tensor_scalar(tiles_i[:], base[:, 0, :], float(TM - 1), None, ALU.add))
                then_plan(dve.tensor_scalar(tiles_i[:], tiles_i[:], TM.bit_length() - 1, None, ALU.arith_shift_right))
                dve.memset(plan_f[:, 2 * NE:2 * NE + 1], 0.0)
                dve.tensor_copy(plan_f[:, 0:NE], base[:, 0, :])
                then_plan(dve.tensor_copy(plan_f[:, NE:2 * NE], tiles_i[:]))
                for e in range(1, NE):
                    then_plan(dve.tensor_tensor(plan_f[:, 2 * NE + e:2 * NE + e + 1], plan_f[:, 2 * NE + e - 1:2 * NE + e],
                                                plan_f[:, NE + e - 1:NE + e], ALU.add))
                then_plan(dve.tensor_copy(plan[:], plan_f[:]))

            @block.tensor
            def _(pe):
                pe.wait_ge(ident_ready, 2)
                pe.wait_ge(pool_const, NPOOL)
                pe.wait_ge(weights_loaded, 64)
                rows_qk = [wst_q[:, 0], wst_q[:, 1], wst_l[:, 0], wst_l[:, 1]]
                rows_v = [wst_l[:, 2], wst_l[:, 3]]
                turned = [(psS[0], c * HALF + j * P, rows_qk[j][:, c * P:(c + 1) * P], c) for c in range(EC) for j in range(4)]
                turned += [(psS[1], c * D + j * P, rows_v[j][:, c * P:(c + 1) * P], 2) for c in range(EC) for j in range(2)]
                turned += [(psS[1], HALF + c * D + j * P, wst_o[:, j, c * P:(c + 1) * P], 3) for c in range(EC) for j in range(2)]
                turned += [(psO[0], c * HALF + j * P, wst_c[:, j, c * P:(c + 1) * P], 4 + c) for c in range(2) for j in range(4)]
                for n, (ps, col, src, g) in enumerate(turned):
                    ins = pe.transpose(ps[:, col:col + P], src, ident[:])
                    if n + 1 == len(turned) or turned[n + 1][3] != g:
                        ins.then_inc(wT_done, 1)
                pe.wait_ge(w_ready, GROUPS_W)

                def passes(o, parts):
                    for n, (l, r) in enumerate(parts):
                        ins = pe.matmul(o, l, r, start=(n == 0), stop=(n == len(parts) - 1))
                    return ins

                with pe.Fori(0, B) as b:
                    pe.wait_ge(xn_ready, b * 3 + 1)
                    pe.sem_inc(passed, 1)
                    pe.transpose(psO[0][:, 0:SC], cn[:, 0:P], ident[0:SC, 0:SC]).then_inc(xT_done, 1)
                    pe.transpose(psO[0][:, HALF:HALF + SC], cn[:, P:2 * P], ident[0:SC, 0:SC]).then_inc(xT_done, 1)
                    for hb in range(2):
                        pe.wait_ge(xn_ready, b * 3 + (hb + 2))
                        for c in range(EC):
                            for t in range(HT):
                                ins = pe.transpose(psS[hb][:, c * HALF + t * P:c * HALF + (t + 1) * P],
                                                   xn[:, hb * HT + t, c * P:(c + 1) * P], ident[:])
                            ins.then_inc(xT_done, 1)

                    def project(t):
                        if t in (0, HT):
                            pe.wait_ge(ln_ready, b * GROUPS + (4 if t == 0 else 6))
                        if t >= 2:
                            pe.wait_ge(proj_read, b * NT + (t - 1))
                        o = psO[t % 2]
                        if t < T:
                            cols = slice(t * P, (t + 1) * P)
                            pairs = lambda f: [p for c in range(EC) for p in (
                                (ln_hi[:, c, cols], w_hi[:, c, f]), (ln_hi[:, c, cols], w_lo[:, c, f]),
                                (ln_lo[:, c, cols], w_hi[:, c, f]))]
                            passes(o[:, 0:QK], pairs(slice(0, QK)))
                            passes(o[:, QK:QK + H * DH], pairs(slice(QK, QK + H * DH))).then_inc(proj_done, 1)
                        else:
                            passes(o[:, 0:2 * H * DH], [p for c in range(2) for p in (
                                (lc_hi[:, c, :], wc_hi[:, c, :]), (lc_hi[:, c, :], wc_lo[:, c, :]),
                                (lc_lo[:, c, :], wc_hi[:, c, :]))]).then_inc(proj_done, 1)

                    def turn_heads(t):
                        if t >= 2:
                            pe.wait_ge(qk_ready, b * NT + (t - 1))
                        pe.wait_ge(qkd_ready, b * NT + (t + 1))
                        if t == T:
                            pe.sem_inc(passed, 1)
                        p, n = (P, 2 * H) if t < T else (SC, H)
                        for j in range(n):
                            col = (j if t < T else H) * P if t < T else HALF + j * SC
                            ins = pe.transpose(psS[t % 2][:, col:col + p], qkd[0:p, t % 2, j * P:(j + 1) * P], ident[0:p, 0:p])
                        ins.then_inc(qkT_done, 1)

                    for t in range(NT + 2):
                        if t < NT:
                            project(t)
                        if t >= 2:
                            turn_heads(t - 2)

                    def scores(i):
                        h, kt = divmod(i, KT)
                        if i >= 2:
                            pe.wait_ge(exp_done, b * NI + (i - 1))
                        keys = slice(kt * P, (kt + 1) * P)
                        for n in range(2):
                            pe.matmul(psS[i % 2][:, n * HALF:(n + 1) * HALF], K1[:, h, keys], Q1[:, h, n * HALF:(n + 1) * HALF],
                                      start=True, stop=False)
                        for n in range(2):
                            ins = pe.matmul(psS[i % 2][:, n * HALF:(n + 1) * HALF], K2[:, h, keys],
                                            Q1[0:DH, h, n * HALF:(n + 1) * HALF], start=False, stop=True)
                        ins.then_inc(s_done, 1)

                    def values(i):
                        h, kt = divmod(i, KT)
                        pe.wait_ge(exp_done, b * NI + (i + 1))
                        if kt == 0 and h >= 2:
                            pe.wait_ge(o_read, b * H + (h - 1))
                        p = P if kt < T else SC
                        for n in range(2):
                            ins = pe.matmul(psO[h % 2][:, n * HALF:(n + 1) * HALF], Vt[0:p, kt, h * P:(h + 1) * P],
                                            pr[i % NP_RING][0:p, n * HALF:(n + 1) * HALF], start=(kt == 0), stop=(kt == KT - 1))
                        ins.then_inc(av_done, 1)

                    pe.wait_ge(qk_ready, b * NT + NT)
                    for i in range(NI + 1):
                        if i < NI:
                            scores(i)
                        if i >= 1:
                            values(i - 1)

                    pe.wait_ge(att_ready, b * EC + EC)
                    for t in range(T):
                        if t >= 4:
                            pe.wait_ge(x2_ready, b * T + (t - 3))
                        cols = slice(t * P, (t + 1) * P)
                        passes(out_psum(t), [p for c in range(EC) for p in (
                            (att_hi[:, c, cols], wo_hi[:, c, :]), (att_hi[:, c, cols], wo_lo[:, c, :]),
                            (att_lo[:, c, cols], wo_hi[:, c, :]))]).then_inc(o_done, 1)

                    for hb in range(2):
                        pe.wait_ge(y_ready, b * T + HT * (hb + 1))
                        for c in range(EC):
                            for t in range(HT):
                                ins = pe.transpose(psO[hb][:, c * HALF + t * P:c * HALF + (t + 1) * P],
                                                   rows[0][:, hb * HT + t, c * P:(c + 1) * P], ident[:])
                        ins.then_inc(yT_done, 1)
                    for t in range(T):
                        pe.wait_ge(yT_ready, b * 2 + (t // HT + 1))
                        ins = passes(psS[0][:, t * NE:(t + 1) * NE], [(yT[:, c, t * P:(t + 1) * P], router[:, c, :]) for c in range(EC)])
                    ins.then_inc(logits_done, 1)
                    pe.wait_ge(chosen_ready, b + 1)
                    pe.matmul(psS[1][:, 0:T * NE], tri[:], chosen[:], start=True, stop=True)
                    pe.matmul(psS[1][:, HALF:HALF + T * NE], ones[:], chosen[:], start=True, stop=True).then_inc(rank_done, 1)
                    pe.wait_ge(slots_ready, b + 1)

        experts_phase(nc, plan, pad_rows, ident, w1_raw, w2_raw, w1, b1, w2, b2, routed, total, out)


def experts_phase(nc, plan, pad_rows, ident, w1_raw, w2_raw, w1, b1, w2, b2, routed, total, out):
    NE, D, HID = w1.shape
    EC, HC = D // P, HID // P
    MH, ROW = pad_rows.shape[1:]
    TM = MH * P
    REGION = routed.shape[0] // NE
    NTOK = REGION - TM
    MAXT = NTOK // TM
    NQ = HC // 2

    with ExitStack() as ctx:
        def sb(name, shape, dt=F32):
            return ctx.enter_context(nc.sbuf_tensor(name, shape, dt))

        def sem(name):
            return ctx.enter_context(nc.semaphore(name))

        w1_hi = [sb(f"w1_hi{s}", [P, EC, HID], F32R) for s in range(2)]
        w1_lo = [sb(f"w1_lo{s}", [P, EC, HID], F32R) for s in range(2)]
        w2_hi = [sb(f"w2_hi{s}", [P, HC, D], F32R) for s in range(2)]
        w2_lo = [sb(f"w2_lo{s}", [P, HC, D], F32R) for s in range(2)]
        b1_col = [sb(f"b1_col{s}", [P, HC]) for s in range(2)]
        b2_row = [sb(f"b2_row{s}", [P, D]) for s in range(2)]
        xrow = sb("xrow", [P, MH, ROW])
        xT_hi = sb("xT_hi", [P, EC, TM], F32R)
        xT_lo = sb("xT_lo", [P, EC, TM], F32R)
        g32 = sb("g32", [P, 2, 2 * TM])
        g_hi = sb("g_hi", [P, HC, TM], F32R)
        g_lo = sb("g_lo", [P, HC, TM], F32R)
        meta_next = sb("meta_next", [P, MH, 2])
        meta_now = sb("meta_now", [P, MH, 2])
        token_i = sb("token_i", [P, MH], I32)
        y1 = sb("y1", [P, MH, D])
        y_out = sb("y_out", [P, MH, D])

        psH = [ctx.enter_context(nc.psum_tensor(f"psH{i}", [P, 2 * TM], F32)) for i in range(NQ)]
        psX = ctx.enter_context(nc.psum_tensor("psX", [P, EC, TM], F32))
        psY = [ctx.enter_context(nc.psum_tensor(f"psY{i}", [P, 512], F32)) for i in range(MH)]

        pads_filled = sem("pads_filled")
        x_loaded = sem("x_loaded")
        xT_done = sem("xT_done2")
        meta_taken = sem("meta_taken")
        meta_moved = sem("meta_moved")
        xT_hi_ready = sem("xT_hi_ready")
        xT_ready = sem("xT_ready")
        raw_loaded = sem("raw_loaded2")
        bias_loaded = sem("bias_loaded")
        w_hi_ready = sem("w_hi_ready2")
        w_ready = sem("w_ready2")
        h_done = sem("h_done")
        gelu_done = sem("gelu_done")
        g_hi_ready = sem("g_hi_ready")
        g_ready = sem("g_ready")
        y_done = sem("y_done")
        y_read = sem("y_read")
        y_ready = sem("y_ready2")
        added = sem("added")
        rows_free = sem("rows_free")
        out_stored = sem("out_stored")
        passed = sem("passed2")

        def tiles_of(eng, body, start=None):
            with eng.Fori(0, NE // 2) as e2:
                for s in range(2):
                    e = e2 * 2 + s
                    n = eng.value_load(plan[0:1, bass.ds(e + NE, 1)], min_val=0, max_val=MAXT)
                    before = eng.value_load(plan[0:1, bass.ds(e + 2 * NE, 1)], min_val=0, max_val=MAXT * 2 + NE)
                    if start is not None:
                        start(e2, s, before)
                    with eng.Fori(0, MAXT) as j:
                        with eng.If(j < n):
                            body(e2, s, before + j, j)

        def tiles_in_all(eng):
            n = eng.value_load(plan[0:1, 2 * NE - 1:2 * NE], min_val=0, max_val=MAXT)
            before = eng.value_load(plan[0:1, 3 * NE - 1:3 * NE], min_val=0, max_val=MAXT * 2 + NE)
            return before + n

        def halves(s):
            for c in range(2):
                yield w1_raw[:, c, :], w1_hi[s][:, c, :], w1_lo[s][:, c, :]
            for c in range(2):
                k = slice(c * HC // 2, (c + 1) * HC // 2)
                yield w2_raw[:, k, :], w2_hi[s][:, k, :], w2_lo[s][:, k, :]

        block = ctx.enter_context(nc.Block())

        @block.sync
        def _(sp):
            for e in range(NE):
                n = sp.value_load(plan[0:1, e:e + 1], min_val=0, max_val=NTOK)
                sp.dma_start(routed[bass.ds(n + e * REGION, TM)].rearrange("(m p) r -> p m r", p=P),
                             pad_rows[:]).then_inc(pads_filled, 16)
            sp.wait_ge(pads_filled, 16 * NE)

            def load(row, t):
                sp.wait_ge(xT_done, t + 1)
                sp.wait_ge(meta_taken, t + 1)
                sp.dma_start(xrow[:], routed[bass.ds(row, TM)].rearrange("(m p) r -> p m r", p=P)).then_inc(x_loaded, 16)

            tiles_of(sp, lambda e2, s, t, j: load(e2 * (2 * REGION) + s * REGION + j * TM, t))
            n = tiles_in_all(sp)
            load(0, n)
            sp.wait_ge(added, n * 32)
            sp.dma_start(out.rearrange("b s d -> (b s) d"), total[0:NTOK]).then_inc(out_stored, 16)
            sp.wait_ge(x_loaded, n * 16 + 16)
            sp.wait_ge(out_stored, 16)
            sp.sem_inc(passed, 1)

        @block.gpsimd
        def _(pool):
            pool.sem_inc(rows_free, 1)
            below = lambda e: nc.s_assert_within(e, 0, NE - 1, skip_runtime_bounds_check_because="it is behind an If on its pair")
            column = lambda e: b1[bass.ds(e, 1)].rearrange("a (c p) -> p (a c)", p=P)
            row = lambda e: b2[bass.ds(e, 1)].to_broadcast([P, D])

            def load_bias(e, s):
                pool.dma_start(b1_col[s][:], column(e)).then_inc(bias_loaded, 16)
                pool.dma_start(b2_row[s][:], row(e)).then_inc(bias_loaded, 16)

            def load_weights(e):
                pool.dma_start(w1_raw[:], w1[bass.ds(e, 1)].rearrange("a (c p) h -> p (a c) h", p=P)).then_inc(raw_loaded, 16)
                pool.dma_start(w2_raw[:], w2[bass.ds(e, 1)].rearrange("a (c p) d -> p (a c) d", p=P)).then_inc(raw_loaded, 16)

            load_bias(0, 0)
            pool.wait_ge(w_ready, 4)
            load_weights(1)

            def start(e2, s, before):
                def go():
                    pool.wait_ge(w_ready, e2 * 8 + (4 * s + 8))
                    load_bias(below(e2 * 2 + (s + 1)), 1 - s)
                if s == 0:
                    go()
                with pool.If(e2 < NE // 2 - 1):
                    if s == 1:
                        go()
                    load_weights(below(e2 * 2 + (s + 2)))

            def add_rows(e2, s, t, j):
                pool.wait_ge(y_ready, t + 1)
                pool.sem_inc(passed, 1)
                for m in range(MH):
                    pool.indirect_dma_start(total, bass.IndirectOffsetOnAxis(ap=token_i[:, m:m + 1], axis=0), y_out[:, m, :],
                                            None, bounds_check=NTOK + TM - 1, compute_op=ALU.add).then_inc(added, 16)
                pool.wait_ge(added, t * 32 + 32)
                pool.sem_inc(rows_free, 1)

            tiles_of(pool, add_rows, start)

        @block.scalar
        def _(act):
            act.sem_inc(gelu_done, HC)
            hi_steps = EC + 2

            def weights_hi(e, s):
                if not (isinstance(e, int) and e == 0):
                    act.wait_ge(raw_loaded, e * 32)
                for raw, hi, _ in halves(s):
                    act.activation(hi, raw, ACT.Copy).then_inc(w_hi_ready, 1)

            def turned_hi(t):
                act.wait_ge(xT_done, t + 2)
                act.activation(xT_hi[:], psX[:], ACT.Copy).then_inc(xT_hi_ready, 1)

            def start(e2, s, before):
                def go():
                    act.wait_ge(y_read, before + 1)
                    weights_hi(e2 * 2 + (s + 1), 1 - s)
                if s == 0:
                    go()
                else:
                    with act.If(e2 < NE // 2 - 1):
                        go()
                act.wait_ge(bias_loaded, e2 * 64 + (32 * s + 32))

            def tile(e2, s, t, j):
                for c in range(HC):
                    q = c // 2
                    if c % 2 == 0:
                        act.wait_ge(h_done, t * HC + (c + 2))
                        act.wait_ge(g_ready, t * NQ + (q - 1 + NQ))
                    act.activation(g32[:, q % 2, (c % 2) * TM:(c % 2 + 1) * TM], psH[q][:, (c % 2) * TM:(c % 2 + 1) * TM],
                                   ACT.Gelu_apprx_tanh, bias=b1_col[s][:, c:c + 1]).then_inc(gelu_done, 1)
                turned_hi(t + 1)

            weights_hi(0, 0)
            turned_hi(0)
            tiles_of(act, tile, start)

        @block.vector
        def _(dve):
            dve.sem_inc(meta_taken, 1)
            dve.sem_inc(g_ready, NQ)
            dve.sem_inc(y_read, 1)

            def weights_lo(e, s):
                for k, (raw, hi, lo) in enumerate(halves(s)):
                    dve.wait_ge(w_hi_ready, e * 4 + (k + 1))
                    dve.tensor_tensor(lo, raw, hi.bitcast(F32), ALU.subtract).then_inc(w_ready, 1)

            def turned_lo(t):
                dve.wait_ge(xT_hi_ready, t + 1)
                dve.tensor_tensor(xT_lo[:], psX[:], xT_hi[:].bitcast(F32), ALU.subtract).then_inc(xT_ready, 1)

            def take_meta(t):
                dve.wait_ge(x_loaded, t * 16 + 16)
                dve.tensor_copy(meta_next[:], xrow[:, :, D:ROW]).then_inc(meta_taken, 1)

            def start(e2, s, before):
                def go():
                    dve.wait_ge(y_read, before + 1)
                    weights_lo(e2 * 2 + (s + 1), 1 - s)
                if s == 0:
                    go()
                else:
                    with dve.If(e2 < NE // 2 - 1):
                        go()
                dve.wait_ge(bias_loaded, e2 * 64 + (32 * s + 32))
                dve.sem_inc(passed, 1)

            def tile(e2, s, t, j):
                for q in range(NQ):
                    dve.wait_ge(gelu_done, t * HC + (2 * q + 2 + HC))
                    g = g32[:, q % 2, :].rearrange("p (c n) -> p c n", c=2)
                    dve.tensor_copy(g_hi[:, 2 * q:2 * q + 2, :], g).then_inc(g_hi_ready, 1)
                    dve.wait_ge(g_hi_ready, t * NQ + (q + 1))
                    dve.tensor_tensor(g_lo[:, 2 * q:2 * q + 2, :], g, g_hi[:, 2 * q:2 * q + 2, :].bitcast(F32),
                                      ALU.subtract).then_inc(g_ready, 1)
                dve.wait_ge(meta_taken, t + 2)
                dve.tensor_copy(meta_now[:], meta_next[:]).then_inc(meta_moved, 1)
                turned_lo(t + 1)
                dve.wait_ge(meta_moved, t + 1)
                take_meta(t + 1)
                for m in range(MH):
                    dve.wait_ge(y_done, t * MH + (m + 1))
                    ins = dve.tensor_tensor(y1[:, m, :], psY[m][:, 0:D], b2_row[s][:], ALU.add)
                ins.then_inc(y_read, 1)
                dve.wait_ge(rows_free, t + 1)
                dve.tensor_copy(token_i[:], meta_now[:, :, 0])
                dve.wait_ge(y_read, t + 2)
                for m in range(MH):
                    ins = dve.tensor_scalar(y_out[:, m, :], y1[:, m, :], meta_now[:, m, 1:2], None, ALU.mult)
                ins.then_inc(y_ready, 1)

            weights_lo(0, 0)
            turned_lo(0)
            take_meta(0)
            tiles_of(dve, tile, start)

        @block.tensor
        def _(pe):
            pe.sem_inc(xT_done, 1)

            def turn(t):
                pe.wait_ge(x_loaded, t * 16 + 16)
                for c in range(EC):
                    for m in range(MH):
                        ins = pe.transpose(psX[:, c, m * P:(m + 1) * P], xrow[:, m, c * P:(c + 1) * P], ident[:])
                ins.then_inc(xT_done, 1)

            def tile(e2, s, t, j):
                pe.wait_ge(xT_ready, t + 1)
                pe.wait_ge(w_ready, e2 * 8 + (4 * s + 4))
                for c in range(HC):
                    q = c // 2
                    if c % 2 == 0:
                        pe.wait_ge(gelu_done, t * HC + (2 * q + 2))
                    o = psH[q][:, (c % 2) * TM:(c % 2 + 1) * TM]
                    f = slice(c * P, (c + 1) * P)
                    parts = [p for k in range(EC) for p in ((w1_hi[s][:, k, f], xT_hi[:, k, :]), (w1_hi[s][:, k, f], xT_lo[:, k, :]),
                                                            (w1_lo[s][:, k, f], xT_hi[:, k, :]))]
                    for n, (l, r) in enumerate(parts):
                        ins = pe.matmul(o, l, r, start=(n == 0), stop=(n == len(parts) - 1))
                    ins.then_inc(h_done, 1)
                turn(t + 1)
                pe.wait_ge(y_read, t + 1)
                for q in range(NQ):
                    pe.wait_ge(g_ready, t * NQ + (q + 1 + NQ))
                    for m in range(MH):
                        cols = slice(m * P, (m + 1) * P)
                        for c in (2 * q, 2 * q + 1):
                            for n, (l, r) in enumerate(((g_hi, w2_hi), (g_hi, w2_lo), (g_lo, w2_hi))):
                                ins = pe.matmul(psY[m][:, 0:D], l[:, c, cols], r[s][:, c, :], start=(c == 0 and n == 0),
                                                stop=(c == HC - 1 and n == 2))
                        if q == NQ - 1:
                            ins.then_inc(y_done, 1)

            turn(0)
            tiles_of(pe, tile)


_INS = ['x', 'ctx_768', 'mask_BxS2_bk0', 'g_xattn', 'g_ffn', 'L0_xattn_ln_x_g', 'L0_xattn_ln_x_b', 'L0_xattn_ln_l_g',
        'L0_xattn_ln_l_b', 'L0_xattn_qn_g', 'L0_xattn_kn_g', 'L0_xattn_Wq', 'L0_xattn_Wkv', 'L0_xattn_Wlkv', 'L0_xattn_Wo',
        'L0_xattn_bo', 'L0_ffn_w_router', 'L0_ffn_w1', 'L0_ffn_b1', 'L0_ffn_w2', 'L0_ffn_b2']


def kernel(**inputs):
    import numpy as np
    import concourse.bacc as bacc
    from concourse.bass_utils import run_bass_kernel_spmd

    nc = bacc.Bacc("TRN2", target_bir_lowering=False, num_devices=1)
    arrays, args = {}, []
    for name in _INS:
        a = np.ascontiguousarray(inputs[name])
        arrays[f"in_{name}"] = a
        args.append(nc.dram_tensor(f"in_{name}", a.shape, mybir.dt.from_np(a.dtype), kind="ExternalInput").ap())
    shape = inputs["x"].shape
    out = nc.dram_tensor("out", shape, F32, kind="ExternalOutput").ap()
    flamingo_gated_layer(nc, *args, out)
    r = run_bass_kernel_spmd(nc, [arrays], core_ids=[0])
    return r.results[0]["out"]
```

```python
from contextlib import ExitStack

import concourse.bass as bass
from concourse import mybir

F32 = mybir.dt.float32
F32R = mybir.dt.float32r
BF16 = mybir.dt.bfloat16
I32 = mybir.dt.int32
U8 = mybir.dt.uint8
ALU = mybir.AluOpType
ACT = mybir.ActivationFunctionType
AX = mybir.AxisListType.X

P = 128


def flamingo_gated_layer(nc, x, ctx_768, mask, g_xattn, g_ffn, ln_x_g, ln_x_b, ln_l_g, ln_l_b, qn_g, kn_g,
                         Wq, Wkv, Wlkv, Wo, bo, w_router, w1, b1, w2, b2, out):
    B, S, D = x.shape
    _, SC, DC = ctx_768.shape
    DH = qn_g.shape[0]
    H = Wq.shape[0] // DH
    NE = w_router.shape[1]
    HID = w1.shape[2]
    T = S // P
    NT = T + 1
    EC = D // P
    QK = 2 * H * DH
    HALF = S // 2
    HT = T // 2
    GROUPS_W = 6
    LATENT_GROUPS = 2 * EC
    GROUPS = LATENT_GROUPS + 2
    KT = NT
    NI = H * KT
    OUT_SLOTS = 3
    NP_RING = 3
    EPS, RMS_EPS = 1e-5, 1e-8
    SCALE = float(DH) ** -0.5
    SAFE = 60.0
    TM = 256
    MH = TM // P
    NTOK = B * S
    REGION = NTOK + TM
    ROW = D + 2
    HC = HID // P
    NTILES = 2 * NTOK // TM + NE - 1

    routed = nc.dram_tensor("routed", (NE * REGION + TM, ROW), F32).ap()
    total = nc.dram_tensor("total", (NTOK + TM, D), F32).ap()

    persistent = ExitStack()
    with persistent, nc.allow_non_contiguous_dma(reason="columns of parameters, a few bytes each"):
        pad_rows = persistent.enter_context(nc.sbuf_tensor("pad_rows", [P, MH, ROW], F32))
        pad_at = persistent.enter_context(nc.sbuf_tensor("pad_at", [P, NE], I32))
        tile_row = persistent.enter_context(nc.sbuf_tensor("tile_row", [P, NTILES], I32))
        tile_expert = persistent.enter_context(nc.sbuf_tensor("tile_expert", [P, NTILES], I32))
        tile_last = persistent.enter_context(nc.sbuf_tensor("tile_last", [P, NTILES], I32))
        b1_raw = persistent.enter_context(nc.sbuf_tensor("b1_raw", [P, HC], F32))
        b2_raw = persistent.enter_context(nc.sbuf_tensor("b2_raw", [P, D], F32))
        w1_raw = persistent.enter_context(nc.sbuf_tensor("w1_raw", [P, EC, HID], F32))
        w2_raw = persistent.enter_context(nc.sbuf_tensor("w2_raw", [P, HC, D], F32))
        ident = persistent.enter_context(nc.sbuf_tensor("ident", [P, P], F32))

        with ExitStack() as ctx:
            def sb(name, shape, dt=F32):
                return ctx.enter_context(nc.sbuf_tensor(name, shape, dt))

            def sem(name):
                return ctx.enter_context(nc.semaphore(name))

            w_hi = sb("w_hi", [P, EC, 768], F32R)
            w_lo = sb("w_lo", [P, EC, 768], F32R)
            wo_hi = sb("wo_hi", [P, EC, D], F32R)
            wo_lo = sb("wo_lo", [P, EC, D], F32R)
            wc_hi = sb("wc_hi", [P, 2, 512], F32R)
            wc_lo = sb("wc_lo", [P, 2, 512], F32R)
            router = sb("router", [P, EC, NE])
            tri = sb("tri", [P, P], BF16)
            ones = sb("ones", [P, P], BF16)
            gl = sb("gl", [P, EC])
            bl = sb("bl", [P, EC])
            gx = sb("gx", [P, 2])
            bx = sb("bx", [P, 2])
            qg = sb("qg", [P, 1])
            kg = sb("kg", [P, 1])
            gqk = sb("gqk", [P, 1])
            qg_row = sb("qg_row", [P, DH])
            kg_row = sb("kg_row", [P, DH])
            gate_raw = sb("gate_raw", [P, 2])
            gate = sb("gate", [P, 2])
            bo_row = sb("bo_row", [P, D])
            tbo = sb("tbo", [P, D])
            shift = sb("shift", [P, 1])
            minus_half = sb("minus_half", [P, 16])
            iota_i = sb("iota_i", [P, 16], I32)
            expert_id = sb("expert_id", [P, NE])
            region0 = sb("region0", [P, NE])
            token_id = sb("token_id", [P, T])
            xr = sb("xr", [P, T, D])
            cr = sb("cr", [SC, DC])
            mask_u8 = sb("mask_u8", [SC, 1], U8)
            mask_bias = sb("mask_bias", [SC, 1])
            stats = sb("stats", [P, NT, 6])
            mv = sb("mv", [P, NT, 2])
            var_in = sb("var_in", [P, NT])
            rstd = sb("rstd", [P, NT])
            xn = sb("xn", [P, T, D])
            cn = sb("cn", [SC, 2 * P])
            xb = sb("xb", [P, T, D])
            lnf = sb("lnf", [P, 2, HALF])
            ln_hi = sb("ln_hi", [P, EC, S], F32R)
            ln_lo = sb("ln_lo", [P, EC, S], F32R)
            lc_hi = sb("lc_hi", [P, 2, P], F32R)
            lc_lo = sb("lc_lo", [P, 2, P], F32R)
            big = sb("big", [P, 2 * T * ROW])
            qk_sb = sb("qk_sb", [P, 3, QK])
            sq = sb("sq", [P, 2, QK])
            ss = sb("ss", [P, 2, 8])
            ssm = sb("ssm", [P, 2, 8])
            rr = sb("rr", [P, 2, 8])
            qkd = sb("qkd", [P, 2, 2 * QK])
            Q1 = sb("Q1", [P, H, S], F32R)
            K1 = sb("K1", [P, H, S + P], F32R)
            K2 = sb("K2", [DH, H, S + P], F32R)
            Vt = sb("Vt", [P, KT, H * P])
            st2 = sb("st2", [P, T, 6])
            mv2 = sb("mv2", [P, T, 2])
            var2 = sb("var2", [P, T])
            rstd2 = sb("rstd2", [P, T])
            lg = sb("lg", [P, T, NE])
            lmax = sb("lmax", [P, T])
            lz = sb("lz", [P, T, NE])
            pe_ = sb("pe_", [P, T, NE])
            psum_ = sb("psum_", [P, T])
            prob = sb("prob", [P, T, NE])
            top = sb("top", [P, 2, T])
            eq = sb("eq", [P, T, NE])
            cand = sb("cand", [P, T, NE])
            pick = sb("pick", [P, 2, T])
            hot = sb("hot", [P, 2, T, NE])
            prob2 = sb("prob2", [P, T, NE])
            chosen = sb("chosen", [P, T * NE], BF16)
            base = sb("base", [P, T + 1, NE])
            slot = sb("slot", [P, T, NE])
            slot_hot = sb("slot_hot", [P, 2, T, NE])
            slot_f = sb("slot_f", [P, 2, T])
            slot_i = sb("slot_i", [P, 2, T], I32)
            tiles_i = sb("tiles_i", [P, NE], I32)
            tiles = sb("tiles", [P, NE])
            ends = sb("ends", [P, NE])
            jump = sb("jump", [P, NE])
            tile_i = sb("tile_i", [P, NTILES], I32)
            tile_id = sb("tile_id", [P, NTILES])
            begun = sb("begun", [P, NTILES, NE])
            jumped = sb("jumped", [P, NTILES, NE])
            row_f = sb("row_f", [P, NTILES])
            expert_f = sb("expert_f", [P, NTILES])
            last_f = sb("last_f", [P, NTILES])

            att_hi, att_lo = ln_hi, ln_lo
            pr = [w1_raw[:, 0, :], w1_raw[:, 1, :], sq[:].rearrange("p t d -> p (t d)")]
            den = lnf[:].rearrange("p t d -> p (t d)")
            attf = qkd
            yT = w2_raw[:].rearrange("p c d -> p (c d)").rearrange("p (c s) -> p c s", c=EC)
            wst_q = big[:, 0:512].rearrange("p (b e) -> p b e", b=2)
            wst_l = big[:, 512:1536].rearrange("p (b e) -> p b e", b=4)
            wst_o = big[:, 1536:2048].rearrange("p (b e) -> p b e", b=2)
            wst_c = big[:, 2048:2048 + 4 * 2 * P].rearrange("p (b e) -> p b e", b=4)
            rows = [big[:, k * T * ROW:(k + 1) * T * ROW].rearrange("p (t r) -> p t r", t=T) for k in range(2)]

            psS = [ctx.enter_context(nc.psum_tensor(f"psS{i}", [P, S], F32)) for i in range(2)]
            psO = [ctx.enter_context(nc.psum_tensor(f"psO{i}", [P, S], F32)) for i in range(2)]

            consts_loaded = sem("consts_loaded")
            weights_loaded = sem("weights_loaded")
            ident_ready = sem("ident_ready")
            iota_done = sem("iota_done")
            pool_const = sem("pool_const")
            dve_const = sem("dve_const")
            gate_ready = sem("gate_ready")
            wT_done = sem("wT_done")
            w_hi_ready = sem("w_hi_ready")
            w_ready = sem("w_ready")
            seq_loaded = sem("seq_loaded")
            stat_ready = sem("stat_ready")
            mv_ready = sem("mv_ready")
            var_ready = sem("var_ready")
            rstd_ready = sem("rstd_ready")
            xn_ready = sem("xn_ready")
            xb_ready = sem("xb_ready")
            mask_cut = sem("mask_cut")
            mask_ready = sem("mask_ready")
            xT_done = sem("xT_done")
            lnf_ready = sem("lnf_ready")
            ln_hi_ready = sem("ln_hi_ready")
            ln_ready = sem("ln_ready")
            proj_done = sem("proj_done")
            proj_read = sem("proj_read")
            ss_ready = sem("ss_ready")
            ssm_ready = sem("ssm_ready")
            rr_ready = sem("rr_ready")
            qkd_ready = sem("qkd_ready")
            qkT_done = sem("qkT_done")
            qk_hi_ready = sem("qk_hi_ready")
            qk_ready = sem("qk_ready")
            s_done = sem("s_done")
            exp_done = sem("exp_done")
            av_done = sem("av_done")
            den_ready = sem("den_ready")
            o_read = sem("o_read")
            att_hi_ready = sem("att_hi_ready")
            att_ready = sem("att_ready")
            o_done = sem("o_done")
            x2_ready = sem("x2_ready")
            x2_stored = sem("x2_stored")
            st2_ready = sem("st2_ready")
            mv2_ready = sem("mv2_ready")
            var2_ready = sem("var2_ready")
            rstd2_ready = sem("rstd2_ready")
            y_ready = sem("y_ready")
            y2_ready = sem("y2_ready")
            yT_done = sem("yT_done")
            yT_ready = sem("yT_ready")
            logits_done = sem("logits_done")
            route = sem("route")
            ez_ready = sem("ez_ready")
            chosen_ready = sem("chosen_ready")
            rank_done = sem("rank_done")
            base_ready = sem("base_ready")
            plan_ready = sem("plan_ready")
            slots_ready = sem("slots_ready")
            scattered = sem("scattered")
            dump_zeroed = sem("dump_zeroed")
            zero_ready = sem("zero_ready")
            raw_loaded = sem("raw_loaded")
            passed = sem("passed")

            NCONST = 16
            NPOOL = 16
            ROUTE = 21
            block = ctx.enter_context(nc.Block())

            def load_sequence(sp, b):
                sp.dma_start(xr[:], x[bass.ds(b, 1)].rearrange("a (t p) d -> p (a t) d", p=P)).then_inc(seq_loaded, 16)
                sp.dma_start(cr[:], ctx_768[bass.ds(b, 1)].rearrange("a s d -> (a s) d")).then_inc(seq_loaded, 16)
                sp.dma_start(mask_u8[:], mask[bass.ds(b, 1)].rearrange("a s -> s a")).then_inc(seq_loaded, 16)

            def store_tokens(sp, b):
                sp.wait_ge(x2_ready, b * T + T)
                sp.dma_start(total[bass.ds(b * S, S)].rearrange("(t p) d -> p t d", p=P), xb[:]).then_inc(x2_stored, 16)

            def value_slots(t, p):
                return Vt[0:p, t, :].rearrange("p (i s d) -> p i s d", i=2, s=4)[:, :, 0:4:3, :]

            def norm_group(g):
                if g >= LATENT_GROUPS:
                    c = g - LATENT_GROUPS
                    return lnf[:, g % 2, 0:SC], lc_hi[:, c, 0:SC], lc_lo[:, c, 0:SC]
                hb, c = divmod(g, EC)
                cols = slice(hb * HALF, (hb + 1) * HALF)
                return lnf[:, g % 2, :], ln_hi[:, c, cols], ln_lo[:, c, cols]

            def weight_groups():
                f = lambda o, n: o[:, n * HALF:(n + 1) * HALF]
                two = lambda a: a.rearrange("p (c n) -> p c n", c=2)
                yield f(psS[0], 0), w_hi[:, 0, 0:QK], w_lo[:, 0, 0:QK]
                yield f(psS[0], 1), w_hi[:, 1, 0:QK], w_lo[:, 1, 0:QK]
                yield two(f(psS[1], 0)), w_hi[:, :, QK:768], w_lo[:, :, QK:768]
                yield two(f(psS[1], 1)), wo_hi[:], wo_lo[:]
                yield f(psO[0], 0), wc_hi[:, 0, :], wc_lo[:, 0, :]
                yield f(psO[0], 1), wc_hi[:, 1, :], wc_lo[:, 1, :]

            def norm_psum(g):
                if g >= LATENT_GROUPS:
                    return psO[1][:, (g - LATENT_GROUPS) * HALF:(g - LATENT_GROUPS) * HALF + SC]
                hb, c = divmod(g, EC)
                return psS[hb][:, c * HALF:(c + 1) * HALF]

            def out_psum(t):
                n = t % OUT_SLOTS
                return psO[n // 2][:, (n % 2) * HALF:(n % 2) * HALF + D]

            @block.sync
            def _(sp):
                sp.dma_start(wst_q, Wq.rearrange("(b p) e -> p b e", p=P)).then_inc(weights_loaded, 16)
                sp.dma_start(wst_l, Wlkv.rearrange("(b p) e -> p b e", p=P)).then_inc(weights_loaded, 16)
                sp.dma_start(wst_c[:, :, 0:DC], Wkv.rearrange("(b p) e -> p b e", p=P)).then_inc(weights_loaded, 16)
                sp.dma_start(wst_o, Wo.rearrange("(b p) e -> p b e", p=P)).then_inc(weights_loaded, 16)
                load_sequence(sp, 0)
                sp.wait_ge(pool_const, NPOOL)
                column = lambda v: v.rearrange("(d a) -> d a", a=1)
                wide = lambda v: v.rearrange("(a d) -> a d", a=1)
                for dst, src in (
                    (gl[:], ln_l_g.rearrange("(c p) -> p c", p=P)), (bl[:], ln_l_b.rearrange("(c p) -> p c", p=P)),
                    (gx[:, 0:1], column(ln_x_g[0:P])), (bx[:, 0:1], column(ln_x_b[0:P])),
                    (gx[0:DC - P, 1:2], column(ln_x_g[P:DC])), (bx[0:DC - P, 1:2], column(ln_x_b[P:DC])),
                    (qg[0:DH, :], column(qn_g)), (qg[DH:P, :], column(qn_g)),
                    (kg[0:DH, :], column(kn_g)), (kg[DH:P, :], column(kn_g)),
                    (qg_row[:], wide(qn_g).to_broadcast([P, DH])), (kg_row[:], wide(kn_g).to_broadcast([P, DH])),
                    (gate_raw[:, 0:1], wide(g_xattn).to_broadcast([P, 1])),
                    (gate_raw[:, 1:2], wide(g_ffn).to_broadcast([P, 1])),
                    (bo_row[:], wide(bo).to_broadcast([P, D])),
                    (router[:], w_router.rearrange("(c p) e -> p c e", p=P)),
                ):
                    sp.dma_start(dst, src).then_inc(consts_loaded, 16)
                sp.dma_start(b1_raw[:], b1[0].rearrange("(c p) -> p c", p=P)).then_inc(raw_loaded, 16)
                sp.dma_start(b2_raw[:], b2[0:1].to_broadcast([P, D])).then_inc(raw_loaded, 16)
                sp.wait_ge(zero_ready, 1)
                sp.dma_start(total[NTOK:NTOK + TM].rearrange("(t p) d -> p t d", p=P),
                             pad_rows[:, :, 0:D]).then_inc(dump_zeroed, 16)
                with sp.Fori(0, B - 1) as b:
                    sp.wait_ge(xn_ready, b * 3 + 3)
                    sp.sem_inc(passed, 1)
                    sp.wait_ge(xb_ready, b + 1)
                    sp.wait_ge(mask_ready, b + 1)
                    load_sequence(sp, b + 1)
                    store_tokens(sp, b)
                sp.wait_ge(av_done, B * NI)
                sp.dma_start(w1_raw[:], w1[0].rearrange("(c p) h -> p c h", p=P)).then_inc(raw_loaded, 16)
                store_tokens(sp, B - 1)
                sp.wait_ge(logits_done, B)
                sp.dma_start(w2_raw[:], w2[0].rearrange("(c p) d -> p c d", p=P)).then_inc(raw_loaded, 16)
                sp.wait_ge(x2_stored, 16 * B)
                sp.wait_ge(dump_zeroed, 16)
                sp.wait_ge(raw_loaded, 64)

            @block.gpsimd
            def _(pool):
                pool.memset(ident[:], 0.0).then_inc(pool_const, 1)
                pool.memset(tri[:], 1.0).then_inc(pool_const, 1)
                pool.memset(ones[:], 1.0).then_inc(pool_const, 1)
                pool.memset(minus_half[:], -0.5).then_inc(pool_const, 1)
                pool.memset(pad_rows[:], 0.0).then_inc(pool_const, 1)
                pool.memset(var_in[:], 1.0).then_inc(pool_const, 1)
                pool.memset(base[:], 0.0).then_inc(pool_const, 1)
                for pad in (gx[:], bx[:], cn[:, DC:2 * P], wst_c[:, :, DC:2 * P], lc_hi[:, :, SC:P], lc_lo[:, :, SC:P],
                            K1[:, :, S + SC:S + P], K2[:, :, S + SC:S + P]):
                    pool.memset(pad if pad.dtype == F32 else pad.bitcast(F32), 0.0).then_inc(pool_const, 1)
                pool.memset(Vt[:], 1.0).then_inc(pool_const, 1)
                pool.wait_ge(pool_const, NPOOL)
                pool.affine_select(out=ident[:], in_=ident[:], compare_op=ALU.not_equal, fill=1.0, base=0,
                                   pattern=[[-1, P]], channel_multiplier=1).then_inc(ident_ready, 1)
                pool.affine_select(out=tri[:], in_=tri[:], compare_op=ALU.is_gt, fill=0.0, base=0,
                                   pattern=[[1, P]], channel_multiplier=-1).then_inc(ident_ready, 1)
                pool.iota(iota_i[:, 0:8], [[1, 8]], base=0, channel_multiplier=0).then_inc(iota_done, 1)
                pool.iota(iota_i[:, 8:16], [[P, 8]], base=0, channel_multiplier=1).then_inc(iota_done, 1)
                pool.iota(tile_i[:], [[1, NTILES]], base=0, channel_multiplier=0).then_inc(iota_done, 1)
                pool.engine_nop().then_inc(zero_ready, 1)

                def norm_root(b):
                    pool.wait_ge(var_ready, b + 1)
                    pool.tensor_tensor(rstd[:], var_in[:], minus_half[:, 0:NT], ALU.pow).then_inc(rstd_ready, 1)

                def head_roots(b):
                    for t in range(NT):
                        n = 8 if t < T else H
                        p = P if t < T else SC
                        pool.wait_ge(ssm_ready, b * NT + (t + 1))
                        pool.tensor_tensor(rr[0:p, t % 2, 0:n], ssm[0:p, t % 2, 0:n], minus_half[0:p, 0:n],
                                           ALU.pow).then_inc(rr_ready, 1)

                def residual(b):
                    pool.tensor_tensor(xb[:], xr[:], tbo[:].unsqueeze(1).to_broadcast([P, T, D]),
                                       ALU.add).then_inc(xb_ready, 1)

                def scatter(b):
                    pool.wait_ge(slots_ready, b + 1)
                    pool.wait_ge(y2_ready, b + 1)
                    pool.sem_inc(passed, 1)
                    for t in range(T):
                        for k in range(2):
                            pool.indirect_dma_start(routed, bass.IndirectOffsetOnAxis(ap=slot_i[:, k, t:t + 1], axis=0),
                                                    rows[k][:, t, :], None,
                                                    bounds_check=NE * REGION - 1).then_inc(scattered, 16)

                def second_root(b):
                    pool.wait_ge(var2_ready, b + 1)
                    pool.tensor_tensor(rstd2[:], var2[:], minus_half[:, 0:T], ALU.pow).then_inc(rstd2_ready, 1)

                norm_root(0)
                head_roots(0)
                pool.wait_ge(dve_const, 6)
                pool.wait_ge(seq_loaded, 48)
                residual(0)
                norm_root(1)
                with pool.Fori(1, B) as b:
                    second_root(b - 1)
                    head_roots(b)
                    pool.wait_ge(x2_stored, b * 16)
                    pool.wait_ge(y_ready, b * T)
                    pool.sem_inc(passed, 1)
                    residual(b)
                    scatter(b - 1)
                    with pool.If(b < B - 1):
                        norm_root(b + 1)
                    pool.wait_ge(scattered, b * (32 * T))
                    pool.sem_inc(passed, 1)
                second_root(B - 1)
                scatter(B - 1)
                pool.wait_ge(scattered, B * (32 * T))

            @block.scalar
            def _(act):
                act.wait_ge(consts_loaded, 16 * NCONST)
                act.activation(gate[:], gate_raw[:], ACT.Tanh).then_inc(gate_ready, 1)
                for g, (src, dst, _) in enumerate(weight_groups()):
                    act.wait_ge(wT_done, g + 1)
                    act.activation(dst, src, ACT.Copy).then_inc(w_hi_ready, 1)

                act.wait_ge(dve_const, 6)

                def front(b, with_router):
                    for g in range(GROUPS):
                        act.wait_ge(lnf_ready, b * GROUPS + (g + 1))
                        src, hi, _ = norm_group(g)
                        act.activation(hi, src, ACT.Copy).then_inc(ln_hi_ready, 1)

                    def read_projection(t):
                        act.wait_ge(proj_done, b * NT + (t + 1))
                        if t >= 3:
                            act.wait_ge(qkd_ready, b * NT + (t - 2))
                        if t >= 2:
                            act.wait_ge(ss_ready, b * NT + (t - 1))
                        o = psO[t % 2]
                        if t < T:
                            act.activation(qk_sb[:, t % 3, :], o[:, 0:QK], ACT.Copy)
                            act.activation(sq[:, t % 2, :], o[:, 0:QK], ACT.Square)
                            act.activation(value_slots(t, P), o[:, QK:QK + H * DH].rearrange(
                                "p (i s d) -> p i s d", i=2, s=2), ACT.Copy).then_inc(proj_read, 1)
                        else:
                            act.activation(qk_sb[0:SC, t % 3, 0:H * DH], o[0:SC, 0:H * DH], ACT.Copy)
                            act.activation(sq[0:SC, t % 2, 0:H * DH], o[0:SC, 0:H * DH], ACT.Square)
                            act.activation(value_slots(t, SC), o[0:SC, H * DH:2 * H * DH].rearrange(
                                "p (i s d) -> p i s d", i=2, s=2), ACT.Copy).then_inc(proj_read, 1)

                    def heads_hi(t):
                        act.wait_ge(qkT_done, b * NT + (t + 1))
                        ps = psS[t % 2]
                        if t < T:
                            act.activation(Q1[:, :, t * P:(t + 1) * P], ps[:, 0:512].rearrange("p (h n) -> p h n", h=H),
                                           ACT.Copy, scale=gqk[:, 0:1])
                            act.activation(K1[:, :, t * P:(t + 1) * P], ps[:, 512:1024].rearrange("p (h n) -> p h n", h=H),
                                           ACT.Copy).then_inc(qk_hi_ready, 1)
                        else:
                            act.activation(K1[:, :, S:S + SC], ps[:, 512:512 + H * SC].rearrange("p (h n) -> p h n", h=H),
                                           ACT.Copy).then_inc(qk_hi_ready, 1)

                    for t in range(NT + 2):
                        if t < NT:
                            read_projection(t)
                        if t >= 2:
                            heads_hi(t - 2)
                    if with_router:
                        turned_rows(b - 1)

                def turned_rows(b):
                    for hb in range(2):
                        act.wait_ge(yT_done, b * 2 + (hb + 1))
                        act.activation(yT[:, :, hb * HALF:(hb + 1) * HALF],
                                       psO[1 - hb][:].rearrange("p (c n) -> p c n", c=EC), ACT.Copy).then_inc(yT_ready, 1)

                def router_exp(b):
                    act.wait_ge(route, b * ROUTE + 3)
                    act.activation(pe_[:], lz[:], ACT.Exp).then_inc(ez_ready, 1)

                def second_rows(b):
                    act.wait_ge(y_ready, b * T + T)
                    act.activation(rows[1][:, :, 0:D], rows[0][:, :, 0:D], ACT.Copy).then_inc(y2_ready, 1)

                def attention(b, with_router):
                    def attention_hi(c):
                        for n in range(2):
                            act.wait_ge(o_read, b * 2 * H + (4 * c + 3 + n))
                            cols = slice(n * HALF, (n + 1) * HALF)
                            act.activation(att_hi[:, c, cols], attf[:, c, cols], ACT.Copy).then_inc(att_hi_ready, 1)

                    act.wait_ge(mask_ready, b + 1)
                    for i in range(NI):
                        h, kt = divmod(i, KT)
                        p = P if kt < T else SC
                        bias = shift[:, 0:1] if kt < T else mask_bias[:, 0:1]
                        act.wait_ge(s_done, b * NI + (i + 1))
                        if i >= NP_RING:
                            act.wait_ge(av_done, b * NI + (i - NP_RING + 1))
                        act.activation(pr[i % NP_RING][0:p, :], psS[i % 2][0:p, :], ACT.Exp, bias=bias).then_inc(exp_done, 1)
                        if with_router and i == 3:
                            router_exp(b - 1)
                        if with_router and i == 5:
                            second_rows(b - 1)
                        if kt == 4 and h == 2:
                            attention_hi(0)
                    attention_hi(1)

                front(0, False)
                attention(0, False)
                with act.Fori(1, B) as b:
                    front(b, True)
                    attention(b, True)
                turned_rows(B - 1)
                router_exp(B - 1)
                second_rows(B - 1)

            @block.vector
            def _(dve):
                dve.wait_ge(iota_done, 3)
                dve.tensor_copy(expert_id[:], iota_i[:, 0:8])
                dve.tensor_copy(token_id[:], iota_i[:, 8:16])
                dve.tensor_copy(tile_id[:], tile_i[:])
                dve.tensor_scalar(region0[:], iota_i[:, 0:8], float(REGION), None, ALU.mult).then_inc(dve_const, 1)
                dve.wait_ge(zero_ready, 1)
                dve.wait_ge(dump_zeroed, 16)
                dve.tensor_scalar(pad_rows[:, :, D:D + 1].rearrange("p m a -> p (m a)"), iota_i[:, 8:8 + MH],
                                  float(NTOK), None, ALU.add).then_inc(dve_const, 1)
                dve.wait_ge(consts_loaded, 16 * NCONST)
                dve.tensor_tensor(qg_row[:], qg_row[:], kg_row[:], ALU.mult).then_inc(dve_const, 1)
                dve.scalar_tensor_tensor(out=gqk[:], in0=qg[:], scalar=SCALE, in1=kg[:], op0=ALU.mult,
                                         op1=ALU.mult).then_inc(dve_const, 1)
                dve.wait_ge(dve_const, 3)
                dve.tensor_reduce(shift[:], qg_row[:], AX, ALU.max, apply_absolute_value=True).then_inc(dve_const, 1)
                dve.wait_ge(gate_ready, 1)
                dve.tensor_scalar(tbo[:], bo_row[:], gate[:, 0:1], None, ALU.mult).then_inc(dve_const, 1)
                dve.wait_ge(dve_const, 5)
                dve.tensor_scalar(shift[:], shift[:], -SCALE * DH, SAFE, ALU.mult, ALU.add).then_inc(dve_const, 1)
                dve.wait_ge(dve_const, 7)
                dve.tensor_scalar(shift[:], shift[:], 0.0, None, ALU.min).then_inc(dve_const, 1)
                dve.wait_ge(dve_const, 8)
                for g, (src, hi, lo) in enumerate(weight_groups()):
                    dve.wait_ge(w_hi_ready, g + 1)
                    dve.tensor_tensor(lo, src, hi.bitcast(F32), ALU.subtract).then_inc(w_ready, 1)

                dve.wait_ge(pool_const, NPOOL)

                def norm(b):
                    dve.wait_ge(seq_loaded, b * 48 + 48)
                    dve.bn_stats(stats[0:SC, T, :], cr[:])
                    for t in range(T):
                        dve.bn_stats(stats[:, t, :], xr[:, t, :]).then_inc(stat_ready, 1)
                    dve.wait_ge(stat_ready, b * T + T)
                    dve.sem_inc(passed, 1)
                    for t in range(T):
                        dve.bn_aggr(mv[:, t, :], stats[:, t, :])
                    dve.bn_aggr(mv[0:SC, T, :], stats[0:SC, T, :]).then_inc(mv_ready, 1)
                    dve.wait_ge(mv_ready, b + 1)
                    dve.tensor_scalar(var_in[:, 0:T], mv[:, 0:T, 1], 1.0 + EPS, EPS * EPS, ALU.mult, ALU.add)
                    dve.tensor_scalar(var_in[0:SC, T:NT], mv[0:SC, T, 1:2], EPS, None, ALU.add).then_inc(var_ready, 1)
                    dve.wait_ge(rstd_ready, b + 1)
                    dve.tensor_scalar(cn[:, 0:DC], cr[:], mv[0:SC, T, 0:1], rstd[0:SC, T:NT], ALU.subtract,
                                      ALU.mult).then_inc(xn_ready, 1)
                    for t in range(T):
                        ins = dve.tensor_scalar(xn[:, t, :], xr[:, t, :], mv[:, t, 0:1], rstd[:, t:t + 1], ALU.subtract, ALU.mult)
                        if t % HT == HT - 1:
                            ins.then_inc(xn_ready, 1)

                def affine(b, first=False):
                    if not first:
                        dve.wait_ge(exp_done, b * NI)
                        dve.sem_inc(passed, 1)
                    dve.tensor_scalar(mask_bias[:], mask_u8[:], 3e38, -3e38, ALU.mult, ALU.add).then_inc(mask_cut, 1)
                    dve.wait_ge(mask_cut, b + 1)
                    dve.tensor_tensor(mask_bias[:], mask_bias[:], shift[0:SC, :], ALU.min).then_inc(mask_ready, 1)
                    def norm_affine(g):
                        dve.wait_ge(xT_done, b * GROUPS + (g + 1))
                        if g >= 2:
                            dve.wait_ge(ln_hi_ready, b * GROUPS + (g - 1))
                            dve.wait_ge(ln_ready, b * GROUPS + (g - 1))
                        ga, be = (gl, bl) if g < LATENT_GROUPS else (gx, bx)
                        c = g % EC if g < LATENT_GROUPS else g - LATENT_GROUPS
                        dst, _, _ = norm_group(g)
                        dve.tensor_scalar(dst, norm_psum(g), ga[:, c:c + 1], be[:, c:c + 1], ALU.mult,
                                          ALU.add).then_inc(lnf_ready, 1)

                    def norm_lo(g):
                        dve.wait_ge(ln_hi_ready, b * GROUPS + (g + 1))
                        src, hi, lo = norm_group(g)
                        dve.tensor_tensor(lo, src, hi.bitcast(F32), ALU.subtract).then_inc(ln_ready, 1)

                    for g in range(GROUPS + 1):
                        if g < GROUPS:
                            norm_affine(g)
                        if g >= 1:
                            norm_lo(g - 1)

                def front(b, rows_of_last):
                    def mean_squares(t):
                        p, n = (P, 8) if t < T else (SC, H)
                        dve.wait_ge(proj_read, b * NT + (t + 1))
                        if t >= 2:
                            dve.wait_ge(rr_ready, b * NT + (t - 1))
                        dve.tensor_reduce(ss[0:p, t % 2, 0:n], sq[0:p, t % 2, 0:n * DH].rearrange("p (h d) -> p h d", d=DH),
                                          AX, ALU.add).then_inc(ss_ready, 1)
                        dve.wait_ge(ss_ready, b * NT + (t + 1))
                        dve.tensor_scalar(ssm[0:p, t % 2, 0:n], ss[0:p, t % 2, 0:n], 1.0 / DH, RMS_EPS * RMS_EPS, ALU.mult,
                                          ALU.max).then_inc(ssm_ready, 1)

                    def scale_heads(t):
                        p, n = (P, 8) if t < T else (SC, H)
                        dve.wait_ge(rr_ready, b * NT + (t + 1))
                        if t >= 2:
                            dve.wait_ge(qkT_done, b * NT + (t - 1))
                        for k in range(2):
                            ins = dve.tensor_tensor(
                                qkd[0:p, t % 2, 0:n * P].rearrange("p (h k d) -> p h k d", k=2, d=DH)[:, :, k, :],
                                qk_sb[0:p, t % 3, 0:n * DH].rearrange("p (h d) -> p h d", d=DH),
                                rr[0:p, t % 2, 0:n].unsqueeze(2).to_broadcast([p, n, DH]), ALU.mult)
                        ins.then_inc(qkd_ready, 1)

                    def heads_lo(t):
                        dve.wait_ge(qk_hi_ready, b * NT + (t + 1))
                        ps = psS[t % 2]
                        if t < T:
                            cols = slice(t * P, (t + 1) * P)
                            q_lo = Q1[DH:P, :, cols]
                            dve.scalar_tensor_tensor(out=q_lo, in0=ps[DH:P, 0:512].rearrange("p (h n) -> p h n", h=H),
                                                     scalar=gqk[DH:P, 0:1], in1=q_lo.bitcast(F32), op0=ALU.mult,
                                                     op1=ALU.subtract)
                            dve.tensor_tensor(K2[:, :, cols], ps[0:DH, 512:1024].rearrange("p (h n) -> p h n", h=H),
                                              K1[0:DH, :, cols].bitcast(F32), ALU.subtract).then_inc(qk_ready, 1)
                        else:
                            dve.tensor_tensor(K2[:, :, S:S + SC], ps[0:DH, 512:512 + H * SC].rearrange("p (h n) -> p h n", h=H),
                                              K1[0:DH, :, S:S + SC].bitcast(F32), ALU.subtract).then_inc(qk_ready, 1)

                    for t in range(NT + 2):
                        if t < NT:
                            mean_squares(t)
                        if 1 <= t <= NT:
                            scale_heads(t - 1)
                        if rows_of_last and 1 <= t <= T:
                            normed_row(b - 1, t - 1)
                        if t >= 2:
                            heads_lo(t - 2)

                def attention(b, following):
                    def denominators(h, n):
                        d0 = DH if h % 2 == 0 else 0
                        cols = slice(n * HALF, (n + 1) * HALF)
                        dve.reciprocal(den[DH - d0:P - d0, cols], psO[h % 2][d0:d0 + DH, cols]).then_inc(den_ready, 1)

                    def quotients(h, n):
                        v0 = 0 if h % 2 == 0 else DH
                        cols = slice(n * HALF, (n + 1) * HALF)
                        dve.wait_ge(den_ready, b * 2 * H + (2 * h + n + 1))
                        dve.tensor_tensor(attf[v0:v0 + DH, h // 2, cols], psO[h % 2][v0:v0 + DH, cols], den[v0:v0 + DH, cols],
                                          ALU.mult).then_inc(o_read, 1)

                    def attention_lo(c, n):
                        cols = slice(n * HALF, (n + 1) * HALF)
                        dve.wait_ge(att_hi_ready, b * 2 * EC + (2 * c + n + 1))
                        dve.tensor_tensor(att_lo[:, c, cols], attf[:, c, cols], att_hi[:, c, cols].bitcast(F32),
                                          ALU.subtract).then_inc(att_ready, 1)

                    for h in range(H):
                        dve.wait_ge(av_done, b * NI + KT * (h + 1))
                        denominators(h, 0)
                        quotients(h, 0)
                        denominators(h, 1)
                        if h % 2 == 1:
                            attention_lo(h // 2, 0)
                        quotients(h, 1)
                        if h % 2 == 1:
                            attention_lo(h // 2, 1)
                        if h == 1:
                            following()

                def residuals(b):
                    dve.wait_ge(xb_ready, b + 1)
                    for t in range(T):
                        dve.wait_ge(o_done, b * T + (t + 1))
                        dve.scalar_tensor_tensor(out=xb[:, t, :], in0=out_psum(t), scalar=gate[:, 0:1], in1=xb[:, t, :],
                                                 op0=ALU.mult, op1=ALU.add).then_inc(x2_ready, 1)

                def second_stats(b):
                    dve.wait_ge(x2_ready, b * T + T)
                    dve.sem_inc(passed, 1)
                    for t in range(T):
                        dve.bn_stats(st2[:, t, :], xb[:, t, :]).then_inc(st2_ready, 1)
                    dve.wait_ge(st2_ready, b * T + T)
                    dve.sem_inc(passed, 1)
                    for t in range(T):
                        ins = dve.bn_aggr(mv2[:, t, :], st2[:, t, :])
                    ins.then_inc(mv2_ready, 1)
                    dve.wait_ge(mv2_ready, b + 1)
                    dve.tensor_scalar(var2[:], mv2[:, :, 1], EPS, None, ALU.add).then_inc(var2_ready, 1)

                def normed_row(b, t):
                    if t == 0:
                        dve.wait_ge(rstd2_ready, b + 1)
                    dve.tensor_scalar(rows[0][:, t, 0:D], xb[:, t, :], mv2[:, t, 0:1], rstd2[:, t:t + 1], ALU.subtract,
                                      ALU.mult).then_inc(y_ready, 1)

                def router_steps(b):
                    step = [0]

                    def then_step(ins):
                        step[0] += 1
                        ins.then_inc(route, 1)
                        dve.wait_ge(route, b * ROUTE + step[0])

                    wide = lambda a: a.unsqueeze(2).to_broadcast([P, T, NE])
                    experts = expert_id[:].unsqueeze(1).to_broadcast([P, T, NE])
                    dve.wait_ge(logits_done, b + 1)
                    then_step(dve.tensor_copy(lg[:], psO[1][:, 0:T * NE].rearrange("p (t e) -> p t e", t=T)))
                    then_step(dve.tensor_reduce(lmax[:], lg[:], AX, ALU.max))
                    then_step(dve.tensor_tensor(lz[:], lg[:], wide(lmax[:]), ALU.subtract))
                    dve.wait_ge(ez_ready, b + 1)
                    then_step(dve.tensor_reduce(psum_[:], pe_[:], AX, ALU.add))
                    then_step(dve.reciprocal(psum_[:], psum_[:]))
                    then_step(dve.tensor_tensor(prob[:], pe_[:], wide(psum_[:]), ALU.mult))
                    p_now = prob
                    for k in range(2):
                        then_step(dve.tensor_reduce(top[:, k, :], p_now[:], AX, ALU.max))
                        then_step(dve.tensor_tensor(eq[:], p_now[:], wide(top[:, k, :]), ALU.is_equal))
                        then_step(dve.scalar_tensor_tensor(out=cand[:], in0=eq[:], scalar=-float(NE), in1=experts, op0=ALU.mult,
                                                           op1=ALU.add))
                        then_step(dve.tensor_reduce(pick[:, k, :], cand[:], AX, ALU.min))
                        then_step(dve.tensor_tensor(hot[:, k], cand[:], wide(pick[:, k, :]), ALU.is_equal))
                        if k == 0:
                            then_step(dve.scalar_tensor_tensor(out=prob2[:], in0=hot[:, 0], scalar=-2.0, in1=prob[:], op0=ALU.mult,
                                                               op1=ALU.add))
                            p_now = prob2
                    dve.tensor_tensor(chosen[:].rearrange("p (t e) -> p t e", t=T), hot[:, 0], hot[:, 1],
                                      ALU.add).then_inc(chosen_ready, 1)
                    for k in range(2):
                        dve.tensor_scalar(rows[k][:, :, D:D + 1].rearrange("p t a -> p (t a)"), token_id[:], 0.0, None, ALU.add)
                        ins = dve.tensor_scalar(rows[k][:, :, D + 1:D + 2].rearrange("p t a -> p (t a)"), top[:, k, :], gate[:, 1:2],
                                                None, ALU.mult)
                    then_step(ins)
                    dve.tensor_scalar(token_id[:], token_id[:], float(S), None, ALU.add)
                    dve.wait_ge(rank_done, b + 1)
                    for t in range(T):
                        dve.tensor_tensor(base[:, t + 1, :], base[:, t, :], psO[1][:, HALF + t * NE:HALF + (t + 1) * NE],
                                          ALU.add).then_inc(base_ready, 1)
                        dve.wait_ge(base_ready, b * (T + 2) + (t + 1))
                    then_step(dve.tensor_tensor(slot[:], psO[1][:, 0:T * NE].rearrange("p (t e) -> p t e", t=T), base[:, 0:T, :], ALU.add))
                    then_step(dve.tensor_tensor(slot[:], slot[:], region0[:].unsqueeze(1).to_broadcast([P, T, NE]), ALU.add))
                    then_step(dve.tensor_tensor(slot_hot[:], hot[:], slot[:].unsqueeze(1).to_broadcast([P, 2, T, NE]), ALU.mult))
                    dve.tensor_reduce(slot_f[:], slot_hot[:], AX, ALU.add).then_inc(base_ready, 1)
                    dve.wait_ge(base_ready, b * (T + 2) + T + 1)
                    dve.tensor_copy(base[:, 0, :], base[:, T, :]).then_inc(base_ready, 1)
                    dve.tensor_copy(slot_i[:], slot_f[:]).then_inc(slots_ready, 1)
                    assert step[0] == ROUTE, step[0]
                    dve.wait_ge(base_ready, b * (T + 2) + T + 2)
                    dve.sem_inc(passed, 1)

                norm(0)
                affine(0, first=True)
                front(0, False)
                attention(0, lambda: norm(1))
                with dve.Fori(1, B) as b:
                    residuals(b - 1)
                    affine(b)
                    second_stats(b - 1)
                    front(b, True)
                    router_steps(b - 1)

                    def following():
                        with dve.If(b < B - 1):
                            norm(b + 1)

                    attention(b, following)
                residuals(B - 1)
                second_stats(B - 1)
                for t in range(T):
                    normed_row(B - 1, t)
                router_steps(B - 1)

                plan_step = [0]

                def then_plan(ins):
                    plan_step[0] += 1
                    ins.then_inc(plan_ready, 1)
                    dve.wait_ge(plan_ready, plan_step[0])

                wide_t = lambda a: a.unsqueeze(1).to_broadcast([P, NTILES, NE])
                wide_e = lambda a: a.unsqueeze(2).to_broadcast([P, NTILES, NE])
                count = base[:, 0, :]
                dve.tensor_tensor(pad_at[:], count, region0[:], ALU.add)
                then_plan(dve.tensor_scalar(tiles_i[:], count, float(TM - 1), None, ALU.add))
                then_plan(dve.tensor_scalar(tiles_i[:], tiles_i[:], TM.bit_length() - 1, None, ALU.arith_shift_right))
                then_plan(dve.tensor_scalar(tiles[:], tiles_i[:], 1.0, None, ALU.max))
                dve.tensor_scalar(jump[:], tiles[:], -float(TM), float(REGION), ALU.mult, ALU.add)
                then_plan(dve.tensor_copy(ends[:, 0:1], tiles[:, 0:1]))
                for e in range(1, NE):
                    then_plan(dve.tensor_tensor(ends[:, e:e + 1], ends[:, e - 1:e], tiles[:, e:e + 1], ALU.add))
                then_plan(dve.tensor_tensor(begun[:], wide_e(tile_id[:]), wide_t(ends[:]), ALU.is_ge))
                then_plan(dve.tensor_tensor(jumped[:], begun[:], wide_t(jump[:]), ALU.mult))
                then_plan(dve.tensor_reduce(row_f[:], jumped[:], AX, ALU.add))
                then_plan(dve.scalar_tensor_tensor(out=row_f[:], in0=tile_id[:], scalar=float(TM), in1=row_f[:], op0=ALU.mult,
                                                   op1=ALU.add))
                dve.tensor_scalar(tile_row[:], row_f[:], float(NE * REGION), None, ALU.min)
                dve.tensor_reduce(expert_f[:], begun[:, :, 0:NE - 1], AX, ALU.add)
                then_plan(dve.tensor_scalar(tile_id[:], tile_id[:], 1.0, None, ALU.add))
                then_plan(dve.tensor_tensor(begun[:], wide_e(tile_id[:]), wide_t(ends[:]), ALU.is_equal))
                then_plan(dve.tensor_reduce(last_f[:], begun[:, :, 0:NE - 1], AX, ALU.add))
                dve.tensor_copy(tile_expert[:], expert_f[:])
                then_plan(dve.tensor_copy(tile_last[:], last_f[:]))

            @block.tensor
            def _(pe):
                pe.wait_ge(ident_ready, 2)
                pe.wait_ge(pool_const, NPOOL)
                pe.wait_ge(weights_loaded, 64)
                rows_qk = [wst_q[:, 0], wst_q[:, 1], wst_l[:, 0], wst_l[:, 1]]
                rows_v = [wst_l[:, 2], wst_l[:, 3]]
                turned = [(psS[0], c * HALF + j * P, rows_qk[j][:, c * P:(c + 1) * P], c) for c in range(EC) for j in range(4)]
                turned += [(psS[1], c * D + j * P, rows_v[j][:, c * P:(c + 1) * P], 2) for c in range(EC) for j in range(2)]
                turned += [(psS[1], HALF + c * D + j * P, wst_o[:, j, c * P:(c + 1) * P], 3) for c in range(EC) for j in range(2)]
                turned += [(psO[0], c * HALF + j * P, wst_c[:, j, c * P:(c + 1) * P], 4 + c) for c in range(2) for j in range(4)]
                for n, (ps, col, src, g) in enumerate(turned):
                    ins = pe.transpose(ps[:, col:col + P], src, ident[:])
                    if n + 1 == len(turned) or turned[n + 1][3] != g:
                        ins.then_inc(wT_done, 1)
                pe.wait_ge(w_ready, GROUPS_W)

                def passes(o, parts):
                    for n, (l, r) in enumerate(parts):
                        ins = pe.matmul(o, l, r, start=(n == 0), stop=(n == len(parts) - 1))
                    return ins

                def turn_latents(b, first=False):
                    if not first:
                        pe.wait_ge(exp_done, b * NI)
                        pe.sem_inc(passed, 1)
                    for hb in range(2):
                        pe.wait_ge(xn_ready, b * 3 + (hb + 2))
                        for c in range(EC):
                            for t in range(HT):
                                ins = pe.transpose(psS[hb][:, c * HALF + t * P:c * HALF + (t + 1) * P],
                                                   xn[:, hb * HT + t, c * P:(c + 1) * P], ident[:])
                            ins.then_inc(xT_done, 1)

                def front(b, with_router):
                    pe.wait_ge(xn_ready, b * 3 + 1)
                    pe.sem_inc(passed, 1)
                    if with_router:
                        pe.wait_ge(x2_ready, b * T)
                        pe.sem_inc(passed, 1)
                    pe.transpose(psO[1][:, 0:SC], cn[:, 0:P], ident[0:SC, 0:SC]).then_inc(xT_done, 1)
                    pe.transpose(psO[1][:, HALF:HALF + SC], cn[:, P:2 * P], ident[0:SC, 0:SC]).then_inc(xT_done, 1)

                    def project(t):
                        if t in (0, HT, T):
                            pe.wait_ge(ln_ready, b * GROUPS + EC * (t // HT + 1))
                        if t == 1:
                            pe.wait_ge(lnf_ready, b * GROUPS + GROUPS)
                        if t >= 2:
                            pe.wait_ge(proj_read, b * NT + (t - 1))
                        o = psO[t % 2]
                        if t < T:
                            cols = slice(t * P, (t + 1) * P)
                            pairs = lambda f: [p for c in range(EC) for p in (
                                (ln_hi[:, c, cols], w_hi[:, c, f]), (ln_hi[:, c, cols], w_lo[:, c, f]),
                                (ln_lo[:, c, cols], w_hi[:, c, f]))]
                            passes(o[:, 0:QK], pairs(slice(0, QK)))
                            passes(o[:, QK:QK + H * DH], pairs(slice(QK, QK + H * DH))).then_inc(proj_done, 1)
                        else:
                            passes(o[:, 0:2 * H * DH], [p for c in range(2) for p in (
                                (lc_hi[:, c, :], wc_hi[:, c, :]), (lc_hi[:, c, :], wc_lo[:, c, :]),
                                (lc_lo[:, c, :], wc_hi[:, c, :]))]).then_inc(proj_done, 1)

                    def turn_heads(t):
                        if t >= 2:
                            pe.wait_ge(qk_ready, b * NT + (t - 1))
                        pe.wait_ge(qkd_ready, b * NT + (t + 1))
                        if t == T:
                            pe.sem_inc(passed, 1)
                        p, n = (P, 2 * H) if t < T else (SC, H)
                        for j in range(n):
                            col = (j if t < T else H) * P if t < T else HALF + j * SC
                            ins = pe.transpose(psS[t % 2][:, col:col + p], qkd[0:p, t % 2, j * P:(j + 1) * P], ident[0:p, 0:p])
                        ins.then_inc(qkT_done, 1)

                    for t in range(NT + 2):
                        if t < NT:
                            project(t)
                        if t >= 2:
                            turn_heads(t - 2)
                        if with_router and t >= NT:
                            turn_rows(b - 1, t - NT)

                def turn_rows(b, hb):
                    pe.wait_ge(y_ready, b * T + HT * (hb + 1))
                    for c in range(EC):
                        for t in range(HT):
                            ins = pe.transpose(psO[1 - hb][:, c * HALF + t * P:c * HALF + (t + 1) * P],
                                               rows[0][:, hb * HT + t, c * P:(c + 1) * P], ident[:])
                    ins.then_inc(yT_done, 1)

                def logits(b):
                    for t in range(T):
                        if t % HT == 0:
                            pe.wait_ge(yT_ready, b * 2 + (t // HT + 1))
                        ins = passes(psO[1][:, t * NE:(t + 1) * NE], [(yT[:, c, t * P:(t + 1) * P], router[:, c, :]) for c in range(EC)])
                    ins.then_inc(logits_done, 1)

                def ranks(b):
                    pe.wait_ge(chosen_ready, b + 1)
                    pe.matmul(psO[1][:, 0:T * NE], tri[:], chosen[:], start=True, stop=True)
                    pe.matmul(psO[1][:, HALF:HALF + T * NE], ones[:], chosen[:], start=True, stop=True).then_inc(rank_done, 1)

                def attention(b, with_router):
                    def scores(i):
                        h, kt = divmod(i, KT)
                        if i >= 2:
                            pe.wait_ge(exp_done, b * NI + (i - 1))
                        keys = slice(kt * P, (kt + 1) * P)
                        for n in range(2):
                            pe.matmul(psS[i % 2][:, n * HALF:(n + 1) * HALF], K1[:, h, keys], Q1[:, h, n * HALF:(n + 1) * HALF],
                                      start=True, stop=False)
                        for n in range(2):
                            ins = pe.matmul(psS[i % 2][:, n * HALF:(n + 1) * HALF], K2[:, h, keys],
                                            Q1[0:DH, h, n * HALF:(n + 1) * HALF], start=False, stop=True)
                        ins.then_inc(s_done, 1)

                    def values(i):
                        h, kt = divmod(i, KT)
                        pe.wait_ge(exp_done, b * NI + (i + 1))
                        if kt == 0 and h >= 2:
                            pe.wait_ge(o_read, b * 2 * H + 2 * (h - 1))
                        p = P if kt < T else SC
                        for n in range(2):
                            ins = pe.matmul(psO[h % 2][:, n * HALF:(n + 1) * HALF], Vt[0:p, kt, h * P:(h + 1) * P],
                                            pr[i % NP_RING][0:p, n * HALF:(n + 1) * HALF], start=(kt == 0), stop=(kt == KT - 1))
                        ins.then_inc(av_done, 1)

                    pe.wait_ge(qk_ready, b * NT + NT)
                    for i in range(NI + 1):
                        if i < NI:
                            scores(i)
                        if with_router and i == 1:
                            logits(b - 1)
                        if with_router and i == 5:
                            ranks(b - 1)
                        if with_router and i == KT + 1:
                            pe.wait_ge(slots_ready, b)
                            pe.sem_inc(passed, 1)
                        if i >= 1:
                            values(i - 1)

                def project_out(b):
                    for t in range(T):
                        if t in (0, HT):
                            pe.wait_ge(att_ready, b * 2 * EC + (2 * EC - 1 + t // HT))
                        if t >= OUT_SLOTS:
                            pe.wait_ge(x2_ready, b * T + (t - OUT_SLOTS + 1))
                        cols = slice(t * P, (t + 1) * P)
                        passes(out_psum(t), [p for c in range(EC) for p in (
                            (att_hi[:, c, cols], wo_hi[:, c, :]), (att_hi[:, c, cols], wo_lo[:, c, :]),
                            (att_lo[:, c, cols], wo_hi[:, c, :]))]).then_inc(o_done, 1)

                turn_latents(0, first=True)
                front(0, False)
                attention(0, False)
                with pe.Fori(1, B) as b:
                    turn_latents(b)
                    project_out(b - 1)
                    front(b, True)
                    attention(b, True)
                project_out(B - 1)
                for hb in range(2):
                    pe.wait_ge(x2_ready, B * T)
                    turn_rows(B - 1, hb)
                logits(B - 1)
                ranks(B - 1)

        experts_phase(nc, (pad_at, tile_row, tile_expert, tile_last), pad_rows, ident, (w1_raw, w2_raw, b1_raw, b2_raw),
                      w1, b1, w2, b2, routed, total, out)


def experts_phase(nc, plan, pad_rows, ident, raw, w1, b1, w2, b2, routed, total, out):
    NE, D, HID = w1.shape
    EC, HC = D // P, HID // P
    MH, ROW = pad_rows.shape[1:]
    TM = MH * P
    REGION = (routed.shape[0] - TM) // NE
    NTOK = REGION - TM
    NQ = HC // 2
    pad_at, tile_row, tile_expert, tile_last = plan
    w1_raw, w2_raw, b1_raw, b2_raw = raw
    NTILES = tile_row.shape[1]

    with ExitStack() as ctx:
        def sb(name, shape, dt=F32):
            return ctx.enter_context(nc.sbuf_tensor(name, shape, dt))

        def sem(name):
            return ctx.enter_context(nc.semaphore(name))

        w1_hi = sb("w1_hi", [P, EC, HID], F32R)
        w1_lo = sb("w1_lo", [P, EC, HID], F32R)
        w2_hi = sb("w2_hi", [P, HC, D], F32R)
        w2_lo = sb("w2_lo", [P, HC, D], F32R)
        b1_col = sb("b1_col", [P, HC])
        b2_row = sb("b2_row", [P, D])
        xrow = sb("xrow", [P, MH, ROW])
        xT_hi = sb("xT_hi", [P, EC, TM], F32R)
        xT_lo = sb("xT_lo", [P, EC, TM], F32R)
        g32 = sb("g32", [P, 2, 2 * TM])
        g_hi = sb("g_hi", [P, HC, TM], F32R)
        g_lo = sb("g_lo", [P, HC, TM], F32R)
        meta_next = sb("meta_next", [P, MH, 2])
        meta_now = sb("meta_now", [P, MH, 2])
        token_i = sb("token_i", [P, MH], I32)
        y1 = sb("y1", [P, MH, D])
        y_out = sb("y_out", [P, MH, D])

        psH = [ctx.enter_context(nc.psum_tensor(f"psH{i}", [P, 2 * TM], F32)) for i in range(NQ)]
        psX = ctx.enter_context(nc.psum_tensor("psX", [P, EC, TM], F32))
        psY = [ctx.enter_context(nc.psum_tensor(f"psY{i}", [P, 512], F32)) for i in range(MH)]

        pads_filled = sem("pads_filled")
        pads_filled2 = sem("pads_filled2")
        x_loaded = sem("x_loaded")
        xT_done = sem("xT_done2")
        meta_taken = sem("meta_taken")
        meta_moved = sem("meta_moved")
        xT_hi_ready = sem("xT_hi_ready")
        xT_ready = sem("xT_ready")
        raw_loaded = sem("raw_loaded2")
        w_hi_ready = sem("w_hi_ready2")
        w1_ready = sem("w1_ready")
        w2_ready = sem("w2_ready")
        w_cut = sem("w_cut")
        b1_taken = sem("b1_taken")
        h_done = sem("h_done")
        gelu_done = sem("gelu_done")
        g_hi_ready = sem("g_hi_ready")
        g_ready = sem("g_ready")
        y_done = sem("y_done")
        y_read = sem("y_read")
        y_ready = sem("y_ready2")
        added = sem("added")
        rows_free = sem("rows_free")
        out_stored = sem("out_stored")
        passed = sem("passed2")

        w1_parts = [(w1_raw[:, c, :], w1_hi[:, c, :], w1_lo[:, c, :]) for c in range(2)]
        w2_parts = [(w2_raw[:, k:k + HC // 2, :], w2_hi[:, k:k + HC // 2, :], w2_lo[:, k:k + HC // 2, :])
                    for k in (0, HC // 2)]
        PARTS = len(w1_parts) + len(w2_parts)

        def is_last(eng, t):
            return eng.value_load(tile_last[0:1, bass.ds(t, 1)], min_val=0, max_val=1) > 0

        def expert_of(eng, t):
            return eng.value_load(tile_expert[0:1, bass.ds(t, 1)], min_val=0, max_val=NE - 1)

        block = ctx.enter_context(nc.Block())

        def fill_pads(eng, experts, filled):
            for e in experts:
                at = eng.value_load(pad_at[0:1, e:e + 1], min_val=0, max_val=NE * REGION - TM) if e < NE else NE * REGION
                eng.dma_start(routed[bass.ds(at, TM)].rearrange("(m p) r -> p m r", p=P), pad_rows[:]).then_inc(filled, 16)

        @block.sync
        def _(sp):
            fill_pads(sp, range(0, NE + 1, 2), pads_filled)
            sp.wait_ge(pads_filled, 16 * (NE // 2 + 1))
            sp.wait_ge(pads_filled2, 16 * (NE // 2))

            def load(t):
                row = sp.value_load(tile_row[0:1, bass.ds(t, 1)], min_val=0, max_val=NE * REGION)
                sp.wait_ge(xT_done, t + 1)
                sp.wait_ge(meta_taken, t + 1)
                sp.dma_start(xrow[:], routed[bass.ds(row, TM)].rearrange("(m p) r -> p m r", p=P)).then_inc(x_loaded, 16)

            with sp.Fori(0, NTILES) as t:
                load(t)
            sp.wait_ge(added, 32 * NTILES)
            sp.dma_start(out.rearrange("b s d -> (b s) d"), total[0:NTOK]).then_inc(out_stored, 16)
            sp.wait_ge(x_loaded, 16 * NTILES)
            sp.wait_ge(out_stored, 16)

        @block.gpsimd
        def _(pool):
            pool.sem_inc(rows_free, 1)
            fill_pads(pool, range(1, NE + 1, 2), pads_filled2)

            def load_expert(e):
                pool.dma_start(w1_raw[:], w1[bass.ds(e, 1)].rearrange("a (c p) h -> p (a c) h", p=P)).then_inc(raw_loaded, 16)
                pool.dma_start(w2_raw[:], w2[bass.ds(e, 1)].rearrange("a (c p) d -> p (a c) d", p=P)).then_inc(raw_loaded, 16)
                pool.dma_start(b1_raw[:], b1[bass.ds(e, 1)].rearrange("a (c p) -> p (a c)", p=P)).then_inc(raw_loaded, 16)
                pool.dma_start(b2_raw[:], b2[bass.ds(e, 1)].to_broadcast([P, D])).then_inc(raw_loaded, 16)

            pool.wait_ge(w_cut, 1)
            pool.wait_ge(b1_taken, 1)
            load_expert(1)
            with pool.Fori(0, NTILES) as t:
                pool.wait_ge(y_ready, t + 1)
                pool.sem_inc(passed, 1)
                for m in range(MH):
                    pool.indirect_dma_start(total, bass.IndirectOffsetOnAxis(ap=token_i[:, m:m + 1], axis=0), y_out[:, m, :],
                                            None, bounds_check=NTOK + TM - 1, compute_op=ALU.add).then_inc(added, 16)
                pool.wait_ge(added, t * 32 + 32)
                pool.sem_inc(rows_free, 1)
                with pool.If(is_last(pool, t)):
                    e = expert_of(pool, t)
                    with pool.If(e < NE - 2):
                        pool.wait_ge(w_cut, e + 2)
                        pool.wait_ge(b1_taken, e + 2)
                        pool.sem_inc(passed, 1)
                        load_expert(nc.s_assert_within(e + 2, 0, NE - 1, skip_runtime_bounds_check_because="the If around it holds it"))

        @block.scalar
        def _(act):
            act.sem_inc(gelu_done, HC)

            def turned_hi(t):
                act.wait_ge(xT_done, t + 2)
                act.activation(xT_hi[:], psX[:], ACT.Copy).then_inc(xT_hi_ready, 1)

            for raw, hi, _ in w1_parts + w2_parts:
                act.activation(hi, raw, ACT.Copy).then_inc(w_hi_ready, 1)
            act.activation(b1_col[:], b1_raw[:], ACT.Copy).then_inc(b1_taken, 1)
            turned_hi(0)
            act.wait_ge(b1_taken, 1)
            with act.Fori(0, NTILES) as t:
                for c in range(HC):
                    q = c // 2
                    if c % 2 == 0:
                        act.wait_ge(h_done, t * HC + (c + 2))
                        act.wait_ge(g_ready, t * NQ + (q - 1 + NQ))
                    act.activation(g32[:, q % 2, (c % 2) * TM:(c % 2 + 1) * TM], psH[q][:, (c % 2) * TM:(c % 2 + 1) * TM],
                                   ACT.Gelu_apprx_tanh, bias=b1_col[:, c:c + 1]).then_inc(gelu_done, 1)
                with act.If(t < NTILES - 1):
                    turned_hi(t + 1)
                with act.If(is_last(act, t)):
                    e = expert_of(act, t)
                    act.wait_ge(raw_loaded, e * 64 + 64)
                    for raw, hi, _ in w1_parts:
                        act.activation(hi, raw, ACT.Copy).then_inc(w_hi_ready, 1)
                    act.wait_ge(gelu_done, t * HC + 2 * HC)
                    act.sem_inc(passed, 1)
                    act.activation(b1_col[:], b1_raw[:], ACT.Copy).then_inc(b1_taken, 1)
                    act.wait_ge(y_done, t * MH + MH)
                    for raw, hi, _ in w2_parts:
                        act.activation(hi, raw, ACT.Copy).then_inc(w_hi_ready, 1)
                    act.wait_ge(b1_taken, e + 2)
                    act.sem_inc(passed, 1)

        @block.vector
        def _(dve):
            dve.sem_inc(meta_taken, 1)
            dve.sem_inc(g_ready, NQ)
            dve.sem_inc(y_read, 1)

            def turned_lo(t):
                dve.wait_ge(xT_hi_ready, t + 1)
                dve.tensor_tensor(xT_lo[:], psX[:], xT_hi[:].bitcast(F32), ALU.subtract).then_inc(xT_ready, 1)

            def take_meta(t):
                dve.wait_ge(x_loaded, t * 16 + 16)
                dve.tensor_copy(meta_next[:], xrow[:, :, D:ROW]).then_inc(meta_taken, 1)

            def cut(parts, first, ready):
                for k, (raw, hi, lo) in enumerate(parts):
                    dve.wait_ge(w_hi_ready, first + (k + 1))
                    ins = dve.tensor_tensor(lo, raw, hi.bitcast(F32), ALU.subtract)
                ins.then_inc(ready, 1)

            def results(t):
                for m in range(MH):
                    dve.wait_ge(y_done, t * MH + (m + 1))
                    ins = dve.tensor_tensor(y1[:, m, :], psY[m][:, 0:D], b2_row[:], ALU.add)
                ins.then_inc(y_read, 1)
                dve.wait_ge(rows_free, t + 1)
                dve.tensor_copy(token_i[:], meta_now[:, :, 0])
                dve.wait_ge(y_read, t + 2)
                for m in range(MH):
                    ins = dve.tensor_scalar(y_out[:, m, :], y1[:, m, :], meta_now[:, m, 1:2], None, ALU.mult)
                ins.then_inc(y_ready, 1)

            cut(w1_parts, 0, w1_ready)
            cut(w2_parts, len(w1_parts), w2_ready)
            dve.tensor_copy(b2_row[:], b2_raw[:]).then_inc(w_cut, 1)
            turned_lo(0)
            take_meta(0)
            dve.wait_ge(w_cut, 1)
            with dve.Fori(0, NTILES) as t:
                for q in range(NQ):
                    dve.wait_ge(gelu_done, t * HC + (2 * q + 2 + HC))
                    g = g32[:, q % 2, :].rearrange("p (c n) -> p c n", c=2)
                    dve.tensor_copy(g_hi[:, 2 * q:2 * q + 2, :], g).then_inc(g_hi_ready, 1)
                    dve.wait_ge(g_hi_ready, t * NQ + (q + 1))
                    dve.tensor_tensor(g_lo[:, 2 * q:2 * q + 2, :], g, g_hi[:, 2 * q:2 * q + 2, :].bitcast(F32),
                                      ALU.subtract).then_inc(g_ready, 1)
                dve.wait_ge(meta_taken, t + 2)
                dve.tensor_copy(meta_now[:], meta_next[:]).then_inc(meta_moved, 1)
                dve.wait_ge(meta_moved, t + 1)
                dve.sem_inc(passed, 1)
                with dve.If(t < NTILES - 1):
                    turned_lo(t + 1)
                    take_meta(t + 1)
                with dve.If(is_last(dve, t)):
                    e = expert_of(dve, t)
                    cut(w1_parts, e * PARTS + PARTS, w1_ready)
                    results(t)
                    cut(w2_parts, e * PARTS + (PARTS + len(w1_parts)), w2_ready)
                    dve.tensor_copy(b2_row[:], b2_raw[:]).then_inc(w_cut, 1)
                    dve.wait_ge(w_cut, e + 2)
                    dve.sem_inc(passed, 1)
                with dve.Else():
                    dve.sem_inc(w1_ready, 1)
                    dve.sem_inc(w2_ready, 1)
                    results(t)

        @block.tensor
        def _(pe):
            pe.sem_inc(xT_done, 1)

            def turn(t):
                pe.wait_ge(x_loaded, t * 16 + 16)
                for c in range(EC):
                    for m in range(MH):
                        ins = pe.transpose(psX[:, c, m * P:(m + 1) * P], xrow[:, m, c * P:(c + 1) * P], ident[:])
                ins.then_inc(xT_done, 1)

            def first_layer(t):
                pe.wait_ge(xT_ready, t + 1)
                pe.wait_ge(w1_ready, t + 1)
                for c in range(HC):
                    q = c // 2
                    if c % 2 == 0:
                        pe.wait_ge(gelu_done, t * HC + (2 * q + 2))
                    o = psH[q][:, (c % 2) * TM:(c % 2 + 1) * TM]
                    f = slice(c * P, (c + 1) * P)
                    parts = [p for k in range(EC) for p in ((w1_hi[:, k, f], xT_hi[:, k, :]), (w1_hi[:, k, f], xT_lo[:, k, :]),
                                                            (w1_lo[:, k, f], xT_hi[:, k, :]))]
                    for n, (l, r) in enumerate(parts):
                        ins = pe.matmul(o, l, r, start=(n == 0), stop=(n == len(parts) - 1))
                    ins.then_inc(h_done, 1)

            def second_layer(t):
                pe.wait_ge(y_read, t + 1)
                pe.wait_ge(w2_ready, t + 1)
                for q in range(NQ):
                    pe.wait_ge(g_ready, t * NQ + (q + 1 + NQ))
                    for m in range(MH):
                        cols = slice(m * P, (m + 1) * P)
                        for c in (2 * q, 2 * q + 1):
                            for n, (l, r) in enumerate(((g_hi, w2_hi), (g_hi, w2_lo), (g_lo, w2_hi))):
                                ins = pe.matmul(psY[m][:, 0:D], l[:, c, cols], r[:, c, :], start=(c == 0 and n == 0),
                                                stop=(c == HC - 1 and n == 2))
                        if q == NQ - 1:
                            ins.then_inc(y_done, 1)

            turn(0)
            with pe.Fori(0, NTILES - 1) as t:
                first_layer(t)
                turn(t + 1)
                second_layer(t)
            first_layer(NTILES - 1)
            second_layer(NTILES - 1)


_INS = ['x', 'ctx_768', 'mask_BxS2_bk0', 'g_xattn', 'g_ffn', 'L0_xattn_ln_x_g', 'L0_xattn_ln_x_b', 'L0_xattn_ln_l_g',
        'L0_xattn_ln_l_b', 'L0_xattn_qn_g', 'L0_xattn_kn_g', 'L0_xattn_Wq', 'L0_xattn_Wkv', 'L0_xattn_Wlkv', 'L0_xattn_Wo',
        'L0_xattn_bo', 'L0_ffn_w_router', 'L0_ffn_w1', 'L0_ffn_b1', 'L0_ffn_w2', 'L0_ffn_b2']


def kernel(**inputs):
    import numpy as np
    import concourse.bacc as bacc
    from concourse.bass_utils import run_bass_kernel_spmd

    nc = bacc.Bacc("TRN2", target_bir_lowering=False, num_devices=1)
    arrays, args = {}, []
    for name in _INS:
        a = np.ascontiguousarray(inputs[name])
        arrays[f"in_{name}"] = a
        args.append(nc.dram_tensor(f"in_{name}", a.shape, mybir.dt.from_np(a.dtype), kind="ExternalInput").ap())
    shape = inputs["x"].shape
    out = nc.dram_tensor("out", shape, F32, kind="ExternalOutput").ap()
    flamingo_gated_layer(nc, *args, out)
    r = run_bass_kernel_spmd(nc, [arrays], core_ids=[0])
    return r.results[0]["out"]
```

```python
from contextlib import ExitStack

import concourse.bass as bass
from concourse import mybir

F32 = mybir.dt.float32
F32R = mybir.dt.float32r
BF16 = mybir.dt.bfloat16
I32 = mybir.dt.int32
U8 = mybir.dt.uint8
ALU = mybir.AluOpType
ACT = mybir.ActivationFunctionType
AX = mybir.AxisListType.X

P = 128


def flamingo_gated_layer(nc, x, ctx_768, mask, g_xattn, g_ffn, ln_x_g, ln_x_b, ln_l_g, ln_l_b, qn_g, kn_g,
                         Wq, Wkv, Wlkv, Wo, bo, w_router, w1, b1, w2, b2, out):
    B, S, D = x.shape
    _, SC, DC = ctx_768.shape
    DH = qn_g.shape[0]
    H = Wq.shape[0] // DH
    NE = w_router.shape[1]
    HID = w1.shape[2]
    T = S // P
    NT = T + 1
    EC = D // P
    QK = 2 * H * DH
    HALF = S // 2
    HT = T // 2
    GROUPS_W = 6
    LATENT_GROUPS = 2 * EC
    GROUPS = LATENT_GROUPS + 2
    KT = NT
    NI = H * KT
    BLOCK = 32
    OUT_SLOTS = 3
    NP_RING = 3
    POOL_LO = (16, 18, 25, 27)
    ROWS_AT = 4
    AHEAD = 2
    EPS, RMS_EPS = 1e-5, 1e-8
    SCALE = float(DH) ** -0.5
    SAFE = 60.0
    TM = 256
    MH = TM // P
    NTOK = B * S
    REGION = NTOK + TM
    ROW = D + 2
    HC = HID // P
    NTILES = 2 * NTOK // TM + NE - 1

    routed = nc.dram_tensor("routed", (NE * REGION, ROW), F32).ap()
    total = nc.dram_tensor("total", (NTOK + TM, D), F32).ap()

    persistent = ExitStack()
    with persistent, nc.allow_non_contiguous_dma(reason="columns of parameters, a few bytes each"):
        pad_rows = persistent.enter_context(nc.sbuf_tensor("pad_rows", [P, MH, ROW], F32))
        pad_at = persistent.enter_context(nc.sbuf_tensor("pad_at", [P, NE], I32))
        tile_count = persistent.enter_context(nc.sbuf_tensor("tile_count", [P, 1], I32))
        tile_row = persistent.enter_context(nc.sbuf_tensor("tile_row", [P, NTILES], I32))
        tile_switch = persistent.enter_context(nc.sbuf_tensor("tile_switch", [P, NTILES], I32))
        b1_raw = persistent.enter_context(nc.sbuf_tensor("b1_raw", [P, HC], F32))
        b2_raw = persistent.enter_context(nc.sbuf_tensor("b2_raw", [P, D], F32))
        ident = persistent.enter_context(nc.sbuf_tensor("ident", [P, P], F32))
        lnf = persistent.enter_context(nc.sbuf_tensor("lnf", [P, 2, HALF], F32))
        xr = persistent.enter_context(nc.sbuf_tensor("xr", [P, T, D], F32))
        xn = persistent.enter_context(nc.sbuf_tensor("xn", [P, T, D], F32))
        Q1 = persistent.enter_context(nc.sbuf_tensor("Q1", [P, H, S], F32R))
        K1 = persistent.enter_context(nc.sbuf_tensor("K1", [P, H, S + P], F32R))
        flat = lambda a: a[:].rearrange("p a b -> p (a b)")
        xrow = flat(lnf)[:, 0:MH * ROW].rearrange("p (m r) -> p m r", m=MH)
        x_loaded = persistent.enter_context(nc.semaphore("x_loaded"))
        w1_raw = flat(xr).rearrange("p (c h) -> p c h", c=EC)
        w2_raw = flat(xn).rearrange("p (c d) -> p c d", c=HC)
        w1_hi, w1_lo = (flat(Q1)[:, k * EC * HID:(k + 1) * EC * HID].rearrange("p (c h) -> p c h", c=EC) for k in range(2))
        w2_hi, w2_lo = (flat(K1)[:, k * HC * D:(k + 1) * HC * D].rearrange("p (c d) -> p c d", c=HC) for k in range(2))
        w1_parts = [tuple(w[:, :, k * HID // 2:(k + 1) * HID // 2] for w in (w1_raw, w1_hi, w1_lo)) for k in range(2)]
        w2_parts = [tuple(w[:, k * HC // 2:(k + 1) * HC // 2, :] for w in (w2_raw, w2_hi, w2_lo)) for k in range(2)]

        with ExitStack() as ctx:
            def sb(name, shape, dt=F32):
                return ctx.enter_context(nc.sbuf_tensor(name, shape, dt))

            def sem(name):
                return ctx.enter_context(nc.semaphore(name))

            w_hi = sb("w_hi", [P, EC, 768], F32R)
            w_lo = sb("w_lo", [P, EC, 768], F32R)
            wo_hi = sb("wo_hi", [P, EC, D], F32R)
            wo_lo = sb("wo_lo", [P, EC, D], F32R)
            wc_hi = sb("wc_hi", [P, 2, 512], F32R)
            wc_lo = sb("wc_lo", [P, 2, 512], F32R)
            router = sb("router", [P, EC, NE])
            tri = sb("tri", [P, P], BF16)
            ones = sb("ones", [P, P], BF16)
            gl = sb("gl", [P, EC])
            bl = sb("bl", [P, EC])
            gx = sb("gx", [P, 2])
            bx = sb("bx", [P, 2])
            qg = sb("qg", [P, 1])
            kg = sb("kg", [P, 1])
            gqk = sb("gqk", [P, 1])
            qg_row = sb("qg_row", [P, DH])
            kg_row = sb("kg_row", [P, DH])
            gate_raw = sb("gate_raw", [P, 2])
            gate = sb("gate", [P, 2])
            bo_row = sb("bo_row", [P, D])
            tbo = sb("tbo", [P, D])
            shift = sb("shift", [P, 1])
            minus_half = sb("minus_half", [P, 16])
            iota_i = sb("iota_i", [P, 16], I32)
            expert_id = sb("expert_id", [P, NE])
            region0 = sb("region0", [P, NE])
            token_id = sb("token_id", [P, T])
            cr = sb("cr", [SC, DC])
            mask_u8 = sb("mask_u8", [SC, 1], U8)
            mask_bias = sb("mask_bias", [SC, 1])
            stats = sb("stats", [P, NT, 6])
            mv = sb("mv", [P, NT, 2])
            var_in = sb("var_in", [P, NT])
            rstd = sb("rstd", [P, NT])
            cn = sb("cn", [SC, 2 * P])
            xb = sb("xb", [P, T, D])
            ln_hi = sb("ln_hi", [P, EC, S], F32R)
            ln_lo = sb("ln_lo", [P, EC, S], F32R)
            lc_hi = sb("lc_hi", [P, 2, P], F32R)
            lc_lo = sb("lc_lo", [P, 2, P], F32R)
            big = sb("big", [P, 2 * T * ROW])
            qk_sb = sb("qk_sb", [P, 3, QK])
            sq = sb("sq", [P, 2, QK])
            ss = sb("ss", [P, 2, 8])
            ssm = sb("ssm", [P, 2, 8])
            rr = sb("rr", [P, 2, 8])
            qkd = sb("qkd", [P, 2, 2 * QK])
            K2 = sb("K2", [P, H // 2, S + P], F32R)
            V_hi = sb("V_hi", [P, KT, H // 2 * 3 * DH], F32R)
            V_lo = sb("V_lo", [P, KT, H // 2 * 3 * DH], F32R)
            p_ring_hi = sb("p_ring_hi", [P, 2, S], F32R)
            p_ring_lo = sb("p_ring_lo", [P, 2, S], F32R)
            st2 = sb("st2", [P, T, 6])
            mv2 = sb("mv2", [P, T, 2])
            var2 = sb("var2", [P, T])
            rstd2 = sb("rstd2", [P, T])
            lg = sb("lg", [P, T, NE])
            lmax = sb("lmax", [P, T])
            lz = sb("lz", [P, T, NE])
            pe_ = sb("pe_", [P, T, NE])
            psum_ = sb("psum_", [P, T])
            prob = sb("prob", [P, T, NE])
            top = sb("top", [P, 2, T])
            eq = sb("eq", [P, T, NE])
            cand = sb("cand", [P, T, NE])
            pick = sb("pick", [P, 2, T])
            hot = sb("hot", [P, 2, T, NE])
            prob2 = sb("prob2", [P, T, NE])
            chosen = sb("chosen", [P, T * NE], BF16)
            base = sb("base", [P, T + 1, NE])
            slot = sb("slot", [P, T, NE])
            slot_hot = sb("slot_hot", [P, 2, T, NE])
            slot_f = sb("slot_f", [P, 2, T])
            slot_i = sb("slot_i", [P, 2, T], I32)
            den_inv = sb("den_inv", [P, HALF // BLOCK])
            tiles_i = sb("tiles_i", [P, NE], I32)
            tiles = sb("tiles", [P, NE])
            ends = sb("ends", [P, NE])
            jump = sb("jump", [P, NE])
            tile_i = sb("tile_i", [P, NTILES], I32)
            tile_id = sb("tile_id", [P, NTILES])
            begun = sb("begun", [P, NTILES, NE])
            jumped = sb("jumped", [P, NTILES, NE])
            row_f = sb("row_f", [P, NTILES])
            expert_f = sb("expert_f", [P, NTILES])
            last_f = sb("last_f", [P, NTILES])

            att_hi, att_lo = ln_hi, ln_lo
            p_f32 = [qk_sb[:, 0:2, :].rearrange("p t d -> p (t d)"), sq[:].rearrange("p t d -> p (t d)")]
            p_hi = [ln_hi[:, 1, :], p_ring_hi[:, 0, :], p_ring_hi[:, 1, :]]
            p_lo = [ln_lo[:, 1, :], p_ring_lo[:, 0, :], p_ring_lo[:, 1, :]]
            den = lnf[:].rearrange("p t d -> p (t d)")
            attf = qkd
            yT = xn[:].rearrange("p t d -> p (t d)").rearrange("p (c s) -> p c s", c=EC)
            wst_q = big[:, 0:512].rearrange("p (b e) -> p b e", b=2)
            wst_l = big[:, 512:1536].rearrange("p (b e) -> p b e", b=4)
            wst_o = big[:, 1536:2048].rearrange("p (b e) -> p b e", b=2)
            wst_c = big[:, 2048:2048 + 4 * 2 * P].rearrange("p (b e) -> p b e", b=4)
            rows = [big[:, k * T * ROW:(k + 1) * T * ROW].rearrange("p (t r) -> p t r", t=T) for k in range(2)]

            psS = [ctx.enter_context(nc.psum_tensor(f"psS{i}", [P, S], F32)) for i in range(2)]
            psO = [ctx.enter_context(nc.psum_tensor(f"psO{i}", [P, S], F32)) for i in range(2)]

            consts_loaded = sem("consts_loaded")
            weights_loaded = sem("weights_loaded")
            ident_ready = sem("ident_ready")
            iota_done = sem("iota_done")
            pool_const = sem("pool_const")
            dve_const = sem("dve_const")
            gate_ready = sem("gate_ready")
            wT_done = sem("wT_done")
            w_hi_ready = sem("w_hi_ready")
            w_ready = sem("w_ready")
            seq_loaded = sem("seq_loaded")
            stat_ready = sem("stat_ready")
            mv_ready = sem("mv_ready")
            var_ready = sem("var_ready")
            rstd_ready = sem("rstd_ready")
            xn_ready = sem("xn_ready")
            xb_ready = sem("xb_ready")
            mask_cut = sem("mask_cut")
            mask_ready = sem("mask_ready")
            xT_done = sem("xT_done")
            ln_hi_ready = sem("ln_hi_ready")
            ln_ready = sem("ln_ready")
            proj_done = sem("proj_done")
            proj_read = sem("proj_read")
            ss_ready = sem("ss_ready")
            ssm_ready = sem("ssm_ready")
            rr_ready = sem("rr_ready")
            qkd_ready = sem("qkd_ready")
            qkT_done = sem("qkT_done")
            qk_hi_ready = sem("qk_hi_ready")
            qk_ready = sem("qk_ready")
            v_ready = sem("v_ready")
            s_done = sem("s_done")
            p_hi_done = sem("p_hi_done")
            p_ready = sem("p_ready")
            p_ready_pool = sem("p_ready_pool")
            exp_done = sem("exp_done")
            av_done = sem("av_done")
            den_step = sem("den_step")
            den_ready = sem("den_ready")
            o_read = sem("o_read")
            att_hi_ready = sem("att_hi_ready")
            att_ready = sem("att_ready")
            o_done = sem("o_done")
            x2_ready = sem("x2_ready")
            x2_stored = sem("x2_stored")
            st2_ready = sem("st2_ready")
            mv2_ready = sem("mv2_ready")
            var2_ready = sem("var2_ready")
            rstd2_ready = sem("rstd2_ready")
            y_ready = [sem("y_ready"), sem("y_ready_pool")]
            y2_ready = sem("y2_ready")
            yT_done = sem("yT_done")
            yT_ready = sem("yT_ready")
            logits_done = sem("logits_done")
            route = sem("route")
            ez_ready = sem("ez_ready")
            chosen_ready = sem("chosen_ready")
            rank_done = sem("rank_done")
            base_ready = sem("base_ready")
            plan_ready = sem("plan_ready")
            slots_ready = sem("slots_ready")
            scattered = sem("scattered")
            dump_zeroed = sem("dump_zeroed")
            zero_ready = sem("zero_ready")
            raw_loaded = sem("raw_loaded")
            first_hi_ready = sem("first_hi_ready")
            first_cut = sem("first_cut")
            pads_known = sem("pads_known")
            rows_known = sem("rows_known")
            pads_filled = sem("pads_filled")
            passed = sem("passed")

            NCONST = 16
            NPOOL = 17
            ROUTE = 21
            block = ctx.enter_context(nc.Block())

            def load_sequence(sp, b):
                sp.dma_start(xr[:], x[bass.ds(b, 1)].rearrange("a (t p) d -> p (a t) d", p=P)).then_inc(seq_loaded, 16)
                sp.dma_start(cr[:], ctx_768[bass.ds(b, 1)].rearrange("a s d -> (a s) d")).then_inc(seq_loaded, 16)
                sp.dma_start(mask_u8[:], mask[bass.ds(b, 1)].rearrange("a s -> s a")).then_inc(seq_loaded, 16)

            def store_tokens(sp, b):
                sp.wait_ge(x2_ready, b * T + T)
                sp.dma_start(total[bass.ds(b * S, S)].rearrange("(t p) d -> p t d", p=P), xb[:]).then_inc(x2_stored, 16)

            def value_slots(V, t, p):
                return V[0:p, t, :].rearrange("p (i s d) -> p i s d", i=H // 2, s=3)[:, :, 0:3:2, :]

            def halves(odd):
                return (slice(DH, P), slice(0, DH)) if odd else (slice(0, DH), slice(DH, P))

            def turned_heads(t, keep):
                ps, n = psS[t % 2], P if t < T else SC
                pairs = lambda c: ps[keep, c:c + H // 2 * n].rearrange("p (h n) -> p h n", h=H // 2)
                return pairs(0), pairs(H // 2 * P), slice(t * P, t * P + n)

            def wait_probabilities(eng, b, i):
                before = sum(k < i for k in POOL_LO)
                if i in POOL_LO:
                    eng.wait_ge(p_ready_pool, b * len(POOL_LO) + (before + 1))
                else:
                    eng.wait_ge(p_ready, b * (NI - len(POOL_LO)) + (i - before + 1))

            def probabilities_lo(eng, b, i):
                p = P if i % KT < T else SC
                eng.wait_ge(exp_done, b * NI + (i + 1))
                hi = p_hi[i % NP_RING]
                lo = p_lo[i % NP_RING] if i % KT < T else hi[SC:2 * SC, :]
                return eng.tensor_tensor(lo[0:p, :], p_f32[i % 2][0:p, :], hi[0:p, :].bitcast(F32), ALU.subtract)

            def normed_row(eng, b, t):
                if t % HT == 0:
                    eng.wait_ge(rstd2_ready, b + 1)
                    eng.sem_inc(passed, 1)
                eng.tensor_scalar(rows[0][:, t, 0:D], xb[:, t, :], mv2[:, t, 0:1], rstd2[:, t:t + 1], ALU.subtract,
                                  ALU.mult).then_inc(y_ready[t // HT], 1)

            def norm_group(g):
                if g >= LATENT_GROUPS:
                    c = g - LATENT_GROUPS
                    return lnf[:, g % 2, 0:SC], lc_hi[:, c, 0:SC], lc_lo[:, c, 0:SC]
                hb, c = divmod(g, EC)
                cols = slice(hb * HALF, (hb + 1) * HALF)
                return lnf[:, g % 2, :], ln_hi[:, c, cols], ln_lo[:, c, cols]

            def weight_groups():
                f = lambda o, n: o[:, n * HALF:(n + 1) * HALF]
                two = lambda a: a.rearrange("p (c n) -> p c n", c=2)
                yield f(psS[0], 0), w_hi[:, 0, 0:QK], w_lo[:, 0, 0:QK]
                yield f(psS[0], 1), w_hi[:, 1, 0:QK], w_lo[:, 1, 0:QK]
                yield two(f(psS[1], 0)), w_hi[:, :, QK:768], w_lo[:, :, QK:768]
                yield two(f(psS[1], 1)), wo_hi[:], wo_lo[:]
                yield f(psO[0], 0), wc_hi[:, 0, :], wc_lo[:, 0, :]
                yield f(psO[0], 1), wc_hi[:, 1, :], wc_lo[:, 1, :]

            def norm_psum(g):
                if g >= LATENT_GROUPS:
                    return psS[0][:, (g - LATENT_GROUPS) * HALF:(g - LATENT_GROUPS) * HALF + SC]
                hb, c = divmod(g, EC)
                return psS[hb][:, c * HALF:(c + 1) * HALF]

            def scores_psum(i):
                return psS[(i + 1) % 2]

            def out_psum(t):
                n = t % OUT_SLOTS
                return psO[n // 2][:, (n % 2) * HALF:(n % 2) * HALF + D]

            @block.sync
            def _(sp):
                load_sequence(sp, 0)
                sp.dma_start(wst_q, Wq.rearrange("(b p) e -> p b e", p=P)).then_inc(weights_loaded, 16)
                sp.dma_start(wst_l, Wlkv.rearrange("(b p) e -> p b e", p=P)).then_inc(weights_loaded, 16)
                sp.dma_start(wst_c[:, :, 0:DC], Wkv.rearrange("(b p) e -> p b e", p=P)).then_inc(weights_loaded, 16)
                sp.dma_start(wst_o, Wo.rearrange("(b p) e -> p b e", p=P)).then_inc(weights_loaded, 16)
                sp.wait_ge(pool_const, 2)
                column = lambda v: v.rearrange("(d a) -> d a", a=1)
                wide = lambda v: v.rearrange("(a d) -> a d", a=1)
                for dst, src in (
                    (gl[:], ln_l_g.rearrange("(c p) -> p c", p=P)), (bl[:], ln_l_b.rearrange("(c p) -> p c", p=P)),
                    (gx[:, 0:1], column(ln_x_g[0:P])), (bx[:, 0:1], column(ln_x_b[0:P])),
                    (gx[0:DC - P, 1:2], column(ln_x_g[P:DC])), (bx[0:DC - P, 1:2], column(ln_x_b[P:DC])),
                    (qg[0:DH, :], column(qn_g)), (qg[DH:P, :], column(qn_g)),
                    (kg[0:DH, :], column(kn_g)), (kg[DH:P, :], column(kn_g)),
                    (qg_row[:], wide(qn_g).to_broadcast([P, DH])), (kg_row[:], wide(kn_g).to_broadcast([P, DH])),
                    (gate_raw[:, 0:1], wide(g_xattn).to_broadcast([P, 1])),
                    (gate_raw[:, 1:2], wide(g_ffn).to_broadcast([P, 1])),
                    (bo_row[:], wide(bo).to_broadcast([P, D])),
                    (router[:], w_router.rearrange("(c p) e -> p c e", p=P)),
                ):
                    sp.dma_start(dst, src).then_inc(consts_loaded, 16)
                sp.dma_start(b1_raw[:], b1[0].rearrange("(c p) -> p c", p=P)).then_inc(raw_loaded, 16)
                sp.dma_start(b2_raw[:], b2[0:1].to_broadcast([P, D])).then_inc(raw_loaded, 16)
                sp.wait_ge(zero_ready, 1)
                sp.dma_start(total[NTOK:NTOK + TM].rearrange("(t p) d -> p t d", p=P),
                             pad_rows[:, :, 0:D]).then_inc(dump_zeroed, 16)
                with sp.Fori(0, B - 1) as b:
                    sp.wait_ge(xn_ready, b * 3 + 3)
                    sp.sem_inc(passed, 1)
                    sp.wait_ge(xb_ready, b + 1)
                    sp.wait_ge(mask_ready, b + 1)
                    load_sequence(sp, b + 1)
                    store_tokens(sp, b)
                sp.wait_ge(xb_ready, B)
                sp.wait_ge(xn_ready, B * 3)
                sp.dma_start(w1_raw, w1[0].rearrange("(c p) h -> p c h", p=P)).then_inc(raw_loaded, 16)
                store_tokens(sp, B - 1)
                sp.wait_ge(logits_done, B)
                sp.dma_start(w2_raw, w2[0].rearrange("(c p) d -> p c d", p=P)).then_inc(raw_loaded, 16)
                sp.wait_ge(pads_known, 1)
                for e in range(NE):
                    at = sp.value_load(pad_at[0:1, e:e + 1], min_val=0, max_val=NE * REGION - TM)
                    sp.dma_start(routed[bass.ds(at, TM)].rearrange("(m p) r -> p m r", p=P), pad_rows[:]).then_inc(pads_filled, 16)
                sp.wait_ge(pads_filled, 16 * NE)
                sp.wait_ge(rows_known, 1)
                row = sp.value_load(tile_row[0:1, 0:1], min_val=0, max_val=NE * REGION - TM)
                sp.wait_ge(scattered, B * (32 * T))
                sp.dma_start(xrow, routed[bass.ds(row, TM)].rearrange("(m p) r -> p m r", p=P)).then_inc(x_loaded, 16)
                sp.wait_ge(x2_stored, 16 * B)
                sp.wait_ge(dump_zeroed, 16)
                sp.wait_ge(raw_loaded, 64)

            @block.gpsimd
            def _(pool):
                for a, value in ((gx, 0.0), (bx, 0.0), (ident, 0.0), (tri, 1.0), (ones, 1.0), (minus_half, -0.5), (pad_rows, 0.0),
                                 (var_in, 1.0), (base, 0.0)):
                    pool.memset(a[:], value).then_inc(pool_const, 1)
                pool.wait_ge(pool_const, 4)
                pool.affine_select(out=ident[:], in_=ident[:], compare_op=ALU.not_equal, fill=1.0, base=0,
                                   pattern=[[-1, P]], channel_multiplier=1).then_inc(ident_ready, 1)
                pool.affine_select(out=tri[:], in_=tri[:], compare_op=ALU.is_gt, fill=0.0, base=0,
                                   pattern=[[1, P]], channel_multiplier=-1).then_inc(ident_ready, 1)
                for a, value in ((wst_c[:, :, DC:2 * P], 0.0), (cn[:, DC:2 * P], 0.0), (lc_hi[:, :, SC:P], 0.0), (lc_lo[:, :, SC:P], 0.0),
                                 (K1[:, :, S + SC:S + P], 0.0), (K2[:, :, S + SC:S + P], 0.0), (V_hi[:], 1.0), (V_lo[:], 0.0)):
                    pool.memset(a if a.dtype == F32 else a.bitcast(F32), value).then_inc(pool_const, 1)
                pool.iota(iota_i[:, 0:8], [[1, 8]], base=0, channel_multiplier=0).then_inc(iota_done, 1)
                pool.iota(iota_i[:, 8:16], [[P, 8]], base=0, channel_multiplier=1).then_inc(iota_done, 1)
                pool.iota(tile_i[:], [[1, NTILES]], base=0, channel_multiplier=0).then_inc(iota_done, 1)
                pool.engine_nop().then_inc(zero_ready, 1)

                def norm_root(b):
                    pool.wait_ge(var_ready, b + 1)
                    pool.tensor_tensor(rstd[:], var_in[:], minus_half[:, 0:NT], ALU.pow).then_inc(rstd_ready, 1)

                def second_root(b):
                    pool.wait_ge(var2_ready, b + 1)
                    pool.tensor_tensor(rstd2[:], var2[:], minus_half[:, 0:T], ALU.pow).then_inc(rstd2_ready, 1)

                def head_roots(b, with_rows):
                    for t in range(NT):
                        n = 8 if t < T else H
                        p = P if t < T else SC
                        pool.wait_ge(ssm_ready, b * NT + (t + 1))
                        pool.tensor_tensor(rr[0:p, t % 2, 0:n], ssm[0:p, t % 2, 0:n], minus_half[0:p, 0:n],
                                           ALU.pow).then_inc(rr_ready, 1)
                        if with_rows and t == 1:
                            second_root(b - 1)
                        if with_rows and 2 <= t < 2 + T - HT:
                            normed_row(pool, b - 1, HT + t - 2)

                def residual(b):
                    pool.tensor_tensor(xb[:], xr[:], tbo[:].unsqueeze(1).to_broadcast([P, T, D]),
                                       ALU.add).then_inc(xb_ready, 1)

                def scatter(b):
                    pool.wait_ge(slots_ready, b + 1)
                    pool.wait_ge(y2_ready, b + 1)
                    pool.sem_inc(passed, 1)
                    for t in range(T):
                        for k in range(2):
                            pool.indirect_dma_start(routed, bass.IndirectOffsetOnAxis(ap=slot_i[:, k, t:t + 1], axis=0),
                                                    rows[k][:, t, :], None,
                                                    bounds_check=NE * REGION - 1).then_inc(scattered, 16)

                def second_rows(b):
                    for half in y_ready:
                        pool.wait_ge(half, b * HT + HT)
                        pool.sem_inc(passed, 1)
                    pool.tensor_copy(rows[1][:, :, 0:D], rows[0][:, :, 0:D]).then_inc(y2_ready, 1)

                def cut_probabilities(b, steps):
                    for i in steps:
                        probabilities_lo(pool, b, i).then_inc(p_ready_pool, 1)

                norm_root(0)
                head_roots(0, False)
                pool.wait_ge(dve_const, 5)
                pool.wait_ge(seq_loaded, 48)
                residual(0)
                cut_probabilities(0, POOL_LO[0:2])
                norm_root(1)
                cut_probabilities(0, POOL_LO[2:])
                with pool.Fori(1, B) as b:
                    head_roots(b, True)
                    pool.wait_ge(x2_stored, b * 16)
                    for half in y_ready:
                        pool.wait_ge(half, b * HT)
                        pool.sem_inc(passed, 1)
                    residual(b)
                    second_rows(b - 1)
                    scatter(b - 1)
                    cut_probabilities(b, POOL_LO[0:2])
                    with pool.If(b < B - 1):
                        norm_root(b + 1)
                    cut_probabilities(b, POOL_LO[2:])
                    pool.wait_ge(scattered, b * (32 * T))
                    pool.sem_inc(passed, 1)
                second_root(B - 1)
                scatter(B - 1)
                pool.wait_ge(scattered, B * (32 * T))

            @block.scalar
            def _(act):
                for g, (src, dst, _) in enumerate(weight_groups()):
                    act.wait_ge(wT_done, g + 1)
                    act.activation(dst, src, ACT.Copy).then_inc(w_hi_ready, 1)

                act.wait_ge(consts_loaded, 16 * NCONST)
                act.activation(gate[:], gate_raw[:], ACT.Tanh).then_inc(gate_ready, 1)

                def front(b, with_router):
                    def norm_hi(g):
                        gain, bias = (gl, bl) if g < LATENT_GROUPS else (gx, bx)
                        c = g % EC if g < LATENT_GROUPS else g - LATENT_GROUPS
                        dst, hi, _ = norm_group(g)
                        act.wait_ge(xT_done, b * GROUPS + (g + 1))
                        if g >= 2:
                            act.wait_ge(ln_ready, b * GROUPS + (g - 1))
                        act.activation(dst, norm_psum(g), ACT.Identity, scale=gain[:, c:c + 1], bias=bias[:, c:c + 1])
                        if with_router and g in (0, EC):
                            act.wait_ge(o_done, b * T - (HT if g == 0 else 0))
                        act.activation(hi, norm_psum(g), ACT.Identity, scale=gain[:, c:c + 1],
                                       bias=bias[:, c:c + 1]).then_inc(ln_hi_ready, 1)

                    def read_projection(t):
                        act.wait_ge(proj_done, b * NT + (t + 1))
                        if t >= 3:
                            act.wait_ge(qkd_ready, b * NT + (t - 2))
                        if t >= 2:
                            act.wait_ge(ss_ready, b * NT + (t - 1))
                        o = psO[t % 2]
                        if t < T:
                            act.activation(qk_sb[:, t % 3, :], o[:, 0:QK], ACT.Copy)
                            act.activation(sq[:, t % 2, :], o[:, 0:QK], ACT.Square)
                            act.activation(value_slots(V_hi, t, P), o[:, QK:QK + H * DH].rearrange(
                                "p (i s d) -> p i s d", i=2, s=2), ACT.Copy).then_inc(proj_read, 1)
                        else:
                            act.activation(qk_sb[0:SC, t % 3, 0:H * DH], o[0:SC, 0:H * DH], ACT.Copy)
                            act.activation(sq[0:SC, t % 2, 0:H * DH], o[0:SC, 0:H * DH], ACT.Square)
                            for rows_of in (slice(0, SC), slice(SC, 2 * SC)):
                                ins = act.activation(value_slots(V_hi[rows_of], t, SC), o[0:SC, H * DH:2 * H * DH].rearrange(
                                    "p (i s d) -> p i s d", i=2, s=2), ACT.Copy)
                            ins.then_inc(proj_read, 1)

                    def heads_hi(t):
                        act.wait_ge(qkT_done, b * NT + (t + 1))
                        for odd in range(2):
                            keep, other = halves(odd)
                            q_src, k_src, cols = turned_heads(t, keep)
                            if t < T:
                                act.activation(Q1[keep, odd:H:2, cols], q_src, ACT.Copy, scale=gqk[keep, 0:1])
                            act.activation(K1[keep, odd:H:2, cols], k_src, ACT.Copy)
                            ins = act.activation(K1[other, odd:H:2, cols], k_src, ACT.Copy)
                        ins.then_inc(qk_hi_ready, 1)

                    for g in range(LATENT_GROUPS):
                        norm_hi(g)
                    if not with_router:
                        act.wait_ge(dve_const, 5)
                    for t in range(NT + 2):
                        if t < NT:
                            read_projection(t)
                        if t == 1:
                            for g in range(LATENT_GROUPS, GROUPS):
                                norm_hi(g)
                        if t >= 2:
                            heads_hi(t - 2)
                    if with_router:
                        turned_rows(b - 1)

                def turned_rows(b):
                    for hb in range(2):
                        act.wait_ge(yT_done, b * 2 + (hb + 1))
                        act.activation(yT[:, :, hb * HALF:(hb + 1) * HALF],
                                       psO[1 - hb][:].rearrange("p (c n) -> p c n", c=EC), ACT.Copy).then_inc(yT_ready, 1)

                def router_exp(b):
                    act.wait_ge(route, b * ROUTE + 3)
                    act.activation(pe_[:], lz[:], ACT.Exp).then_inc(ez_ready, 1)

                def second_rows(b):
                    for half in y_ready:
                        act.wait_ge(half, b * HT + HT)
                    act.activation(rows[1][:, :, 0:D], rows[0][:, :, 0:D], ACT.Copy).then_inc(y2_ready, 1)

                def attention(b, with_router):
                    def attention_hi(c, n):
                        act.wait_ge(o_read, b * 2 * H + (4 * c + 3 + n))
                        cols = slice(n * HALF, (n + 1) * HALF)
                        act.activation(att_hi[:, c, cols], attf[:, c, cols], ACT.Copy).then_inc(att_hi_ready, 1)

                    act.wait_ge(mask_ready, b + 1)
                    for i in range(NI):
                        h, kt = divmod(i, KT)
                        p = P if kt < T else SC
                        bias = shift[:, 0:1] if kt < T else mask_bias[:, 0:1]
                        act.wait_ge(s_done, b * NI + (i + 1))
                        if i >= NP_RING:
                            act.wait_ge(av_done, b * NI + (i - NP_RING + 1))
                        act.activation(p_hi[i % NP_RING][0:p, :], scores_psum(i)[0:p, :], ACT.Exp, bias=bias).then_inc(p_hi_done, 1)
                        if i >= 2:
                            wait_probabilities(act, b, i - 2)
                        act.activation(p_f32[i % 2][0:p, :], scores_psum(i)[0:p, :], ACT.Exp, bias=bias).then_inc(exp_done, 1)
                        if with_router and i == 1:
                            router_exp(b - 1)
                        if i in (24, 25):
                            attention_hi(0, i - 24)
                    for n in range(2):
                        attention_hi(1, n)

                front(0, False)
                attention(0, False)
                with act.Fori(1, B) as b:
                    front(b, True)
                    attention(b, True)
                turned_rows(B - 1)
                router_exp(B - 1)
                second_rows(B - 1)
                act.wait_ge(raw_loaded, 64)
                for raw, hi, _ in w1_parts + w2_parts:
                    act.activation(hi, raw, ACT.Copy).then_inc(first_hi_ready, 1)

            @block.vector
            def _(dve):
                def norm_stats(b, part):
                    if part == 0:
                        dve.wait_ge(seq_loaded, b * 48 + 48)
                        dve.bn_stats(stats[0:SC, T, :], cr[:])
                    for t in range(part * HT, part * HT + HT):
                        dve.bn_stats(stats[:, t, :], xr[:, t, :]).then_inc(stat_ready, 1)

                def norm_variance(b):
                    dve.wait_ge(stat_ready, b * T + T)
                    dve.sem_inc(passed, 1)
                    for t in range(T):
                        dve.bn_aggr(mv[:, t, :], stats[:, t, :])
                    dve.bn_aggr(mv[0:SC, T, :], stats[0:SC, T, :]).then_inc(mv_ready, 1)
                    dve.wait_ge(mv_ready, b + 1)
                    dve.tensor_scalar(var_in[:, 0:T], mv[:, 0:T, 1], 1.0 + EPS, EPS * EPS, ALU.mult, ALU.add)
                    dve.tensor_scalar(var_in[0:SC, T:NT], mv[0:SC, T, 1:2], EPS, None, ALU.add).then_inc(var_ready, 1)

                def norm_rows(b, part):
                    if part == 0:
                        dve.wait_ge(rstd_ready, b + 1)
                        dve.tensor_scalar(cn[:, 0:DC], cr[:], mv[0:SC, T, 0:1], rstd[0:SC, T:NT], ALU.subtract,
                                          ALU.mult).then_inc(xn_ready, 1)
                    for t in range(part * HT, part * HT + HT):
                        ins = dve.tensor_scalar(xn[:, t, :], xr[:, t, :], mv[:, t, 0:1], rstd[:, t:t + 1], ALU.subtract, ALU.mult)
                    ins.then_inc(xn_ready, 1)

                NORM_STEPS = (16, 18, 19, 25, 27)

                def norm_part(b, n):
                    if n < 2:
                        norm_stats(b, n)
                    elif n == 2:
                        norm_variance(b)
                    else:
                        norm_rows(b, n - 3)

                def mask_to_bias(b, first=False):
                    if not first:
                        dve.wait_ge(exp_done, b * NI)
                        dve.sem_inc(passed, 1)
                    dve.tensor_scalar(mask_bias[:], mask_u8[:], 3e38, -3e38, ALU.mult, ALU.add).then_inc(mask_cut, 1)
                    dve.wait_ge(mask_cut, b + 1)
                    dve.tensor_tensor(mask_bias[:], mask_bias[:], shift[0:SC, :], ALU.min).then_inc(mask_ready, 1)

                def norm_lo(b, g):
                    dve.wait_ge(ln_hi_ready, b * GROUPS + (g + 1))
                    src, hi, lo = norm_group(g)
                    dve.tensor_tensor(lo, src, hi.bitcast(F32), ALU.subtract).then_inc(ln_ready, 1)

                def front(b, with_last):
                    def mean_squares(t):
                        p, n = (P, 8) if t < T else (SC, H)
                        dve.wait_ge(proj_read, b * NT + (t + 1))
                        if t >= 2:
                            dve.wait_ge(rr_ready, b * NT + (t - 1))
                        dve.tensor_reduce(ss[0:p, t % 2, 0:n], sq[0:p, t % 2, 0:n * DH].rearrange("p (h d) -> p h d", d=DH),
                                          AX, ALU.add).then_inc(ss_ready, 1)
                        dve.wait_ge(ss_ready, b * NT + (t + 1))
                        dve.tensor_scalar(ssm[0:p, t % 2, 0:n], ss[0:p, t % 2, 0:n], 1.0 / DH, RMS_EPS * RMS_EPS, ALU.mult,
                                          ALU.max).then_inc(ssm_ready, 1)
                        v0 = QK if t < T else H * DH
                        dve.tensor_tensor(value_slots(V_lo, t, p),
                                          psO[t % 2][0:p, v0:v0 + H * DH].rearrange("p (i s d) -> p i s d", i=H // 2, s=2),
                                          value_slots(V_hi, t, p).bitcast(F32), ALU.subtract).then_inc(v_ready, 1)

                    def scale_heads(t):
                        p, n = (P, 8) if t < T else (SC, H)
                        dve.wait_ge(rr_ready, b * NT + (t + 1))
                        if t >= 2:
                            dve.wait_ge(qkT_done, b * NT + (t - 1))
                        ins = dve.tensor_tensor(
                            qkd[0:p, t % 2, 0:n * DH].rearrange("p (h d) -> p h d", d=DH),
                            qk_sb[0:p, t % 3, 0:n * DH].rearrange("p (h d) -> p h d", d=DH),
                            rr[0:p, t % 2, 0:n].unsqueeze(2).to_broadcast([p, n, DH]), ALU.mult)
                        ins.then_inc(qkd_ready, 1)

                    def heads_lo(t):
                        dve.wait_ge(qk_hi_ready, b * NT + (t + 1))
                        for odd in range(2):
                            keep, other = halves(odd)
                            q_src, k_src, cols = turned_heads(t, keep)
                            if t < T:
                                dve.scalar_tensor_tensor(
                                    out=Q1[other, odd:H:2, cols], in0=q_src, scalar=gqk[keep, 0:1],
                                    in1=Q1[keep, odd:H:2, cols].bitcast(F32), op0=ALU.mult, op1=ALU.subtract)
                            ins = dve.tensor_tensor(K2[keep, :, cols], k_src, K1[keep, odd:H:2, cols].bitcast(F32), ALU.subtract)
                        ins.then_inc(qk_ready, 1)

                    for t in range(NT + 2):
                        if with_last and t < 2:
                            for u in range(t * HT, t * HT + HT):
                                second_stats(b - 1, u)
                        if with_last and t == 1:
                            second_variance(b - 1)
                        if t == 2:
                            for g in range(LATENT_GROUPS, GROUPS):
                                norm_lo(b, g)
                        if with_last and ROWS_AT <= t < ROWS_AT + HT:
                            normed_row(dve, b - 1, t - ROWS_AT)
                        if t < NT:
                            mean_squares(t)
                        if 1 <= t <= NT:
                            scale_heads(t - 1)
                        if t >= 2:
                            heads_lo(t - 2)

                def attention(b, between):
                    def denominators(h, n):
                        v0 = 0 if h % 2 == 0 else DH
                        d0 = DH - v0
                        cols = slice(n * HALF, (n + 1) * HALF)
                        dve.wait_ge(av_done, b * NI + KT * (h + 1))
                        if h > 0:
                            dve.wait_ge(o_read, b * 2 * H + (2 * h + n - 1))
                        dve.transpose(den[d0:d0 + DH, cols], psO[h % 2][d0:d0 + DH, cols]).then_inc(den_step, 1)
                        dve.wait_ge(den_step, b * 4 * H + (4 * h + 2 * n + 1))
                        dve.reciprocal(den_inv[v0:v0 + DH, :], den[d0:d0 + DH, n * HALF:(n + 1) * HALF:BLOCK]).then_inc(den_step, 1)

                    def quotients(h, n):
                        v0 = 0 if h % 2 == 0 else DH
                        cols = slice(n * HALF, (n + 1) * HALF)
                        dve.wait_ge(den_step, b * 4 * H + (4 * h + 2 * n + 2))
                        dve.transpose(den[v0:v0 + DH, cols].rearrange("p (k j) -> p k j", j=BLOCK),
                                      den_inv[v0:v0 + DH, :].unsqueeze(2).to_broadcast([DH, HALF // BLOCK, BLOCK])).then_inc(den_ready, 1)
                        dve.wait_ge(den_ready, b * 2 * H + (2 * h + n + 1))
                        dve.tensor_tensor(attf[v0:v0 + DH, h // 2, cols], psO[h % 2][v0:v0 + DH, cols], den[v0:v0 + DH, cols],
                                          ALU.mult).then_inc(o_read, 1)

                    def attention_lo(c, n):
                        cols = slice(n * HALF, (n + 1) * HALF)
                        dve.wait_ge(att_hi_ready, b * 2 * EC + (2 * c + n + 1))
                        dve.tensor_tensor(att_lo[:, c, cols], attf[:, c, cols], att_hi[:, c, cols].bitcast(F32),
                                          ALU.subtract).then_inc(att_ready, 1)

                    for i in range(NI):
                        if i not in POOL_LO:
                            probabilities_lo(dve, b, i).then_inc(p_ready, 1)
                        h, kt = divmod(i, KT)
                        if h >= 1 and kt in (2, 4):
                            denominators(h - 1, kt // 2 - 1)
                        if h >= 1 and kt in (3, 5):
                            quotients(h - 1, kt // 2 - 1)
                        if i in (26, 28):
                            attention_lo(0, (i - 26) // 2)
                        between(i)
                    denominators(H - 1, 0)
                    quotients(H - 1, 0)
                    denominators(H - 1, 1)
                    attention_lo(H // 2 - 1, 0)
                    quotients(H - 1, 1)
                    attention_lo(H // 2 - 1, 1)

                def residual(b, t):
                    if t == 0:
                        dve.wait_ge(xb_ready, b + 1)
                    dve.wait_ge(o_done, b * T + (t + 1))
                    dve.scalar_tensor_tensor(out=xb[:, t, :], in0=out_psum(t), scalar=gate[:, 0:1], in1=xb[:, t, :],
                                             op0=ALU.mult, op1=ALU.add).then_inc(x2_ready, 1)

                def second_stats(b, t):
                    dve.wait_ge(x2_ready, b * T + (t + 1))
                    dve.bn_stats(st2[:, t, :], xb[:, t, :]).then_inc(st2_ready, 1)

                def second_variance(b):
                    dve.wait_ge(st2_ready, b * T + T)
                    dve.sem_inc(passed, 1)
                    for t in range(T):
                        ins = dve.bn_aggr(mv2[:, t, :], st2[:, t, :])
                    ins.then_inc(mv2_ready, 1)
                    dve.wait_ge(mv2_ready, b + 1)
                    dve.tensor_scalar(var2[:], mv2[:, :, 1], EPS, None, ALU.add).then_inc(var2_ready, 1)

                wide = lambda a: a.unsqueeze(2).to_broadcast([P, T, NE])
                experts = expert_id[:].unsqueeze(1).to_broadcast([P, T, NE])

                def stepper(b, done):
                    step = [done]

                    def then_step(ins):
                        step[0] += 1
                        ins.then_inc(route, 1)
                        dve.wait_ge(route, b * ROUTE + step[0])

                    return then_step

                def router_logits(b):
                    then_step = stepper(b, 0)
                    dve.wait_ge(logits_done, b + 1)
                    then_step(dve.tensor_copy(lg[:], psO[1][:, 0:T * NE].rearrange("p (t e) -> p t e", t=T)))
                    then_step(dve.tensor_reduce(lmax[:], lg[:], AX, ALU.max))
                    then_step(dve.tensor_tensor(lz[:], lg[:], wide(lmax[:]), ALU.subtract))

                def router_softmax(b):
                    then_step = stepper(b, 3)
                    dve.wait_ge(ez_ready, b + 1)
                    then_step(dve.tensor_reduce(psum_[:], pe_[:], AX, ALU.add))
                    then_step(dve.reciprocal(psum_[:], psum_[:]))
                    then_step(dve.tensor_tensor(prob[:], pe_[:], wide(psum_[:]), ALU.mult))

                def router_largest(b, k):
                    then_step = stepper(b, 6 + 6 * k)
                    then_step(dve.tensor_reduce(top[:, k, :], (prob, prob2)[k][:], AX, ALU.max))
                    then_step(dve.tensor_tensor(eq[:], (prob, prob2)[k][:], wide(top[:, k, :]), ALU.is_equal))
                    then_step(dve.scalar_tensor_tensor(out=cand[:], in0=eq[:], scalar=-float(NE), in1=experts, op0=ALU.mult,
                                                       op1=ALU.add))
                    then_step(dve.tensor_reduce(pick[:, k, :], cand[:], AX, ALU.min))
                    then_step(dve.tensor_tensor(hot[:, k], cand[:], wide(pick[:, k, :]), ALU.is_equal))
                    if k == 0:
                        then_step(dve.scalar_tensor_tensor(out=prob2[:], in0=hot[:, 0], scalar=-2.0, in1=prob[:], op0=ALU.mult,
                                                           op1=ALU.add))

                def router_rows(b):
                    then_step = stepper(b, 17)
                    dve.tensor_tensor(chosen[:].rearrange("p (t e) -> p t e", t=T), hot[:, 0], hot[:, 1],
                                      ALU.add).then_inc(chosen_ready, 1)
                    for k in range(2):
                        dve.tensor_scalar(rows[k][:, :, D:D + 1].rearrange("p t a -> p (t a)"), token_id[:], 0.0, None, ALU.add)
                        ins = dve.tensor_scalar(rows[k][:, :, D + 1:D + 2].rearrange("p t a -> p (t a)"), top[:, k, :], gate[:, 1:2],
                                                None, ALU.mult)
                    then_step(ins)
                    dve.tensor_scalar(token_id[:], token_id[:], float(S), None, ALU.add)

                def router_slots(b):
                    then_step = stepper(b, 18)
                    dve.wait_ge(rank_done, b + 1)
                    for t in range(T):
                        dve.tensor_tensor(base[:, t + 1, :], base[:, t, :], psO[1][:, HALF + t * NE:HALF + (t + 1) * NE],
                                          ALU.add).then_inc(base_ready, 1)
                        dve.wait_ge(base_ready, b * (T + 2) + (t + 1))
                    then_step(dve.tensor_tensor(slot[:], psO[1][:, 0:T * NE].rearrange("p (t e) -> p t e", t=T), base[:, 0:T, :], ALU.add))
                    then_step(dve.tensor_tensor(slot[:], slot[:], region0[:].unsqueeze(1).to_broadcast([P, T, NE]), ALU.add))
                    then_step(dve.tensor_tensor(slot_hot[:], hot[:], slot[:].unsqueeze(1).to_broadcast([P, 2, T, NE]), ALU.mult))
                    dve.tensor_reduce(slot_f[:], slot_hot[:], AX, ALU.add).then_inc(base_ready, 1)
                    dve.wait_ge(base_ready, b * (T + 2) + T + 1)
                    dve.tensor_copy(base[:, 0, :], base[:, T, :]).then_inc(base_ready, 1)
                    dve.tensor_copy(slot_i[:], slot_f[:]).then_inc(slots_ready, 1)
                    dve.wait_ge(base_ready, b * (T + 2) + T + 2)
                    dve.sem_inc(passed, 1)

                def router_steps(b):
                    router_logits(b)
                    router_softmax(b)
                    for k in range(2):
                        router_largest(b, k)
                    router_rows(b)
                    router_slots(b)

                norm_part(0, 0)
                norm_part(0, 1)
                dve.wait_ge(pool_const, NPOOL)
                norm_part(0, 2)
                dve.wait_ge(iota_done, 3)
                dve.tensor_copy(expert_id[:], iota_i[:, 0:8])
                dve.tensor_copy(token_id[:], iota_i[:, 8:16])
                dve.tensor_copy(tile_id[:], tile_i[:])
                dve.tensor_scalar(region0[:], iota_i[:, 0:8], float(REGION), None, ALU.mult).then_inc(dve_const, 1)
                for g, (src, hi, lo) in enumerate(weight_groups()):
                    dve.wait_ge(w_hi_ready, g + 1)
                    dve.tensor_tensor(lo, src, hi.bitcast(F32), ALU.subtract).then_inc(w_ready, 1)
                norm_part(0, 3)
                norm_part(0, 4)
                dve.wait_ge(consts_loaded, 16 * NCONST)
                dve.tensor_tensor(qg_row[:], qg_row[:], kg_row[:], ALU.mult).then_inc(dve_const, 1)
                dve.scalar_tensor_tensor(out=gqk[:], in0=qg[:], scalar=SCALE, in1=kg[:], op0=ALU.mult,
                                         op1=ALU.mult).then_inc(dve_const, 1)
                dve.wait_ge(dve_const, 2)
                dve.tensor_reduce(shift[:], qg_row[:], AX, ALU.max, apply_absolute_value=True).then_inc(dve_const, 1)
                dve.wait_ge(gate_ready, 1)
                dve.tensor_scalar(tbo[:], bo_row[:], gate[:, 0:1], None, ALU.mult).then_inc(dve_const, 1)
                dve.wait_ge(dve_const, 4)
                dve.tensor_scalar(shift[:], shift[:], -SCALE * DH, SAFE, ALU.mult, ALU.add).then_inc(dve_const, 1)
                dve.wait_ge(dve_const, 6)
                dve.tensor_scalar(shift[:], shift[:], 0.0, None, ALU.min).then_inc(dve_const, 1)
                dve.wait_ge(dve_const, 7)
                dve.wait_ge(zero_ready, 1)
                dve.wait_ge(dump_zeroed, 16)
                dve.tensor_scalar(pad_rows[:, :, D:D + 1].rearrange("p m a -> p (m a)"), iota_i[:, 8:8 + MH],
                                  float(NTOK), None, ALU.add).then_inc(dve_const, 1)
                mask_to_bias(0, first=True)
                for g in range(LATENT_GROUPS):
                    norm_lo(0, g)
                front(0, False)

                def next_norm(i):
                    if i in NORM_STEPS:
                        norm_part(1, NORM_STEPS.index(i))

                attention(0, next_norm)
                with dve.Fori(1, B) as b:
                    for t in range(T):
                        residual(b - 1, t)
                        if t >= T - 2:
                            norm_lo(b, t - (T - 2))
                    for g in range(2, LATENT_GROUPS):
                        norm_lo(b, g)
                    mask_to_bias(b)
                    front(b, True)

                    def router_and_norm(i):
                        if i == 0:
                            router_logits(b - 1)
                        if i == 2:
                            router_softmax(b - 1)
                        if i in (3, 4):
                            router_largest(b - 1, i - 3)
                        if i == 5:
                            router_rows(b - 1)
                        if i == 7:
                            router_slots(b - 1)
                        if i in NORM_STEPS:
                            with dve.If(b < B - 1):
                                norm_part(b + 1, NORM_STEPS.index(i))

                    attention(b, router_and_norm)
                for t in range(T):
                    residual(B - 1, t)
                    second_stats(B - 1, t)
                second_variance(B - 1)
                for t in range(T):
                    normed_row(dve, B - 1, t)
                router_steps(B - 1)

                plan_step = [0]

                def then_plan(ins):
                    plan_step[0] += 1
                    ins.then_inc(plan_ready, 1)
                    dve.wait_ge(plan_ready, plan_step[0])

                wide_t = lambda a: a.unsqueeze(1).to_broadcast([P, NTILES, NE])
                wide_e = lambda a: a.unsqueeze(2).to_broadcast([P, NTILES, NE])
                count = base[:, 0, :]
                dve.tensor_tensor(pad_at[:], count, region0[:], ALU.add).then_inc(pads_known, 1)
                then_plan(dve.tensor_scalar(tiles_i[:], count, float(TM - 1), None, ALU.add))
                then_plan(dve.tensor_scalar(tiles_i[:], tiles_i[:], TM.bit_length() - 1, None, ALU.arith_shift_right))
                then_plan(dve.tensor_scalar(tiles[:], tiles_i[:], 1.0, None, ALU.max))
                dve.tensor_scalar(jump[:], tiles[:], -float(TM), float(REGION), ALU.mult, ALU.add)
                then_plan(dve.tensor_copy(ends[:, 0:1], tiles[:, 0:1]))
                for e in range(1, NE):
                    then_plan(dve.tensor_tensor(ends[:, e:e + 1], ends[:, e - 1:e], tiles[:, e:e + 1], ALU.add))
                then_plan(dve.tensor_tensor(begun[:], wide_e(tile_id[:]), wide_t(ends[:]), ALU.is_ge))
                then_plan(dve.tensor_tensor(jumped[:], begun[:], wide_t(jump[:]), ALU.mult))
                then_plan(dve.tensor_reduce(row_f[:], jumped[:], AX, ALU.add))
                then_plan(dve.scalar_tensor_tensor(out=row_f[:], in0=tile_id[:], scalar=float(TM), in1=row_f[:], op0=ALU.mult,
                                                   op1=ALU.add))
                dve.tensor_copy(tile_row[:], row_f[:]).then_inc(rows_known, 1)
                dve.tensor_reduce(expert_f[:], begun[:, :, 0:NE - 1], AX, ALU.add)
                then_plan(dve.tensor_scalar(tile_id[:], tile_id[:], 1.0, None, ALU.add))
                then_plan(dve.tensor_tensor(begun[:], wide_e(tile_id[:]), wide_t(ends[:]), ALU.is_equal))
                then_plan(dve.tensor_reduce(last_f[:], begun[:, :, 0:NE - 1], AX, ALU.add))
                dve.tensor_copy(tile_count[:], ends[:, NE - 1:NE])
                then_plan(dve.scalar_tensor_tensor(out=tile_switch[:], in0=expert_f[:], scalar=1.0, in1=last_f[:], op0=ALU.add,
                                                   op1=ALU.mult))
                for k, (raw, hi, lo) in enumerate(w1_parts + w2_parts):
                    dve.wait_ge(first_hi_ready, k + 1)
                    dve.tensor_tensor(lo, raw, hi.bitcast(F32), ALU.subtract).then_inc(first_cut, 1)

            @block.tensor
            def _(pe):
                pe.wait_ge(ident_ready, 2)
                pe.wait_ge(pool_const, NPOOL)
                pe.wait_ge(weights_loaded, 64)
                rows_qk = [wst_q[:, 0], wst_q[:, 1], wst_l[:, 0], wst_l[:, 1]]
                rows_v = [wst_l[:, 2], wst_l[:, 3]]
                turned = [(psS[0], c * HALF + j * P, rows_qk[j][:, c * P:(c + 1) * P], c) for c in range(EC) for j in range(4)]
                turned += [(psS[1], c * D + j * P, rows_v[j][:, c * P:(c + 1) * P], 2) for c in range(EC) for j in range(2)]
                turned += [(psS[1], HALF + c * D + j * P, wst_o[:, j, c * P:(c + 1) * P], 3) for c in range(EC) for j in range(2)]
                turned += [(psO[0], c * HALF + j * P, wst_c[:, j, c * P:(c + 1) * P], 4 + c) for c in range(2) for j in range(4)]
                for n, (ps, col, src, g) in enumerate(turned):
                    ins = pe.transpose(ps[:, col:col + P], src, ident[:])
                    if n + 1 == len(turned) or turned[n + 1][3] != g:
                        ins.then_inc(wT_done, 1)
                pe.wait_ge(w_ready, GROUPS_W)

                def passes(o, parts):
                    for n, (l, r) in enumerate(parts):
                        ins = pe.matmul(o, l, r, start=(n == 0), stop=(n == len(parts) - 1))
                    return ins

                def turn_latents(b, first=False):
                    if not first:
                        pe.wait_ge(exp_done, b * NI)
                        pe.sem_inc(passed, 1)
                    for hb in range(2):
                        pe.wait_ge(xn_ready, b * 3 + (hb + 2))
                        for c in range(EC):
                            for t in range(HT):
                                ins = pe.transpose(psS[hb][:, c * HALF + t * P:c * HALF + (t + 1) * P],
                                                   xn[:, hb * HT + t, c * P:(c + 1) * P], ident[:])
                            ins.then_inc(xT_done, 1)

                def front(b, with_router):
                    def turn_context():
                        pe.wait_ge(xn_ready, b * 3 + 1)
                        pe.sem_inc(passed, 1)
                        pe.wait_ge(ln_hi_ready, b * GROUPS + EC)
                        pe.sem_inc(passed, 1)
                        for c in range(2):
                            pe.transpose(psS[0][:, c * HALF:c * HALF + SC], cn[:, c * P:(c + 1) * P], ident[0:SC, 0:SC]).then_inc(xT_done, 1)

                    def project(t):
                        if t in (0, HT, T):
                            pe.wait_ge(ln_ready, b * GROUPS + EC * (t // HT + 1))
                        if with_router and t < 2:
                            pe.wait_ge(x2_ready, b * T)
                        if t >= 2:
                            pe.wait_ge(v_ready, b * NT + (t - 1))
                        o = psO[t % 2]
                        if t < T:
                            cols = slice(t * P, (t + 1) * P)
                            pairs = lambda f: [p for c in range(EC) for p in (
                                (ln_hi[:, c, cols], w_hi[:, c, f]), (ln_hi[:, c, cols], w_lo[:, c, f]),
                                (ln_lo[:, c, cols], w_hi[:, c, f]))]
                            passes(o[:, 0:QK], pairs(slice(0, QK)))
                            passes(o[:, QK:QK + H * DH], pairs(slice(QK, QK + H * DH))).then_inc(proj_done, 1)
                        else:
                            passes(o[:, 0:2 * H * DH], [p for c in range(2) for p in (
                                (lc_hi[:, c, :], wc_hi[:, c, :]), (lc_hi[:, c, :], wc_lo[:, c, :]),
                                (lc_lo[:, c, :], wc_hi[:, c, :]))]).then_inc(proj_done, 1)

                    def turn_heads(t):
                        if t < 2:
                            pe.wait_ge(ln_hi_ready, b * GROUPS + GROUPS)
                        if t >= 2:
                            pe.wait_ge(qk_ready, b * NT + (t - 1))
                        pe.wait_ge(qkd_ready, b * NT + (t + 1))
                        if t == T:
                            pe.sem_inc(passed, 1)
                        p, n = (P, H) if t < T else (SC, H // 2)
                        for j in range(n):
                            col = j * P if t < T else H // 2 * P + j * SC
                            ins = pe.transpose(psS[t % 2][:, col:col + p], qkd[0:p, t % 2, j * P:(j + 1) * P], ident[0:p, 0:p])
                        ins.then_inc(qkT_done, 1)

                    for t in range(NT + 2):
                        if t < NT:
                            project(t)
                        if t == 1:
                            turn_context()
                        if t >= 2:
                            turn_heads(t - 2)
                        if with_router and t >= NT:
                            turn_rows(b - 1, t - NT)

                def turn_rows(b, hb):
                    pe.wait_ge(y_ready[hb], b * HT + HT)
                    for c in range(EC):
                        for t in range(HT):
                            ins = pe.transpose(psO[1 - hb][:, c * HALF + t * P:c * HALF + (t + 1) * P],
                                               rows[0][:, hb * HT + t, c * P:(c + 1) * P], ident[:])
                    ins.then_inc(yT_done, 1)

                def logits(b):
                    for t in range(T):
                        if t % HT == 0:
                            pe.wait_ge(yT_ready, b * 2 + (t // HT + 1))
                        ins = passes(psO[1][:, t * NE:(t + 1) * NE], [(yT[:, c, t * P:(t + 1) * P], router[:, c, :]) for c in range(EC)])
                    ins.then_inc(logits_done, 1)

                def ranks(b):
                    pe.wait_ge(chosen_ready, b + 1)
                    pe.matmul(psO[1][:, 0:T * NE], tri[:], chosen[:], start=True, stop=True)
                    pe.matmul(psO[1][:, HALF:HALF + T * NE], ones[:], chosen[:], start=True, stop=True).then_inc(rank_done, 1)

                def attention(b, with_router):
                    def scores(i):
                        h, kt = divmod(i, KT)
                        if i < 2:
                            pe.wait_ge(qk_ready, b * NT + (T + i))
                        if i >= 2:
                            pe.wait_ge(exp_done, b * NI + (i - 1))
                        keys = slice(kt * P, (kt + 1) * P)
                        for n in range(2):
                            pe.matmul(scores_psum(i)[:, n * HALF:(n + 1) * HALF], K1[:, h, keys], Q1[:, h, n * HALF:(n + 1) * HALF],
                                      start=True, stop=False)
                        rows_hi = slice(0, DH) if h % 2 == 0 else slice(DH, P)
                        for n in range(2):
                            ins = pe.matmul(scores_psum(i)[:, n * HALF:(n + 1) * HALF], K2[rows_hi, h // 2, keys],
                                            Q1[rows_hi, h, n * HALF:(n + 1) * HALF], start=False, stop=True)
                        ins.then_inc(s_done, 1)

                    def values(i):
                        h, kt = divmod(i, KT)
                        wait_probabilities(pe, b, i)
                        if kt == 0 and h >= 2:
                            pe.wait_ge(o_read, b * 2 * H + 2 * (h - 1))
                        p = P if kt < T else SC
                        v0 = (3 * (h // 2) + h % 2) * DH
                        vh, vl = V_hi[:, kt, v0:v0 + P], V_lo[0:p, kt, v0:v0 + P]
                        ph, pl = p_hi[i % NP_RING], p_lo[i % NP_RING]
                        products = [(vh, ph), (vh, pl), (vl, ph[0:p])] if kt < T else [(vh, ph), (vl, ph[0:p])]
                        for n in range(2):
                            cols = slice(n * HALF, (n + 1) * HALF)
                            for k, (v, pr) in enumerate(products):
                                ins = pe.matmul(psO[h % 2][:, cols], v, pr[:, cols], start=(kt == 0 and k == 0),
                                                stop=(kt == KT - 1 and k == len(products) - 1))
                        ins.then_inc(av_done, 1)

                    for i in range(NI + AHEAD):
                        if i < NI:
                            scores(i)
                        if with_router and i == 1:
                            logits(b - 1)
                        if with_router and i == 8:
                            ranks(b - 1)
                        if with_router and i == KT + AHEAD:
                            pe.wait_ge(slots_ready, b)
                            pe.sem_inc(passed, 1)
                        if i >= AHEAD:
                            values(i - AHEAD)

                def project_out(b):
                    for t in range(T):
                        if t in (0, HT):
                            pe.wait_ge(att_ready, b * 2 * EC + (2 * EC - 1 + t // HT))
                        if t >= OUT_SLOTS:
                            pe.wait_ge(x2_ready, b * T + (t - OUT_SLOTS + 1))
                        cols = slice(t * P, (t + 1) * P)
                        passes(out_psum(t), [p for c in range(EC) for p in (
                            (att_hi[:, c, cols], wo_hi[:, c, :]), (att_hi[:, c, cols], wo_lo[:, c, :]),
                            (att_lo[:, c, cols], wo_hi[:, c, :]))]).then_inc(o_done, 1)

                turn_latents(0, first=True)
                front(0, False)
                attention(0, False)
                with pe.Fori(1, B) as b:
                    turn_latents(b)
                    project_out(b - 1)
                    front(b, True)
                    attention(b, True)
                project_out(B - 1)
                for hb in range(2):
                    pe.wait_ge(x2_ready, B * T)
                    turn_rows(B - 1, hb)
                logits(B - 1)
                ranks(B - 1)

        experts_phase(nc, (tile_count, tile_row, tile_switch), pad_rows, ident,
                      xrow, x_loaded, (b1_raw, b2_raw, w1_raw, w2_raw), ((w1_hi, w1_lo), (w2_hi, w2_lo)), (w1_parts, w2_parts),
                      w1, b1, w2, b2, routed, total, out)


def experts_phase(nc, plan, pad_rows, ident, xrow, x_loaded, raw, cut_weights, parts, w1, b1, w2, b2, routed, total, out):
    NE, D, HID = w1.shape
    EC, HC = D // P, HID // P
    MH, ROW = pad_rows.shape[1:]
    TM = MH * P
    REGION = routed.shape[0] // NE
    NTOK = REGION - TM
    NQ = HC // 2
    tile_count, tile_row, tile_switch = plan
    b1_raw, b2_raw, w1_raw, w2_raw = raw
    w1_parts, w2_parts = parts
    (w1_hi, w1_lo), (w2_hi, w2_lo) = cut_weights
    NTILES = tile_row.shape[1]

    with ExitStack() as ctx:
        def sb(name, shape, dt=F32):
            return ctx.enter_context(nc.sbuf_tensor(name, shape, dt))

        def sem(name):
            return ctx.enter_context(nc.semaphore(name))

        b1_col = sb("b1_col", [P, HC])
        b2_row = sb("b2_row", [P, D])
        xT_hi = sb("xT_hi", [P, EC, TM], F32R)
        xT_lo = sb("xT_lo", [P, EC, TM], F32R)
        g32 = sb("g32", [P, 2, 2 * TM])
        g_hi = sb("g_hi", [P, HC, TM], F32R)
        g_lo = sb("g_lo", [P, HC, TM], F32R)
        meta_next = sb("meta_next", [P, MH, 2])
        meta_now = sb("meta_now", [P, MH, 2])
        token_i = sb("token_i", [P, MH], I32)
        y1 = sb("y1", [P, MH, D])
        y_out = sb("y_out", [P, MH, D])

        psH = [ctx.enter_context(nc.psum_tensor(f"psH{i}", [P, 2 * TM], F32)) for i in range(NQ)]
        psX = ctx.enter_context(nc.psum_tensor("psX", [P, EC, TM], F32))
        psY = [ctx.enter_context(nc.psum_tensor(f"psY{i}", [P, 512], F32)) for i in range(MH)]

        xT_done = sem("xT_done2")
        meta_taken = sem("meta_taken")
        meta_moved = sem("meta_moved")
        xT_hi_ready = sem("xT_hi_ready")
        xT_ready = sem("xT_ready")
        raw_loaded = sem("raw_loaded2")
        w_hi_ready = sem("w_hi_ready2")
        w1_ready = sem("w1_ready")
        w1_pool_ready = sem("w1_pool_ready")
        w2_ready = sem("w2_ready")
        w_cut = sem("w_cut")
        b1_taken = sem("b1_taken")
        h_done = sem("h_done")
        gelu_done = sem("gelu_done")
        g_hi_ready = sem("g_hi_ready")
        g_ready = sem("g_ready")
        y_done = sem("y_done")
        y_read = sem("y_read")
        y_ready = sem("y_ready2")
        added = sem("added")
        rows_free = sem("rows_free")
        out_stored = sem("out_stored")
        passed = sem("passed2")

        PARTS = len(w1_parts) + len(w2_parts)

        def next_expert(eng, t):
            return eng.value_load(tile_switch[0:1, bass.ds(t, 1)], min_val=0, max_val=NE - 1)

        def count_of(eng):
            return eng.value_load(tile_count[0:1, 0:1], min_val=1, max_val=NTILES)

        block = ctx.enter_context(nc.Block())

        @block.sync
        def _(sp):
            def load(t):
                row = sp.value_load(tile_row[0:1, bass.ds(t, 1)], min_val=0, max_val=NE * REGION - TM)
                sp.wait_ge(xT_done, t + 1)
                sp.wait_ge(meta_taken, t + 1)
                sp.dma_start(xrow, routed[bass.ds(row, TM)].rearrange("(m p) r -> p m r", p=P)).then_inc(x_loaded, 16)

            tiles = count_of(sp)
            with sp.Fori(1, NTILES) as t, sp.If(t < tiles):
                load(t)
            sp.wait_ge(x_loaded, tiles * 16)
            sp.sem_inc(passed, 1)
            sp.wait_ge(added, tiles * 32)
            sp.dma_start(out.rearrange("b s d -> (b s) d"), total[0:NTOK]).then_inc(out_stored, 16)
            sp.wait_ge(out_stored, 16)

        @block.gpsimd
        def _(pool):
            pool.sem_inc(rows_free, 1)
            pool.sem_inc(w1_pool_ready, 1)

            def load_expert(e):
                pool.dma_start(w1_raw, w1[bass.ds(e, 1)].rearrange("a (c p) h -> p (a c) h", p=P)).then_inc(raw_loaded, 16)
                pool.dma_start(w2_raw, w2[bass.ds(e, 1)].rearrange("a (c p) d -> p (a c) d", p=P)).then_inc(raw_loaded, 16)
                pool.dma_start(b1_raw[:], b1[bass.ds(e, 1)].rearrange("a (c p) -> p (a c)", p=P)).then_inc(raw_loaded, 16)
                pool.dma_start(b2_raw[:], b2[bass.ds(e, 1)].to_broadcast([P, D])).then_inc(raw_loaded, 16)

            pool.wait_ge(w_cut, 1)
            pool.wait_ge(b1_taken, 1)
            pool.wait_ge(x_loaded, 16)
            load_expert(1)
            tiles = count_of(pool)
            with pool.Fori(0, NTILES) as t, pool.If(t < tiles):
                expert = next_expert(pool, t)
                with pool.If(expert > 0):
                    pool.wait_ge(w_hi_ready, expert * PARTS + len(w1_parts))
                    raw, hi, lo = w1_parts[1]
                    pool.tensor_tensor(lo, raw, hi.bitcast(F32), ALU.subtract).then_inc(w1_pool_ready, 1)
                with pool.Else():
                    pool.wait_ge(h_done, t * HC + HC)
                    pool.sem_inc(w1_pool_ready, 1)
                pool.wait_ge(y_ready, t + 1)
                pool.sem_inc(passed, 1)
                for m in range(MH):
                    pool.indirect_dma_start(total, bass.IndirectOffsetOnAxis(ap=token_i[:, m:m + 1], axis=0), y_out[:, m, :],
                                            None, bounds_check=NTOK + TM - 1, compute_op=ALU.add).then_inc(added, 16)
                pool.wait_ge(added, t * 32 + 32)
                pool.sem_inc(rows_free, 1)
                with pool.If(expert > 0):
                    with pool.If(expert < NE - 1):
                        pool.wait_ge(w1_pool_ready, t + 2)
                        pool.wait_ge(w2_ready, t * 2 + 4)
                        pool.sem_inc(passed, 1)
                        pool.wait_ge(w_cut, expert + 1)
                        pool.wait_ge(b1_taken, expert + 1)
                        pool.sem_inc(passed, 1)
                        load_expert(nc.s_assert_within(expert + 1, 0, NE - 1, skip_runtime_bounds_check_because="the If around it holds it"))

        @block.scalar
        def _(act):
            act.sem_inc(gelu_done, HC)
            act.sem_inc(w_hi_ready, PARTS)

            def turned_hi(t):
                act.wait_ge(xT_done, t + 2)
                act.activation(xT_hi[:], psX[:], ACT.Copy).then_inc(xT_hi_ready, 1)

            act.activation(b1_col[:], b1_raw[:], ACT.Copy).then_inc(b1_taken, 1)
            turned_hi(0)
            act.wait_ge(b1_taken, 1)
            tiles = count_of(act)
            with act.Fori(0, NTILES) as t, act.If(t < tiles):
                for c in range(HC):
                    q = c // 2
                    if c % 2 == 0:
                        act.wait_ge(h_done, t * HC + (c + 2))
                        act.wait_ge(g_ready, t * NQ + (q - 1 + NQ))
                    act.activation(g32[:, q % 2, (c % 2) * TM:(c % 2 + 1) * TM], psH[q][:, (c % 2) * TM:(c % 2 + 1) * TM],
                                   ACT.Gelu_apprx_tanh, bias=b1_col[:, c:c + 1]).then_inc(gelu_done, 1)
                with act.If(t + 1 < tiles):
                    turned_hi(t + 1)
                expert = next_expert(act, t)
                with act.If(expert > 0):
                    act.wait_ge(raw_loaded, expert * 64)
                    for raw, hi, _ in w1_parts:
                        act.activation(hi, raw, ACT.Copy).then_inc(w_hi_ready, 1)
                    act.wait_ge(gelu_done, t * HC + 2 * HC)
                    act.sem_inc(passed, 1)
                    act.activation(b1_col[:], b1_raw[:], ACT.Copy).then_inc(b1_taken, 1)
                    act.wait_ge(y_done, t * MH + MH)
                    for raw, hi, _ in w2_parts:
                        act.activation(hi, raw, ACT.Copy).then_inc(w_hi_ready, 1)
                    act.wait_ge(b1_taken, expert + 1)
                    act.sem_inc(passed, 1)

        @block.vector
        def _(dve):
            dve.sem_inc(meta_taken, 1)
            dve.sem_inc(g_ready, NQ)
            dve.sem_inc(y_read, 1)

            def turned_lo(t):
                dve.wait_ge(xT_hi_ready, t + 1)
                dve.tensor_tensor(xT_lo[:], psX[:], xT_hi[:].bitcast(F32), ALU.subtract).then_inc(xT_ready, 1)

            def take_meta(t):
                dve.wait_ge(x_loaded, t * 16 + 16)
                dve.tensor_copy(meta_next[:], xrow[:, :, D:ROW]).then_inc(meta_taken, 1)

            def cut(parts, first, ready):
                for k, (raw, hi, lo) in enumerate(parts):
                    dve.wait_ge(w_hi_ready, first + (k + 1))
                    dve.tensor_tensor(lo, raw, hi.bitcast(F32), ALU.subtract).then_inc(ready, 1)

            def results(t):
                for m in range(MH):
                    dve.wait_ge(y_done, t * MH + (m + 1))
                    ins = dve.tensor_tensor(y1[:, m, :], psY[m][:, 0:D], b2_row[:], ALU.add)
                ins.then_inc(y_read, 1)
                dve.wait_ge(rows_free, t + 1)
                dve.tensor_copy(token_i[:], meta_now[:, :, 0])
                dve.wait_ge(y_read, t + 2)
                for m in range(MH):
                    ins = dve.tensor_scalar(y_out[:, m, :], y1[:, m, :], meta_now[:, m, 1:2], None, ALU.mult)
                ins.then_inc(y_ready, 1)

            dve.sem_inc(w1_ready, 1)
            dve.sem_inc(w2_ready, 2)
            dve.tensor_copy(b2_row[:], b2_raw[:]).then_inc(w_cut, 1)
            turned_lo(0)
            take_meta(0)
            dve.wait_ge(w_cut, 1)
            tiles = count_of(dve)
            with dve.Fori(0, NTILES) as t, dve.If(t < tiles):
                for q in range(NQ):
                    dve.wait_ge(gelu_done, t * HC + (2 * q + 2 + HC))
                    g = g32[:, q % 2, :].rearrange("p (c n) -> p c n", c=2)
                    dve.tensor_copy(g_hi[:, 2 * q:2 * q + 2, :], g).then_inc(g_hi_ready, 1)
                    dve.wait_ge(g_hi_ready, t * NQ + (q + 1))
                    dve.tensor_tensor(g_lo[:, 2 * q:2 * q + 2, :], g, g_hi[:, 2 * q:2 * q + 2, :].bitcast(F32),
                                      ALU.subtract).then_inc(g_ready, 1)
                dve.wait_ge(meta_taken, t + 2)
                dve.tensor_copy(meta_now[:], meta_next[:]).then_inc(meta_moved, 1)
                dve.wait_ge(meta_moved, t + 1)
                dve.sem_inc(passed, 1)
                with dve.If(t + 1 < tiles):
                    turned_lo(t + 1)
                    take_meta(t + 1)
                expert = next_expert(dve, t)
                with dve.If(expert > 0):
                    cut(w1_parts[0:1], expert * PARTS, w1_ready)
                    results(t)
                    dve.tensor_copy(b2_row[:], b2_raw[:]).then_inc(w_cut, 1)
                    cut(w2_parts, expert * PARTS + len(w1_parts), w2_ready)
                    dve.wait_ge(w_cut, expert + 1)
                    dve.sem_inc(passed, 1)
                with dve.Else():
                    dve.sem_inc(w1_ready, 1)
                    dve.sem_inc(w2_ready, 2)
                    results(t)

        @block.tensor
        def _(pe):
            pe.sem_inc(xT_done, 1)

            def turn(t):
                pe.wait_ge(x_loaded, t * 16 + 16)
                for c in range(EC):
                    for m in range(MH):
                        ins = pe.transpose(psX[:, c, m * P:(m + 1) * P], xrow[:, m, c * P:(c + 1) * P], ident[:])
                ins.then_inc(xT_done, 1)

            def first_layer(t):
                pe.wait_ge(xT_ready, t + 1)
                for c in range(HC):
                    q = c // 2
                    if c % (HC // 2) == 0:
                        pe.wait_ge(w1_pool_ready if c else w1_ready, t + 1)
                    if c % 2 == 0:
                        pe.wait_ge(gelu_done, t * HC + (2 * q + 2))
                    o = psH[q][:, (c % 2) * TM:(c % 2 + 1) * TM]
                    f = slice(c * P, (c + 1) * P)
                    parts = [p for k in range(EC) for p in ((w1_hi[:, k, f], xT_hi[:, k, :]), (w1_hi[:, k, f], xT_lo[:, k, :]),
                                                            (w1_lo[:, k, f], xT_hi[:, k, :]))]
                    for n, (l, r) in enumerate(parts):
                        ins = pe.matmul(o, l, r, start=(n == 0), stop=(n == len(parts) - 1))
                    ins.then_inc(h_done, 1)

            def second_layer(t):
                pe.wait_ge(y_read, t + 1)
                for q in range(NQ):
                    if q % (NQ // 2) == 0:
                        pe.wait_ge(w2_ready, t * 2 + (q // (NQ // 2) + 1))
                    pe.wait_ge(g_ready, t * NQ + (q + 1 + NQ))
                    for m in range(MH):
                        cols = slice(m * P, (m + 1) * P)
                        for c in (2 * q, 2 * q + 1):
                            for n, (l, r) in enumerate(((g_hi, w2_hi), (g_hi, w2_lo), (g_lo, w2_hi))):
                                ins = pe.matmul(psY[m][:, 0:D], l[:, c, cols], r[:, c, :], start=(c == 0 and n == 0),
                                                stop=(c == HC - 1 and n == 2))
                        if q == NQ - 1:
                            ins.then_inc(y_done, 1)

            turn(0)
            tiles = count_of(pe)
            with pe.Fori(0, NTILES) as t, pe.If(t < tiles):
                first_layer(t)
                with pe.If(t + 1 < tiles):
                    turn(t + 1)
                second_layer(t)


_INS = ['x', 'ctx_768', 'mask_BxS2_bk0', 'g_xattn', 'g_ffn', 'L0_xattn_ln_x_g', 'L0_xattn_ln_x_b', 'L0_xattn_ln_l_g',
        'L0_xattn_ln_l_b', 'L0_xattn_qn_g', 'L0_xattn_kn_g', 'L0_xattn_Wq', 'L0_xattn_Wkv', 'L0_xattn_Wlkv', 'L0_xattn_Wo',
        'L0_xattn_bo', 'L0_ffn_w_router', 'L0_ffn_w1', 'L0_ffn_b1', 'L0_ffn_w2', 'L0_ffn_b2']


def kernel(**inputs):
    import numpy as np
    import concourse.bacc as bacc
    from concourse.bass_utils import run_bass_kernel_spmd

    nc = bacc.Bacc("TRN2", target_bir_lowering=False, num_devices=1)
    arrays, args = {}, []
    for name in _INS:
        a = np.ascontiguousarray(inputs[name])
        arrays[f"in_{name}"] = a
        args.append(nc.dram_tensor(f"in_{name}", a.shape, mybir.dt.from_np(a.dtype), kind="ExternalInput").ap())
    shape = inputs["x"].shape
    out = nc.dram_tensor("out", shape, F32, kind="ExternalOutput").ap()
    flamingo_gated_layer(nc, *args, out)
    r = run_bass_kernel_spmd(nc, [arrays], core_ids=[0])
    return r.results[0]["out"]
```
